# Optimizing a Trainium2 kernel written in Bass

```python
import numpy as np
import jax
import jax.numpy as jnp

def _softmax(x, axis=-1):
    return jax.nn.softmax(x, axis=axis)

def _gelu(x):
    return jax.nn.gelu(x, approximate=True)

def _silu(x):
    return jax.nn.silu(x)

def _sigmoid(x):
    return jax.nn.sigmoid(x)

def _layernorm(x, axis=-1, eps=1e-05):
    m = jnp.mean(x, axis=axis, keepdims=True)
    v = jnp.var(x, axis=axis, keepdims=True)
    return (x - m) / jnp.sqrt(v + eps)

def _scatter_add(tgt, idx, src, axis=0):
    return tgt.at[idx].add(src)

def _segment_sum(src, seg, n):
    return jax.ops.segment_sum(src, seg, n)
kernel_name = 'mk_sandwich_d1_jaxref_r8_d8c8e3'

def setup_inputs(seed: int=0):
    np.random.seed(seed)
    _w = jnp.asarray

    def _L0_attn_setup():
        import jax, jax.numpy as jnp
        import numpy as np
        N_EMBD = 128
        N_HEAD = 16
        DK = N_EMBD // N_HEAD
        key = jax.random.key(seed)
        k1, k2, k3 = jax.random.split(key, 3)
        x = jax.random.normal(k1, (2, 256, N_EMBD), dtype=jnp.float32)
        w_attn = jax.random.normal(k2, (3 * N_EMBD, N_EMBD), dtype=jnp.float32) * N_EMBD ** (-0.5)
        w_proj = jax.random.normal(k3, (N_EMBD, N_EMBD), dtype=jnp.float32) * N_EMBD ** (-0.5)
        return {'x': x, 'w_attn': w_attn, 'w_proj': w_proj}
    _L0_attn_in = _L0_attn_setup()

    def _L0_ffn_setup():
        import jax, jax.numpy as jnp
        import numpy as np
        DIM = 128
        DEPTH = 6
        HEADS = 16
        DIM_HEAD = 64
        WINDOW = 32
        INNER = HEADS * DIM_HEAD
        DIM_INNER = int(DIM * 4 * 2 / 3)
        QK_SCALE = 8.0

        def shift_tokens(t):
            a, s = jnp.split(t, 2, -1)
            s = jnp.pad(s, ((0, 0), (1, 0), (0, 0)))[:, :-1]
            return jnp.concatenate([a, s], -1)

        def l2norm(t):
            return t / jnp.maximum(jnp.linalg.norm(t, axis=-1, keepdims=True), 1e-12)

        def rotate_half(x):
            x1, x2 = jnp.split(x, 2, -1)
            return jnp.concatenate([-x2, x1], -1)

        def rotary_tables(n):
            half = jnp.arange(0, DIM_HEAD, 2, dtype=jnp.float32)
            inv_freq = 1.0 / 10000.0 ** (half / DIM_HEAD)
            t = jnp.arange(n, dtype=jnp.float32)
            freqs = t[:, None] * inv_freq[None, :]
            freqs = jnp.concatenate([freqs, freqs], -1)
            base_scale = (half + 0.4 * DIM_HEAD) / (1.4 * DIM_HEAD)
            power = (t - n // 2) / (WINDOW // 2)
            scale = base_scale[None, :] ** power[:, None]
            scale = jnp.concatenate([scale, scale], -1)
            return (freqs, scale)

        def local_attention(q, k, v):
            b, h, n, d = q.shape
            w = WINDOW
            nw = n // w
            bq = q.reshape(b, h, nw, w, d)
            bk = k.reshape(b, h, nw, w, d)
            bv = v.reshape(b, h, nw, w, d)

            def look(t):
                p = jnp.pad(t, ((0, 0), (0, 0), (1, 0), (0, 0), (0, 0)))
                return jnp.concatenate([p[:, :, :nw], p[:, :, 1:]], axis=3)
            bk2, bv2 = (look(bk), look(bv))
            seq = jnp.arange(n).reshape(nw, w)
            seq_p = jnp.pad(seq, ((1, 0), (0, 0)), constant_values=-1)
            jt = jnp.concatenate([seq_p[:nw], seq_p[1:]], axis=1)
            it = seq[:, :, None]
            jb = jt[:, None, :]
            mask = (it < jb) | (it > jb + w) | (jb == -1)
            sim = jnp.einsum('bhwie,bhwje->bhwij', bq, bk2) * QK_SCALE
            sim = jnp.where(mask, -jnp.finfo(sim.dtype).max, sim)
            attn = jax.nn.softmax(sim, -1)
            out = jnp.einsum('bhwij,bhwje->bhwie', attn, bv2)
            return out.reshape(b, h, n, d)

        def attn_layer(x, Wqkv, qs, ksc, Wo):
            b, n, _ = x.shape
            qkv = x @ Wqkv
            q, k, v = jnp.split(qkv, 3, -1)
            sh = lambda t: t.reshape(b, n, HEADS, DIM_HEAD).transpose(0, 2, 1, 3)
            q, k, v = (sh(q), sh(k), sh(v))
            q = l2norm(q) * qs
            k = l2norm(k) * ksc
            freqs, scale = rotary_tables(n)
            cos, sin = (jnp.cos(freqs), jnp.sin(freqs))
            q = q * cos * scale + rotate_half(q) * sin * scale
            inv = 1.0 / scale
            k = k * cos * inv + rotate_half(k) * sin * inv
            out = local_attention(q, k, v)
            out = out.transpose(0, 2, 1, 3).reshape(b, n, INNER)
            return out @ Wo

        def ffn_layer(x, g, bln, W1, b1, W2, b2):
            mu = x.mean(-1, keepdims=True)
            var = ((x - mu) ** 2).mean(-1, keepdims=True)
            xn = (x - mu) / jnp.sqrt(var + 1e-05) * g + bln
            hg = xn @ W1 + b1
            a, gate = jnp.split(hg, 2, -1)
            return a * jax.nn.gelu(gate, approximate=False) @ W2 + b2
        key = jax.random.key(seed)
        ks = jax.random.split(key, 8)
        B, N = (2, 256)
        init = lambda k, shape: jax.random.normal(k, shape, jnp.float32) * 0.02
        return {'x': jax.random.normal(ks[0], (B, N, DIM), jnp.float32), 'Wqkv': init(ks[1], (DEPTH, DIM, 3 * INNER)), 'q_scale': jnp.ones((DEPTH, DIM_HEAD), jnp.float32), 'k_scale': jnp.ones((DEPTH, DIM_HEAD), jnp.float32), 'Wo': init(ks[2], (DEPTH, INNER, DIM)), 'ln_g': jnp.ones((DEPTH, DIM), jnp.float32), 'ln_b': jnp.zeros((DEPTH, DIM), jnp.float32), 'W1': init(ks[3], (DEPTH, DIM, 2 * DIM_INNER)), 'b1': jnp.zeros((DEPTH, 2 * DIM_INNER), jnp.float32), 'W2': init(ks[4], (DEPTH, DIM_INNER, DIM)), 'b2': jnp.zeros((DEPTH, DIM), jnp.float32)}
    _L0_ffn_in = _L0_ffn_setup()
    _d = {'L0_attn_x': _L0_attn_in['x'], 'L0_attn_w_attn': _L0_attn_in['w_attn'], 'L0_attn_w_proj': _L0_attn_in['w_proj'], 'L0_ffn_Wqkv': _L0_ffn_in['Wqkv'], 'L0_ffn_q_scale': _L0_ffn_in['q_scale'], 'L0_ffn_k_scale': _L0_ffn_in['k_scale'], 'L0_ffn_Wo': _L0_ffn_in['Wo'], 'L0_ffn_ln_g': _L0_ffn_in['ln_g'], 'L0_ffn_ln_b': _L0_ffn_in['ln_b'], 'L0_ffn_W1': _L0_ffn_in['W1'], 'L0_ffn_b1': _L0_ffn_in['b1'], 'L0_ffn_W2': _L0_ffn_in['W2'], 'L0_ffn_b2': _L0_ffn_in['b2']}
    _x0 = _d['L0_attn_x']
    _d['L0_attn_x'] = jax.random.normal(jax.random.fold_in(jax.random.key(seed), 1), (1, 2048, 128), dtype=_x0.dtype)
    del _x0
    return _d

def reference(L0_attn_x, L0_attn_w_attn, L0_attn_w_proj, L0_ffn_Wqkv, L0_ffn_q_scale, L0_ffn_k_scale, L0_ffn_Wo, L0_ffn_ln_g, L0_ffn_ln_b, L0_ffn_W1, L0_ffn_b1, L0_ffn_W2, L0_ffn_b2):

    def _L0_attn_ref(x, w_attn, w_proj):
        import jax, jax.numpy as jnp
        import numpy as np
        N_EMBD = 128
        N_HEAD = 16
        DK = N_EMBD // N_HEAD
        b, t, c = x.shape
        qkv = jnp.einsum('btc,oc->bto', x, w_attn)
        q, k, v = jnp.split(qkv, 3, axis=-1)
        q = q.reshape(b, t, N_HEAD, DK).transpose(0, 2, 1, 3)
        k = k.reshape(b, t, N_HEAD, DK).transpose(0, 2, 1, 3)
        v = v.reshape(b, t, N_HEAD, DK).transpose(0, 2, 1, 3)
        attn = jnp.einsum('bhqd,bhkd->bhqk', q, k) * DK ** (-0.5)
        mask = jnp.triu(jnp.ones((t, t), dtype=bool), k=1)
        attn = jnp.where(mask, -jnp.inf, attn)
        attn = jax.nn.softmax(attn, axis=-1)
        out = jnp.einsum('bhqk,bhkd->bhqd', attn, v)
        out = out.transpose(0, 2, 1, 3).reshape(b, t, c)
        out = jnp.einsum('btc,oc->bto', out, w_proj)
        return out

    def _L0_ffn_ref(x, Wqkv, q_scale, k_scale, Wo, ln_g, ln_b, W1, b1, W2, b2):
        import jax, jax.numpy as jnp
        import numpy as np
        DIM = 128
        DEPTH = 6
        HEADS = 16
        DIM_HEAD = 64
        WINDOW = 32
        INNER = HEADS * DIM_HEAD
        DIM_INNER = int(DIM * 4 * 2 / 3)
        QK_SCALE = 8.0

        def shift_tokens(t):
            a, s = jnp.split(t, 2, -1)
            s = jnp.pad(s, ((0, 0), (1, 0), (0, 0)))[:, :-1]
            return jnp.concatenate([a, s], -1)

        def l2norm(t):
            return t / jnp.maximum(jnp.linalg.norm(t, axis=-1, keepdims=True), 1e-12)

        def rotate_half(x):
            x1, x2 = jnp.split(x, 2, -1)
            return jnp.concatenate([-x2, x1], -1)

        def rotary_tables(n):
            half = jnp.arange(0, DIM_HEAD, 2, dtype=jnp.float32)
            inv_freq = 1.0 / 10000.0 ** (half / DIM_HEAD)
            t = jnp.arange(n, dtype=jnp.float32)
            freqs = t[:, None] * inv_freq[None, :]
            freqs = jnp.concatenate([freqs, freqs], -1)
            base_scale = (half + 0.4 * DIM_HEAD) / (1.4 * DIM_HEAD)
            power = (t - n // 2) / (WINDOW // 2)
            scale = base_scale[None, :] ** power[:, None]
            scale = jnp.concatenate([scale, scale], -1)
            return (freqs, scale)

        def local_attention(q, k, v):
            b, h, n, d = q.shape
            w = WINDOW
            nw = n // w
            bq = q.reshape(b, h, nw, w, d)
            bk = k.reshape(b, h, nw, w, d)
            bv = v.reshape(b, h, nw, w, d)

            def look(t):
                p = jnp.pad(t, ((0, 0), (0, 0), (1, 0), (0, 0), (0, 0)))
                return jnp.concatenate([p[:, :, :nw], p[:, :, 1:]], axis=3)
            bk2, bv2 = (look(bk), look(bv))
            seq = jnp.arange(n).reshape(nw, w)
            seq_p = jnp.pad(seq, ((1, 0), (0, 0)), constant_values=-1)
            jt = jnp.concatenate([seq_p[:nw], seq_p[1:]], axis=1)
            it = seq[:, :, None]
            jb = jt[:, None, :]
            mask = (it < jb) | (it > jb + w) | (jb == -1)
            sim = jnp.einsum('bhwie,bhwje->bhwij', bq, bk2) * QK_SCALE
            sim = jnp.where(mask, -jnp.finfo(sim.dtype).max, sim)
            attn = jax.nn.softmax(sim, -1)
            out = jnp.einsum('bhwij,bhwje->bhwie', attn, bv2)
            return out.reshape(b, h, n, d)

        def attn_layer(x, Wqkv, qs, ksc, Wo):
            b, n, _ = x.shape
            qkv = x @ Wqkv
            q, k, v = jnp.split(qkv, 3, -1)
            sh = lambda t: t.reshape(b, n, HEADS, DIM_HEAD).transpose(0, 2, 1, 3)
            q, k, v = (sh(q), sh(k), sh(v))
            q = l2norm(q) * qs
            k = l2norm(k) * ksc
            freqs, scale = rotary_tables(n)
            cos, sin = (jnp.cos(freqs), jnp.sin(freqs))
            q = q * cos * scale + rotate_half(q) * sin * scale
            inv = 1.0 / scale
            k = k * cos * inv + rotate_half(k) * sin * inv
            out = local_attention(q, k, v)
            out = out.transpose(0, 2, 1, 3).reshape(b, n, INNER)
            return out @ Wo

        def ffn_layer(x, g, bln, W1, b1, W2, b2):
            mu = x.mean(-1, keepdims=True)
            var = ((x - mu) ** 2).mean(-1, keepdims=True)
            xn = (x - mu) / jnp.sqrt(var + 1e-05) * g + bln
            hg = xn @ W1 + b1
            a, gate = jnp.split(hg, 2, -1)
            return a * jax.nn.gelu(gate, approximate=False) @ W2 + b2
        for i in range(DEPTH):
            x = attn_layer(shift_tokens(x), Wqkv[i], q_scale[i], k_scale[i], Wo[i]) + x
            x = ffn_layer(shift_tokens(x), ln_g[i], ln_b[i], W1[i], b1[i], W2[i], b2[i]) + x
        return x
    x = L0_attn_x
    x = x + _layernorm(_L0_attn_ref(_layernorm(x, axis=-1), L0_attn_w_attn, L0_attn_w_proj), axis=-1)
    x = x + _layernorm(_L0_ffn_ref(_layernorm(x, axis=-1), L0_ffn_Wqkv, L0_ffn_q_scale, L0_ffn_k_scale, L0_ffn_Wo, L0_ffn_ln_g, L0_ffn_ln_b, L0_ffn_W1, L0_ffn_b1, L0_ffn_W2, L0_ffn_b2), axis=-1)
    return x

_drawn_inputs = setup_inputs


def setup_inputs(seed=0):
    import zlib

    import numpy as np

    out = dict(_drawn_inputs(seed))
    spreads = {'L0_ffn_q_scale': (1.0, 0.6),
     'L0_ffn_k_scale': (1.0, 0.6),
     'L0_ffn_ln_g': (1.0, 0.6),
     'L0_ffn_ln_b': (0.0, 0.8),
     'L0_ffn_b1': (0.0, 0.8),
     'L0_ffn_b2': (0.0, 0.348)}
    factors = {'L0_ffn_W1': 4.519, 'L0_ffn_W2': 4.42}
    for name, (base, spread) in spreads.items():
        noise = np.random.default_rng([zlib.crc32(name.encode()), seed]).standard_normal(out[name].shape)
        drawn = base * np.exp(spread * noise) if base else spread * noise
        out[name] = jnp.asarray(drawn.astype(out[name].dtype))
    for name, factor in factors.items():
        out[name] = (out[name] * factor).astype(out[name].dtype)
    return out
```

```python
from contextlib import ExitStack

import concourse.bass as bass
from concourse import mybir

F32 = mybir.dt.float32
BF16 = mybir.dt.bfloat16
ALU = mybir.AluOpType
ACT = mybir.ActivationFunctionType
AX = mybir.AxisListType

P = 128
WINDOW = 32
DIM_HEAD = 64
QK_SCALE = 8.0
LN_EPS = 1e-5
NORM_EPS = 1e-12
MASKED = -1e30
LOWEST = -3e38
BANK = 512
PARTS = 3
HEADS1 = 16


def sandwich_kernel(nc, x_in, w_attn, w_proj, wqkv, q_scale, k_scale, wo, ln_g, ln_b, w1, b1, w2, b2,
                    rot_tables, halo_factor, window_mask, out):
    T, C = x_in.shape[1], x_in.shape[2]
    NT = T // P
    NCH = T // BANK
    DK = C // HEADS1
    DEPTH = wqkv.shape[0]
    INNER = wqkv.shape[2] // 3
    HEADS = INNER // DIM_HEAD
    PAIRS = HEADS // 2
    FF = w2.shape[1]
    NF = 3
    FW = [(FF + NF - 1) // NF] * (NF - 1)
    FW.append(FF - sum(FW))
    FO = [sum(FW[:j]) for j in range(NF)]
    NW = P // WINDOW
    assert C == P and NW == 4 and NT % 4 == 0 and PAIRS == 8 and DIM_HEAD == 64

    def loop(eng, start, end):
        return nc.Fori(start, end, engines=(eng.engine,), hint_back_edge=True)

    outer = ExitStack()
    phase_sems = {}

    def clear_semaphores(ctx):
        nums = sorted(s.num for s in phase_sems[ctx])
        with nc.Block() as block:
            @block.gpsimd
            def _(g):
                start = nums[0]
                for a, b in zip(nums, nums[1:] + [None]):
                    if b != a + 1:
                        g.sem_clear(range(start, a + 1))
                        start = b

    with outer:
        def alloc(ctx):
            def sb(name, shape, dt=F32):
                return ctx.enter_context(nc.sbuf_tensor(name, shape, dt))

            def ps(name, shape, dt=F32):
                return ctx.enter_context(nc.psum_tensor(name, shape, dt))

            def sem(name):
                made = ctx.enter_context(nc.semaphore(name))
                phase_sems.setdefault(ctx, []).append(made)
                return made
            return sb, ps, sem

        sb, ps, sem = alloc(outer)
        q_parts = nc.dram_tensor("q_parts", [PARTS, P, T], BF16, kind="Internal").ap()
        k_parts = nc.dram_tensor("k_parts", [PARTS, P, T], BF16, kind="Internal").ap()
        o_heads = nc.dram_tensor("o_heads", [HEADS1, DK + 1, T], F32, kind="Internal").ap()

        ident = sb("ident", [P, P])
        ident_bf = sb("ident_bf", [P, P], BF16)
        mask_qk = sb("mask_qk", [P, P], BF16)
        mask_kq = sb("mask_kq", [P, P], BF16)
        xin = sb("xin", [P, NT, P])
        yrow = sb("yrow", [P, NT, P])
        ln_sq = sb("ln_sq", [P, NT, P])
        ln_mean = sb("ln_mean", [P, NT])
        ln_rstd = sb("ln_rstd", [P, NT])
        minus_half = sb("minus_half", [P, BANK // 8])
        Y = sb("Y", [P, T + 1])
        wproj_t = sb("wproj_t", [P, P])
        v_all = sb("v_all", [P, NT, P])

        const_made = sem("const_made")
        x_loaded = sem("x_loaded")

        def norm_steps(name, src, dst):
            s = {k: sem(f"{name}_{k}") for k in ("sum", "mean", "centred", "squared", "var", "eps", "rstd", "done")}

            def on_vector(v):
                v.tensor_reduce(ln_mean[:], src[:], AX.X, ALU.add).then_inc(s["sum"], 1)
                v.wait_ge(s["sum"], 1)
                v.tensor_scalar(ln_mean[:], ln_mean[:], 1.0 / C, None, ALU.mult).then_inc(s["mean"], 1)
                v.wait_ge(s["mean"], 1)
                v.tensor_tensor(dst[:], src[:], ln_mean[:].unsqueeze(2).broadcast_to([P, NT, C]),
                                ALU.subtract).then_inc(s["centred"], 1)
                v.wait_ge(s["squared"], 1)
                v.tensor_reduce(ln_rstd[:], ln_sq[:], AX.X, ALU.add).then_inc(s["var"], 1)
                v.wait_ge(s["var"], 1)
                v.tensor_scalar(ln_rstd[:], ln_rstd[:], 1.0 / C, LN_EPS, ALU.mult, ALU.add).then_inc(s["eps"], 1)
                v.wait_ge(s["rstd"], 1)
                v.tensor_tensor(dst[:], dst[:], ln_rstd[:].unsqueeze(2).broadcast_to([P, NT, C]),
                                ALU.mult).then_inc(s["done"], 1)

            def on_scalar(a):
                a.wait_ge(s["centred"], 1)
                a.activation(ln_sq[:], dst[:], ACT.Square).then_inc(s["squared"], 1)

            def on_gpsimd(g):
                g.wait_ge(s["eps"], 1)
                g.tensor_tensor(ln_rstd[:], ln_rstd[:], minus_half[:, 0:NT], ALU.pow).then_inc(s["rstd"], 1)
            return on_vector, on_scalar, on_gpsimd, s["done"]

        with ExitStack() as ctx:
            sb, ps, sem1 = alloc(ctx)
            w_rows = sb("w_rows", [P, 4, P])
            w_t = sb("w_t", [P, 3, P])
            xn_t = sb("xn_t", [P, T])
            part = [[sb(f"part{b}_{a}", [P, BANK], BF16) for a in range(PARTS)] for b in range(2)]
            rest = [sb(f"rest{b}", [P, BANK]) for b in range(2)]
            rest2 = [sb(f"rest2{b}", [P, BANK]) for b in range(2)]
            turned = [ps(f"turned{b}", [P, BANK]) for b in range(2)]
            proj = [ps(f"proj{b}", [P, BANK]) for b in range(2)]
            vproj = [ps(f"vproj{b}", [P, BANK]) for b in range(2)]
            turn_full, turn_free = sem1("turn_full"), sem1("turn_free")
            w_loaded = sem1("w_loaded")
            proj_full, proj_free = sem1("proj_full"), sem1("proj_free")
            p1_made, r1_made, p2_made, r2_made = (sem1(n) for n in ("p1_made", "r1_made", "p2_made", "r2_made"))
            parts_stored = [sem1(f"parts_stored{b}") for b in range(2)]
            v_full, v_free = sem1("v_full"), sem1("v_free")
            ln_vector, ln_scalar, ln_gpsimd, ln_done = norm_steps("ln0", xin, yrow)
            NQK = 2 * NCH
            NTURN = (NT + 4) // 4

            with nc.Block() as block:
                @block.sync
                def _(sp):
                    sp.dma_start(xin[:], x_in.rearrange("a (n p) c -> p (a n) c", p=P)).then_inc(x_loaded, 16)
                    sp.dma_start(w_rows[:, 0:3, :], w_attn.rearrange("(n p) c -> p n c", p=P)).then_inc(w_loaded, 16)
                    sp.dma_start(w_rows[:, 3, :], w_proj).then_inc(w_loaded, 16)
                    for u in range(NQK):
                        dst = k_parts if u % 2 else q_parts
                        cols = slice(u // 2 * BANK, (u // 2 + 1) * BANK)
                        sp.wait_ge(r2_made, u + 1)
                        for a in range(PARTS):
                            sp.dma_start(dst[a, :, cols], part[u % 2][a][:]).then_inc(parts_stored[u % 2], 16)
                    for b in range(2):
                        sp.wait_ge(parts_stored[b], 16 * PARTS * NCH)

                @block.gpsimd
                def _(g):
                    g.memset(ident[:], 0.0).then_inc(const_made, 1)
                    g.memset(ident_bf[:], 0.0).then_inc(const_made, 1)
                    g.memset(mask_qk[:], 0.0).then_inc(const_made, 1)
                    g.memset(mask_kq[:], 0.0).then_inc(const_made, 1)
                    g.memset(minus_half[:], -0.5).then_inc(const_made, 1)
                    g.wait_ge(const_made, 5)
                    for t in (ident, ident_bf):
                        g.affine_select(out=t[:], in_=t[:], compare_op=ALU.not_equal, fill=1.0, base=0,
                                        pattern=[[-1, P]], channel_multiplier=1).then_inc(const_made, 1)
                    g.affine_select(out=mask_qk[:], in_=mask_qk[:], compare_op=ALU.is_ge, fill=MASKED, base=0,
                                    pattern=[[-1, P]], channel_multiplier=1).then_inc(const_made, 1)
                    g.affine_select(out=mask_kq[:], in_=mask_kq[:], compare_op=ALU.is_ge, fill=MASKED, base=0,
                                    pattern=[[1, P]], channel_multiplier=-1).then_inc(const_made, 1)
                    ln_gpsimd(g)

                @block.vector
                def _(v):
                    v.wait_ge(x_loaded, 16)
                    ln_vector(v)
                    for u in range(NQK):
                        b = u % 2
                        v.wait_ge(p1_made, u + 1)
                        v.tensor_tensor(rest[b][:], proj[b][:], part[b][0][:], ALU.subtract).then_inc(r1_made, 1)
                        v.wait_ge(r1_made, u + 1)
                        v.tensor_copy(part[b][1][:], rest[b][:]).then_inc(p2_made, 1)
                        v.wait_ge(p2_made, u + 1)
                        v.tensor_tensor(part[b][2][:], rest[b][:], part[b][1][:], ALU.subtract).then_inc(r2_made, 1)

                @block.scalar
                def _(a):
                    ln_scalar(a)
                    for n in range(NTURN):
                        a.wait_ge(turn_full, n + 1)
                        if n == 0:
                            a.activation(w_t[:], turned[0][:, 0:3 * P].rearrange("p (n c) -> p n c", n=3),
                                         ACT.Copy)
                            a.activation(wproj_t[:], turned[0][:, 3 * P:4 * P], ACT.Copy).then_inc(turn_free, 1)
                        else:
                            a.activation(xn_t[:, (n - 1) * BANK:n * BANK], turned[n % 2][:],
                                         ACT.Copy).then_inc(turn_free, 1)
                    for u in range(NQK):
                        a.wait_ge(proj_full, u + 1)
                        if u >= 2:
                            a.wait_ge(parts_stored[u % 2], 16 * PARTS * (u // 2))
                        a.activation(part[u % 2][0][:], proj[u % 2][:], ACT.Copy).then_inc(p1_made, 1)
                    for n in range(NT // 4):
                        a.wait_ge(v_full, n + 1)
                        a.activation(v_all[:, 4 * n:4 * n + 4, :],
                                     vproj[n % 2][:].rearrange("p (n c) -> p n c", n=4),
                                     ACT.Copy).then_inc(v_free, 1)

                @block.tensor
                def _(pe):
                    pe.wait_ge(const_made, 9)
                    pe.wait_ge(w_loaded, 32)
                    for n in range(NTURN):
                        if n == 1:
                            pe.wait_ge(ln_done, 1)
                        if n >= 2:
                            pe.wait_ge(turn_free, n - 1)
                        for j in range(4):
                            src = w_rows[:, j, :] if n == 0 else yrow[:, 4 * (n - 1) + j, :]
                            last = pe.transpose(turned[n % 2][:, j * P:(j + 1) * P], src, ident[:])
                        last.then_inc(turn_full, 1)
                    for u in range(NQK):
                        pe.wait_ge(turn_free, u // 2 + 2)
                        if u >= 2:
                            pe.wait_ge(r1_made, u - 1)
                        pe.matmul(proj[u % 2][:], w_t[:, u % 2, :], xn_t[:, u // 2 * BANK:(u // 2 + 1) * BANK],
                                  start=True, stop=True).then_inc(proj_full, 1)
                    for n in range(NT // 4):
                        if n >= 2:
                            pe.wait_ge(v_free, n - 1)
                        for j in range(4):
                            t = 4 * n + j
                            last = pe.matmul(vproj[n % 2][:, j * P:(j + 1) * P], xn_t[:, t * P:(t + 1) * P],
                                             w_t[:, 2, :], start=True, stop=True)
                        last.then_inc(v_full, 1)
            clear_semaphores(ctx)

        with ExitStack() as ctx:
            sb, ps, sem1 = alloc(ctx)
            ROWS = PARTS * PARTS * DK
            MROW = 96
            KROWS = MROW + PARTS
            Qh = [sb(f"Qh{s}", [P, T], BF16) for s in range(2)]
            Kh = [sb(f"Kh{s}", [P, T], BF16) for s in range(2)]
            Vh = [sb(f"Vh{s}", [P, NT, DK + 1]) for s in range(2)]
            mpart = [sb(f"mpart{s}", [P, NT, NCH]) for s in range(2)]
            mrow = [sb(f"mrow{s}", [P, NT]) for s in range(2)]
            nm = [sb(f"nm{s}", [NT, PARTS, P], BF16) for s in range(2)]
            nrest = [sb(f"nrest{s}", [NT, P]) for s in range(2)]
            probs = [sb(f"probs{r}", [P, BANK]) for r in range(4)]
            Oh = [sb(f"Oh{s}", [DK + 1, T]) for s in range(2)]
            sc_bank = [ps(f"sc{r}", [P, BANK]) for r in range(2)]
            st_bank = [ps(f"st{r}", [P, BANK]) for r in range(4)]
            o_bank = [ps(f"o{r}", [P, BANK]) for r in range(2)]
            m_bank = sc_bank[0]
            qk_loaded = sem1("qk_loaded")
            rows_set = sem1("rows_set")
            vh_made = sem1("vh_made")
            sc_full, sc_free = sem1("sc_full"), sem1("sc_free")
            m_made, m_turned = sem1("m_made"), sem1("m_turned")
            n1, n2, n3, n4 = (sem1(n) for n in ("n1_made", "nrest_made", "n2_made", "n3_made"))
            m_placed = sem1("m_placed")
            st_full, exp_done, pv_done = sem1("st_full"), sem1("exp_done"), sem1("pv_done")
            o_free = sem1("o_free")
            o_stored = [sem1(f"o_stored{s}") for s in range(2)]

            max_units = [(i, kc) for i in range(NT) for kc in range(i // 4 + 1)]
            pv_units = [(c, j) for c in range(NCH) for j in range(4 * c + 4)]
            U = len(pv_units)
            assert len(max_units) == U
            PV_LAG = 2
            SPAN = U // 2
            FIRST = U // 4
            assert U % 4 == 0

            with nc.Block() as block:
                @block.sync
                def _(sp):
                    for s in range(2):
                        sp.sem_inc(o_stored[s], 16)
                    sp.wait_ge(rows_set, 4)

                    def load(h, s, free=True):
                        if free:
                            sp.wait_ge(rows_set, 4)
                            sp.wait_ge(pv_done, U * (h - 1))
                        for b in range(PARTS):
                            r0 = b * PARTS * DK
                            sp.dma_start(Qh[s][r0:r0 + PARTS * DK, :],
                                         q_parts[:, bass.ds(h * DK, DK), :]).then_inc(qk_loaded, 16)
                            for a in range(PARTS):
                                sp.dma_start(Kh[s][r0 + a * DK:r0 + (a + 1) * DK, :],
                                             k_parts[b, bass.ds(h * DK, DK), :]).then_inc(qk_loaded, 16)

                    def place_max(h, s):
                        sp.wait_ge(n4, h + 1)
                        for a in range(PARTS):
                            sp.dma_start(Qh[s][MROW + a:MROW + a + 1, :],
                                         nm[s][:, a, :]).then_inc(m_placed, 16)

                    def store(h, s):
                        sp.wait_ge(o_free, NCH * (h + 1))
                        sp.dma_start(o_heads[bass.ds(h, 1), :, :].rearrange("a d t -> (a d) t"),
                                     Oh[s][:]).then_inc(o_stored[s], 16)

                    load(0, 0, False)
                    load(1, 1, False)
                    place_max(0, 0)
                    place_max(1, 1)
                    store(0, 0)
                    load(2, 0)
                    with loop(sp, 0, HEADS1 // 2 - 2) as it:
                        for r in range(2):
                            h = it * 2 + (1 + r)
                            place_max(h + 1, r)
                            store(h, 1 - r)
                            load(h + 2, 1 - r)
                    h = HEADS1 - 3
                    place_max(h + 1, 0)
                    store(h, 1)
                    load(h + 2, 1)
                    place_max(h + 2, 1)
                    store(h + 1, 0)
                    store(h + 2, 1)
                    for s in range(2):
                        sp.wait_ge(o_stored[s], 16 * (HEADS1 // 2 + 1))

                @block.gpsimd
                def _(g):
                    g.memset(Vh[0][:], 1.0).then_inc(vh_made, 1)
                    g.memset(Vh[1][:], 1.0).then_inc(vh_made, 1)
                    g.wait_ge(vh_made, 2)
                    for s in range(2):
                        g.tensor_copy(Vh[s][:, :, 0:DK], v_all[:, :, s * DK:(s + 1) * DK]).then_inc(vh_made, 1)
                    with loop(g, 0, HEADS1 // 2 - 1) as it:
                        for s in range(2):
                            h = it * 2 + s
                            g.wait_ge(pv_done, U * (h + 1))
                            g.tensor_copy(Vh[s][:, :, 0:DK],
                                          v_all[:, :, bass.ds((h + 2) * DK, DK)]).then_inc(vh_made, 1)

                @block.vector
                def _(v):
                    for s in range(2):
                        v.memset(Qh[s][64:P, :], 0.0).then_inc(rows_set, 1)
                        v.memset(Kh[s][64:96, :], 0.0)
                        v.memset(Kh[s][96:P, :], 1.0).then_inc(rows_set, 1)
                        v.memset(mpart[s][:], LOWEST)

                    def maxima(h, s, u):
                        i, kc = max_units[u]
                        n = BANK if kc < i // 4 else P * (i % 4 + 1)
                        v.wait_ge(sc_full, h * U + (u + 1))
                        v.tensor_reduce(mpart[s][:, i, kc:kc + 1], sc_bank[u % 2][:, 0:n], AX.X,
                                        ALU.max).then_inc(sc_free, 1)

                    def row_max(h, s):
                        v.wait_ge(sc_free, (h + 1) * U)
                        if not isinstance(h, int) or h >= 2:
                            v.wait_ge(m_turned, h - 1)
                        v.tensor_reduce(mrow[s][:], mpart[s][:], AX.X, ALU.max).then_inc(m_made, 1)

                    def split_max(h, s):
                        mt = m_bank[0:NT, 0:P]
                        v.wait_ge(m_turned, h + 1)
                        if not isinstance(h, int) or h >= 2:
                            v.wait_ge(m_placed, 16 * PARTS * (h - 1))
                        v.tensor_scalar(nm[s][:, 0, :], mt, -1.0, None, ALU.mult).then_inc(n1, 1)
                        v.wait_ge(n1, h + 1)
                        v.scalar_tensor_tensor(out=nrest[s][:], in0=mt, scalar=-1.0, in1=nm[s][:, 0, :],
                                               op0=ALU.mult, op1=ALU.subtract).then_inc(n2, 1)
                        v.wait_ge(n2, h + 1)
                        v.tensor_copy(nm[s][:, 1, :], nrest[s][:]).then_inc(n3, 1)
                        v.wait_ge(n3, h + 1)
                        v.tensor_tensor(nm[s][:, 2, :], nrest[s][:], nm[s][:, 1, :],
                                        ALU.subtract).then_inc(n4, 1)

                    def take_out(h, s, c, before):
                        last = pv_units.index((c, 4 * c + 3))
                        v.wait_ge(pv_done, h * U + (last + 1))
                        if c == 0 and (not isinstance(h, int) or h >= 2):
                            v.wait_ge(o_stored[s], 16 * before + 16)
                        v.tensor_copy(Oh[s][:, c * BANK:(c + 1) * BANK],
                                      o_bank[c % 2][0:DK + 1, :]).then_inc(o_free, 1)

                    def step(h, s, with_max, with_pv, before=0):
                        for u in range(U):
                            if with_max and FIRST <= u < FIRST + SPAN:
                                for k in range(2):
                                    maxima(h + 1, 1 - s, 2 * (u - FIRST) + k)
                            if with_max and u == FIRST + SPAN:
                                row_max(h + 1, 1 - s)
                                split_max(h + 1, 1 - s)
                            if with_pv and pv_units[u][0] > 0 and pv_units[u][1] == 3:
                                take_out(h, s, pv_units[u][0] - 1, before)
                        if with_pv:
                            take_out(h, s, NCH - 1, before)

                    step(-1, 1, True, False)
                    step(0, 0, True, True)
                    with loop(v, 0, HEADS1 // 2 - 1) as it:
                        for r in range(2):
                            step(it * 2 + (1 + r), 1 - r, True, True, it + r if r else it)
                    step(HEADS1 - 1, 1, False, True, HEADS1 // 2 - 1)

                @block.scalar
                def _(a):
                    def head(h, s):
                        for u, (c, j) in enumerate(pv_units):
                            off = max(0, j - 4 * c) * P
                            a.wait_ge(st_full, h * U + (u + 1))
                            if not isinstance(h, int) or h * U + u >= len(probs):
                                a.wait_ge(pv_done, h * U + (u + 1 - len(probs)))
                            a.activation(probs[u % 4][:, off:BANK], st_bank[u % 4][:, off:BANK],
                                         ACT.Exp, scale=float(DK) ** -0.5).then_inc(exp_done, 1)
                    head(0, 0)
                    head(1, 1)
                    with loop(a, 1, HEADS1 // 2) as it:
                        for s in range(2):
                            head(it * 2 + s, s)

                @block.tensor
                def _(pe):
                    def scores_qk(h, s, u):
                        i, kc = max_units[u]
                        n = BANK if kc < i // 4 else P * (i % 4 + 1)
                        if not isinstance(h, int) or h * U + u >= 2:
                            pe.wait_ge(sc_free, h * U + (u - 1))
                        if u == 0 and (not isinstance(h, int) or h >= 1):
                            pe.wait_ge(n2, h)
                        last = kc == i // 4
                        mm = pe.matmul(sc_bank[u % 2][:, 0:n], Qh[s][0:MROW, i * P:(i + 1) * P],
                                       Kh[s][0:MROW, kc * BANK:kc * BANK + n], start=True, stop=not last,
                                       skip_group_check=True)
                        if last:
                            mm = pe.matmul(sc_bank[u % 2][:, n - P:n], ident_bf[:], mask_qk[:], start=False,
                                           stop=True, skip_group_check=True)
                        mm.then_inc(sc_full, 1)

                    def turn_max(h, s):
                        pe.wait_ge(m_made, h + 1)
                        pe.transpose(m_bank[0:NT, 0:P], mrow[s][:], ident[:]).then_inc(m_turned, 1)

                    def scores_kq(h, s, u):
                        c, j = pv_units[u]
                        off = max(0, j - 4 * c) * P
                        st = st_bank[u % 4]
                        lag = len(st_bank)
                        if not isinstance(h, int) or h * U + u >= lag:
                            pe.wait_ge(exp_done, h * U + (u + 1 - lag))
                        diag = j >= 4 * c
                        mm = pe.matmul(st[:, off:BANK], Kh[s][0:KROWS, j * P:(j + 1) * P],
                                       Qh[s][0:KROWS, c * BANK + off:(c + 1) * BANK], start=True, stop=not diag,
                                       skip_group_check=True)
                        if diag:
                            mm = pe.matmul(st[:, off:off + P], ident_bf[:], mask_kq[:], start=False, stop=True,
                                           skip_group_check=True)
                        mm.then_inc(st_full, 1)

                    def values(h, s, u):
                        c, j = pv_units[u]
                        off = max(0, j - 4 * c) * P
                        pe.wait_ge(exp_done, h * U + (u + 1))
                        if j == 0 and (not isinstance(h, int) or NCH * h + c >= 2):
                            pe.wait_ge(o_free, NCH * h + (c - 1))
                        mm = pe.matmul(o_bank[c % 2][0:DK + 1, off:BANK], Vh[s][:, j, :], probs[u % 4][:, off:BANK],
                                       start=(j == 0), stop=(j == 4 * c + 3), skip_group_check=True)
                        mm.then_inc(pv_done, 1)

                    def step(h, s, with_max, with_pv):
                        if with_pv:
                            pe.wait_ge(m_placed, 16 * PARTS * (h + 1))
                            pe.wait_ge(vh_made, h + 3)
                        for u in range(U + PV_LAG):
                            if with_max and u == FIRST:
                                loads = 2 if isinstance(h, int) and h < 0 else h + 2
                                pe.wait_ge(qk_loaded, 16 * 12 * loads)
                            if with_max and FIRST <= u < FIRST + SPAN:
                                for k in range(2):
                                    scores_qk(h + 1, 1 - s, 2 * (u - FIRST) + k)
                            if with_max and u == FIRST + SPAN + 1:
                                turn_max(h + 1, 1 - s)
                            if with_pv and u < U:
                                scores_kq(h, s, u)
                            if with_pv and u >= PV_LAG:
                                values(h, s, u - PV_LAG)

                    pe.wait_ge(rows_set, 4)
                    step(-1, 1, True, False)
                    step(0, 0, True, True)
                    with loop(pe, 0, HEADS1 // 2 - 1) as it:
                        for r in range(2):
                            step(it * 2 + (1 + r), 1 - r, True, True)
                    step(HEADS1 - 1, 1, False, True)
            clear_semaphores(ctx)

        with ExitStack() as ctx:
            sb, ps, sem1 = alloc(ctx)
            o_t = sb("o_t", [P, T])
            den = sb("den", [P, T])
            rden = sb("rden", [P, T])
            att = sb("att", [P, NT, P])
            banks = [ps(f"pbank{b}", [P, BANK]) for b in range(2)]
            tbanks = [ps(f"tbank{b}", [P, BANK]) for b in range(2)]
            o_loaded, r_made, on_made = sem1("o_loaded"), sem1("r_made"), sem1("on_made")
            a_full, a_free = sem1("a_full"), sem1("a_free")
            x1_made, t_full, t_free = sem1("x1_made"), sem1("t_full"), sem1("t_free")
            ln1 = norm_steps("ln1", att, yrow)
            ln2 = norm_steps("ln2", xin, yrow)
            with nc.Block() as block:
                @block.sync
                def _(sp):
                    for h in range(HEADS1):
                        sp.dma_start(o_t[h * DK:(h + 1) * DK, :], o_heads[h, 0:DK, :]).then_inc(o_loaded, 16)
                        sp.dma_start(den[h * DK:(h + 1) * DK, :],
                                     o_heads[h, DK:DK + 1, :].broadcast_to([DK, T])).then_inc(o_loaded, 16)

                @block.gpsimd
                def _(g):
                    ln1[2](g)
                    ln2[2](g)

                @block.vector
                def _(v):
                    v.memset(Y[:, 0:1], 0.0)
                    v.wait_ge(o_loaded, 16 * 2 * HEADS1)
                    v.reciprocal(rden[:], den[:]).then_inc(r_made, 1)
                    v.wait_ge(r_made, 1)
                    v.tensor_tensor(o_t[:], o_t[:], rden[:], ALU.mult).then_inc(on_made, 1)
                    v.wait_ge(a_free, NT // 4)
                    ln1[0](v)
                    v.wait_ge(ln1[3], 1)
                    v.tensor_tensor(xin[:], xin[:], yrow[:], ALU.add).then_inc(x1_made, 1)
                    v.wait_ge(x1_made, 1)
                    ln2[0](v)

                @block.scalar
                def _(a):
                    for n in range(NT // 4):
                        a.wait_ge(a_full, n + 1)
                        a.activation(att[:, 4 * n:4 * n + 4, :], banks[n % 2][:].rearrange("p (n c) -> p n c", n=4),
                                     ACT.Copy).then_inc(a_free, 1)
                    ln1[1](a)
                    ln2[1](a)
                    for n in range(NT // 4):
                        a.wait_ge(t_full, n + 1)
                        a.activation(Y[:, 1 + n * BANK:1 + (n + 1) * BANK], tbanks[n % 2][:],
                                     ACT.Copy).then_inc(t_free, 1)

                @block.tensor
                def _(pe):
                    pe.wait_ge(on_made, 1)
                    for n in range(NT // 4):
                        if n >= 2:
                            pe.wait_ge(a_free, n - 1)
                        for j in range(4):
                            t = 4 * n + j
                            last = pe.matmul(banks[n % 2][:, j * P:(j + 1) * P], o_t[:, t * P:(t + 1) * P],
                                             wproj_t[:], start=True, stop=True)
                        last.then_inc(a_full, 1)
                    pe.wait_ge(ln2[3], 1)
                    for n in range(NT // 4):
                        if n >= 2:
                            pe.wait_ge(t_free, n - 1)
                        for j in range(4):
                            last = pe.transpose(tbanks[n % 2][:, j * P:(j + 1) * P], yrow[:, 4 * n + j, :],
                                                ident[:])
                        last.then_inc(t_full, 1)
            clear_semaphores(ctx)

        with ExitStack() as ctx:
            sb, ps, sem2 = alloc(ctx)
            NCHK = INNER // BANK
            HC = BANK // DIM_HEAD
            PC = PAIRS // NCHK
            QKC = 2 * NCHK
            KW = WINDOW + P

            wqkv_sb = sb("wqkv_sb", [P, 3 * INNER])
            wo_sb = sb("wo_sb", [P, PAIRS, P])
            w1_sb = sb("w1_sb", [P, 2 * FF])
            w2_sb = sb("w2_sb", [FW[0], NF, P])
            qk_scales = sb("qk_scales", [P, 4, DIM_HEAD])
            g_col, b_col, b2_col = sb("g_col", [P, 1]), sb("b_col", [P, 1]), sb("b2_col", [P, 1])
            b1_col = sb("b1_col", [FW[0], 2, NF])
            rot = sb("rot", [P, NT, 4, DIM_HEAD])
            halo_col = sb("halo_col", [P, 1])
            wmask = sb("wmask", [P, NT // 2, P], BF16)
            wmask_f = sb("wmask_f", [P, NT // 2, P])
            Z = sb("Z", [P, T + 1])
            xs = [sb(f"xs{s}", [P, P]) for s in range(2)]
            tab = [sb(f"tab{s}", [P, 4, DIM_HEAD]) for s in range(2)]
            squares = [sb(f"squares{m}", [P, HC, DIM_HEAD]) for m in range(QKC)]
            ssum = [sb(f"ssum{m}", [P, HC]) for m in range(QKC)]
            rnorm = [sb(f"rnorm{m}", [P, HC]) for m in range(QKC)]
            qk_n = [sb(f"qk_n{m}", [P, HC, DIM_HEAD]) for m in range(QKC)]
            prod_c = [sb(f"prod_c{m}", [P, HC, DIM_HEAD]) for m in range(QKC)]
            prod_s = [sb(f"prod_s{m}", [P, HC, DIM_HEAD]) for m in range(QKC)]
            qbd = sb("qbd", [P, PAIRS, NW, 2, WINDOW])
            kt = [sb(f"kt{s}", [P, PAIRS, KW]) for s in range(2)]
            v_even = [sb(f"v_even{s}", [P, INNER]) for s in range(2)]
            v_odd = [sb(f"v_odd{s}", [P, INNER]) for s in range(2)]
            G = PC * 2
            smax = [sb(f"smax{b}", [P, G]) for b in range(2)]
            ssx = [sb(f"ssx{b}", [P, G, 2 * WINDOW]) for b in range(2)]
            den = [sb(f"wden{b}", [P, G]) for b in range(2)]
            rden = [sb(f"wrden{b}", [P, G]) for b in range(2)]
            probs = [sb(f"wprobs{b}", [P, G, 2 * WINDOW]) for b in range(2)]
            ptbd = sb("ptbd", [P, PAIRS, 2, 2, 2 * WINDOW])
            ot = sb("ot", [P, PAIRS, P])
            sx = sb("sx", [P, BANK])
            stats = sb("stats", [P, 4, 6])
            mv = sb("mv", [P, 4, 2])
            frstd = sb("frstd", [P, 4])
            xr = sb("xr", [P, 4, P])
            xn = sb("xn", [P, BANK])
            gate = [sb(f"gate{j}", [FW[0], BANK]) for j in range(NF)]
            hid = [sb(f"hid{j}", [FW[0], BANK]) for j in range(NF)]

            pj = [ps(f"pj{b}", [P, BANK]) for b in range(2)]
            tb = [ps(f"tb{b}", [P, BANK]) for b in range(2)]
            sb_ = [ps(f"sb{b}", [P, BANK]) for b in range(2)]
            ub = [ps(f"ub{b}", [P, BANK]) for b in range(2)]

            def fbank(j, k):
                return (sb_ if j == 1 else pj)[k]

            def per(name, count):
                return [sem2(f"{name}{m}") for m in range(count)]
            inits = sem2("inits")
            consts_loaded = sem2("consts_loaded")
            mask_made = sem2("mask_made")
            attn_w, ffn_w = sem2("attn_w"), sem2("ffn_w")
            shifted, tabled = sem2("shifted"), sem2("tabled")
            proj_full = per("wproj_full", 6)
            squared, summed, clamped, rsqrted, normed = (per(x, QKC) for x in
                                                         ("squared", "summed", "clamped", "rsqrted", "normed"))
            v_made = per("v_made", 2)
            cos_done, sin_done = per("cos_done", QKC), per("sin_done", QKC)
            turn_full, turn_taken = per("wturn_full", QKC), per("wturn_taken", QKC)
            halo_made, odd_made = sem2("halo_made"), sem2("odd_made")
            sc_full, sc_max, sc_taken, exped, den_made, rden_made, prob_made = (
                per(x, 2) for x in ("wsc_full", "sc_max", "sc_taken", "exped", "den_made", "rden_made", "prob_made"))
            pt_full, pt_taken = per("pt_full", 2), per("pt_taken", 2)
            pv_full, pv_taken = per("pv_full", 4), per("pv_taken", 4)
            wo_full, z_made = sem2("wo_full"), sem2("z_made")
            y_made = sem2("y_made")
            f_shifted, f_turned, f_stats, f_mv, f_eps, f_rstd, f_rows, f_back, f_xn = (
                sem2(x) for x in ("f_shifted", "f_turned", "f_stats", "f_mv", "f_eps", "f_rstd", "f_rows",
                                  "f_back", "f_xn"))
            gate_full, val_full, gated, hid_made = (per(x, NF) for x in ("gate_full", "val_full", "gated", "hid_made"))
            f_out = sem2("f_out")

            ahead = {
                "sync": [(odd_made, 32)],
                "gpsimd": [(q, 1) for q in (tabled, *rsqrted, *sin_done, *prob_made, f_rstd)],
                "vector": [(q, 1) for q in (shifted, *summed, *clamped, *normed, *cos_done, halo_made, *sc_max,
                                            *sc_taken, *den_made, *rden_made, z_made, y_made, f_stats, f_mv,
                                            f_eps, f_rows, *hid_made)],
                "scalar": [(q, 1) for q in (*squared, *v_made, *turn_taken, *exped, *pt_taken, *pv_taken,
                                            f_shifted, f_xn, *gated)],
                "tensor": [(q, 1) for q in (*proj_full, *turn_full, *sc_full, *pt_full, *pv_full, wo_full,
                                            f_turned, f_back, *gate_full, *val_full, f_out)],
            }

            def start_ahead(eng, name):
                for q, count in ahead[name]:
                    eng.sem_inc(q, count)

            def earlier(n, i):
                return n if isinstance(i, int) and i == 0 else n - 1

            def run_tiles(eng, l, first, both, second):
                base = l * NT + 1
                first(base, 0, 0)
                with loop(eng, 0, NT // 2 - 1) as it:
                    for s in range(2):
                        i = it * 2 + s
                        both(base + i, i, s)
                both(base + (NT - 2), NT - 2, 0)
                second(base + (NT - 1), NT - 1, 1)

            def run_chunks(eng, l, norm, step, mlp):
                base = l * NCH + 1
                norm(base, 0)
                if NCH > 1:
                    with loop(eng, 0, NCH - 1) as c:
                        step(base + c, c)
                mlp(base + (NCH - 1), NCH - 1)

            with nc.Block() as block:
                @block.sync
                def _(sp):
                    start_ahead(sp, "sync")
                    sp.dma_start(rot[:], rot_tables.rearrange("(n p) (k d) -> p n k d", p=P, k=4)).then_inc(consts_loaded, 16)
                    sp.dma_start(halo_col[:], halo_factor).then_inc(consts_loaded, 16)
                    sp.dma_start(wmask_f[:], window_mask).then_inc(consts_loaded, 16)

                    def shift_values(n, s):
                        sp.wait_ge(v_made[0], n + 1)
                        sp.wait_ge(v_made[1], n + 1)
                        sp.dma_start(v_odd[s][WINDOW:P, :], v_even[s][0:P - WINDOW, :]).then_inc(odd_made, 16)
                        sp.dma_start(v_odd[s][0:WINDOW, :], v_even[1 - s][P - WINDOW:P, :]).then_inc(odd_made, 16)

                    def load_attention(l):
                        sp.wait_ge(consts_loaded, 48)
                        sp.wait_ge(z_made, l * NT + 1)
                        sp.wait_ge(tabled, l * NT + 1)
                        wl = bass.ds(l, 1)
                        for k, src in enumerate((q_scale, q_scale, k_scale, k_scale)):
                            sp.dma_start(qk_scales[:, k, :], src[wl, :].broadcast_to([P, DIM_HEAD])).then_inc(attn_w, 16)
                        sp.dma_start(wqkv_sb[:], wqkv[wl, :, :].rearrange("a c n -> (a c) n")).then_inc(attn_w, 16)
                        sp.dma_start(wo_sb[:], wo[wl, :, :].rearrange("a (n p) c -> p (a n) c", p=P)).then_inc(attn_w, 16)

                    def load_ffn(l):
                        sp.wait_ge(consts_loaded, 48)
                        sp.wait_ge(y_made, l * NCH + (NCH + 1))
                        wl = bass.ds(l, 1)
                        for dst, src in ((g_col, ln_g), (b_col, ln_b), (b2_col, b2)):
                            sp.dma_start(dst[:], src[wl, :].rearrange("a p -> p a")).then_inc(ffn_w, 16)
                        for k in range(2):
                            for j in range(NF):
                                sp.dma_start(b1_col[0:FW[j], k, j:j + 1],
                                             b1[wl, k * FF + FO[j]:k * FF + FO[j] + FW[j]].rearrange("a p -> p a")
                                             ).then_inc(ffn_w, 16)
                        sp.dma_start(w1_sb[:], w1[wl, :, :].rearrange("a c n -> (a c) n")).then_inc(ffn_w, 16)
                        for j in range(NF):
                            sp.dma_start(w2_sb[0:FW[j], j, :],
                                         w2[wl, FO[j]:FO[j] + FW[j], :].rearrange("a c n -> (a c) n")).then_inc(ffn_w, 16)

                    with loop(sp, 0, DEPTH) as l:
                        load_attention(l)
                        shift_values(l * NT + 1, 0)
                        load_ffn(l)
                        with loop(sp, 0, NT // 2 - 1) as it:
                            for s in range(2):
                                shift_values(l * NT + it * 2 + (s + 2), 1 - s)
                        shift_values(l * NT + NT, 1)
                    for q, count in ((consts_loaded, 3), (attn_w, 6 * DEPTH), (ffn_w, 13 * DEPTH),
                                     (odd_made, 2 * NT * DEPTH + 2)):
                        sp.wait_ge(q, 16 * count)

                @block.gpsimd
                def _(g):
                    start_ahead(g, "gpsimd")
                    g.memset(kt[1][:], 0.0).then_inc(inits, 1)
                    g.memset(v_even[1][:], 0.0).then_inc(inits, 1)
                    g.memset(qbd[:], 0.0).then_inc(inits, 1)
                    g.memset(ptbd[:], 0.0).then_inc(inits, 1)

                    def make_table(n, i, s):
                        g.wait_ge(attn_w, (layer[0] + 1) * (16 * 6))
                        g.wait_ge(cos_done[QKC - 1], earlier(n, i))
                        g.tensor_tensor(tab[s][:], rot[:, bass.ds(i, 1), :, :].rearrange("p a k d -> p (a k) d"),
                                        qk_scales[:], ALU.mult).then_inc(tabled, 1)

                    layer = [None]

                    def power(n, m):
                        g.wait_ge(clamped[m], n + 1)
                        g.tensor_tensor(rnorm[m][:], ssum[m][:], minus_half[:, 0:HC], ALU.pow).then_inc(rsqrted[m], 1)

                    def sines(n, m, s):
                        g.wait_ge(normed[m], n + 1)
                        g.wait_ge(turn_full[m], n)
                        k = 2 * (m // NCHK) + 1
                        table = tab[s][:, k, :].rearrange("p (t d) -> p t d", t=2).unsqueeze(1)
                        src = qk_n[m][:].rearrange("p h (t d) -> p h t d", t=2)
                        dst = prod_s[m][:].rearrange("p h (t d) -> p h t d", t=2)
                        g.tensor_tensor(dst[:, :, ::-1, :], src, table.broadcast_to([P, HC, 2, DIM_HEAD // 2]),
                                        ALU.mult).then_inc(sin_done[m], 1)

                    def normalise(n, b):
                        g.wait_ge(rden_made[b], n + 1)
                        g.wait_ge(pt_full[b], n)
                        g.tensor_tensor(probs[b][:], ssx[b][:],
                                        rden[b][:].unsqueeze(2).broadcast_to([P, G, 2 * WINDOW]),
                                        ALU.mult).then_inc(prob_made[b], 1)

                    def first(n, i, s):
                        make_table(n, i, s)
                        for m in range(QKC):
                            power(n, m)
                            sines(n, m, s)

                    def both(n, i, s):
                        make_table(n + 1, i + 1, 1 - s)
                        power(n + 1, 0)
                        power(n + 1, 1)
                        normalise(n, 0)
                        normalise(n, 1)
                        power(n + 1, 2)
                        power(n + 1, 3)
                        for m in range(QKC):
                            sines(n + 1, m, 1 - s)

                    def second(n, i, s):
                        normalise(n, 0)
                        normalise(n, 1)

                    def norm(n, c):
                        g.wait_ge(f_eps, n + 1)
                        g.tensor_tensor(frstd[:], frstd[:], minus_half[:, 0:4], ALU.pow).then_inc(f_rstd, 1)

                    g.wait_ge(consts_loaded, 48)
                    with loop(g, 0, DEPTH) as l:
                        layer[0] = l
                        run_tiles(g, l, first, both, second)
                        run_chunks(g, l, norm, lambda n, c: norm(n + 1, c + 1), lambda n, c: None)

                @block.vector
                def _(v):
                    start_ahead(v, "vector")
                    v.memset(Z[:, 0:1], 0.0)
                    v.wait_ge(consts_loaded, 48)
                    v.tensor_copy(wmask[:], wmask_f[:]).then_inc(mask_made, 1)
                    for c in range(NCH):
                        v.memset(xr[:, 0, c:c + 1], 0.0).then_inc(y_made, 1)

                    half = P // 2
                    layer = [None]

                    def shift_tile(n, i, s):
                        chunks = NCH if not isinstance(i, int) else i // 4 + 1
                        v.wait_ge(y_made, layer[0] * NCH + (chunks + 1))
                        v.wait_ge(proj_full[5], earlier(n, i))
                        v.tensor_copy(xs[s][0:half, :], Y[0:half, bass.ds(i * P + 1, P)])
                        v.tensor_copy(xs[s][half:P, :], Y[half:P, bass.ds(i * P, P)]).then_inc(shifted, 1)

                    def sums(n, m):
                        v.wait_ge(squared[m], n + 1)
                        v.tensor_reduce(ssum[m][:], squares[m][:], AX.X, ALU.add).then_inc(summed[m], 1)
                        v.wait_ge(summed[m], n + 1)
                        v.tensor_scalar(ssum[m][:], ssum[m][:], NORM_EPS ** 2, None, ALU.max).then_inc(clamped[m], 1)

                    def scale(n, m):
                        v.wait_ge(rsqrted[m], n + 1)
                        v.wait_ge(sin_done[m], n)
                        src = pj[m % 2][:].rearrange("p (h d) -> p h d", h=HC)
                        v.tensor_tensor(qk_n[m][:], src, rnorm[m][:].unsqueeze(2).broadcast_to([P, HC, DIM_HEAD]),
                                        ALU.mult).then_inc(normed[m], 1)

                    def cosines(n, m, s):
                        v.wait_ge(normed[m], n + 1)
                        v.wait_ge(turn_full[m], n)
                        v.wait_ge(tabled, n + 1)
                        k = 2 * (m // NCHK)
                        v.tensor_tensor(prod_c[m][:], qk_n[m][:],
                                        tab[s][:, k, :].unsqueeze(1).broadcast_to([P, HC, DIM_HEAD]),
                                        ALU.mult).then_inc(cos_done[m], 1)

                    def halo(n, s):
                        for m in range(NCHK, QKC):
                            v.wait_ge(turn_taken[m], n)
                        v.wait_ge(sc_full[1], n - 1 if s is not None and not first_tile[0] else n)
                        v.tensor_scalar(kt[s][:, :, 0:WINDOW], kt[1 - s][:, :, P:KW], halo_col[:, 0:1], None,
                                        ALU.mult).then_inc(halo_made, 1)

                    first_tile = [False]

                    def soft_in(n, b):
                        v.wait_ge(sc_full[b], n + 1)
                        src = sb_[b][:].rearrange("p (g k) -> p g k", g=G)
                        v.tensor_reduce(smax[b][:], src, AX.X, ALU.max).then_inc(sc_max[b], 1)
                        v.wait_ge(sc_max[b], n + 1)
                        v.wait_ge(prob_made[b], n)
                        v.tensor_tensor(ssx[b][:], src, smax[b][:].unsqueeze(2).broadcast_to([P, G, 2 * WINDOW]),
                                        ALU.subtract).then_inc(sc_taken[b], 1)

                    def soft_sum(n, b):
                        v.wait_ge(exped[b], n + 1)
                        v.tensor_reduce(den[b][:], ssx[b][:], AX.X, ALU.add).then_inc(den_made[b], 1)
                        v.wait_ge(den_made[b], n + 1)
                        v.reciprocal(rden[b][:], den[b][:]).then_inc(rden_made[b], 1)

                    def add_stream(n, i):
                        v.wait_ge(wo_full, n + 1)
                        v.tensor_tensor(Z[:, bass.ds(i * P + 1, P)], ub[0][:, 0:P], Y[:, bass.ds(i * P + 1, P)],
                                        ALU.add).then_inc(z_made, 1)

                    def first(n, i, s):
                        shift_tile(n, 0, 0)
                        shift_tile(n + 1, 1, 1)
                        for m in range(QKC):
                            sums(n, m)
                            scale(n, m)
                            cosines(n, m, s)
                        first_tile[0] = True
                        halo(n, s)
                        first_tile[0] = False

                    def both(n, i, s):
                        sums(n + 1, 0)
                        sums(n + 1, 1)
                        soft_in(n, 0)
                        scale(n + 1, 0)
                        soft_in(n, 1)
                        scale(n + 1, 1)
                        soft_sum(n, 0)
                        sums(n + 1, 2)
                        soft_sum(n, 1)
                        sums(n + 1, 3)
                        cosines(n + 1, 0, 1 - s)
                        cosines(n + 1, 1, 1 - s)
                        scale(n + 1, 2)
                        scale(n + 1, 3)
                        cosines(n + 1, 2, 1 - s)
                        cosines(n + 1, 3, 1 - s)
                        halo(n + 1, 1 - s)
                        if not isinstance(i, int) or i + 2 < NT:
                            shift_tile(n + 2, i + 2, s)
                        add_stream(n, i)

                    def second(n, i, s):
                        soft_in(n, 0)
                        soft_in(n, 1)
                        soft_sum(n, 0)
                        soft_sum(n, 1)
                        add_stream(n, i)

                    def norm(n, c):
                        v.wait_ge(f_turned, n + 1)
                        for k in range(4):
                            last = v.bn_stats(stats[:, k, :], tb[0][:, k * P:(k + 1) * P])
                        last.then_inc(f_stats, 1)
                        v.wait_ge(consts_loaded, 48)
                        v.wait_ge(f_stats, n + 1)
                        for k in range(4):
                            last = v.bn_aggr(mv[:, k, :], stats[:, k, :])
                        last.then_inc(f_mv, 1)
                        v.wait_ge(f_mv, n + 1)
                        v.tensor_scalar(frstd[:], mv[:, :, 1], LN_EPS, None, ALU.add).then_inc(f_eps, 1)
                        v.wait_ge(f_rstd, n + 1)
                        for k in range(4):
                            last = v.tensor_scalar(xr[:, k, :], tb[0][:, k * P:(k + 1) * P], mv[:, k, 0:1],
                                                   frstd[:, k:k + 1], ALU.subtract, ALU.mult)
                        last.then_inc(f_rows, 1)

                    def hidden(n, j):
                        v.wait_ge(val_full[j], n + 1)
                        v.wait_ge(gated[j], n + 1)
                        v.scalar_tensor_tensor(out=hid[j][0:FW[j], :], in0=fbank(j, 1)[0:FW[j], :],
                                               scalar=b1_col[0:FW[j], 0, j:j + 1], in1=gate[j][0:FW[j], :],
                                               op0=ALU.add, op1=ALU.mult).then_inc(hid_made[j], 1)

                    def add_ffn(n, c):
                        v.wait_ge(f_out, n + 1)
                        cols = bass.ds(c * BANK + 1, BANK)
                        v.scalar_tensor_tensor(out=Y[:, cols], in0=ub[0][:], scalar=b2_col[:, 0:1], in1=Z[:, cols],
                                               op0=ALU.add, op1=ALU.add).then_inc(y_made, 1)

                    def mlp(n, c):
                        for j in range(NF):
                            hidden(n, j)
                        add_ffn(n, c)

                    def step(n, c):
                        hidden(n, 0)
                        norm(n + 1, c + 1)
                        hidden(n, 1)
                        hidden(n, 2)
                        add_ffn(n, c)

                    with loop(v, 0, DEPTH) as l:
                        layer[0] = l
                        run_tiles(v, l, first, both, second)
                        v.wait_ge(ffn_w, (l + 1) * (16 * 13))
                        run_chunks(v, l, norm, step, mlp)

                @block.scalar
                def _(a):
                    def square(n, m):
                        a.wait_ge(proj_full[m], n + 1)
                        a.activation(squares[m][:], pj[m % 2][:].rearrange("p (h d) -> p h d", h=HC),
                                     ACT.Square).then_inc(squared[m], 1)

                    def take_v(n, i, k, s):
                        a.wait_ge(proj_full[QKC + k], n + 1)
                        a.wait_ge(pv_full[3], earlier(n, i))
                        a.wait_ge(odd_made, n * 32)
                        a.activation(v_even[s][:, k * BANK:(k + 1) * BANK], pj[k][:], ACT.Copy).then_inc(v_made[k], 1)

                    def take_q(n, m):
                        a.wait_ge(turn_full[m], n + 1)
                        a.wait_ge(sc_full[1], n)
                        half = P // 2
                        for h in range(2):
                            rows = slice(h * half, (h + 1) * half)
                            last = a.activation(qbd[rows, m * PC:(m + 1) * PC, :, h, :],
                                                tb[m % 2][rows, :].rearrange("p (a w q) -> p a w q", a=PC, w=NW), ACT.Copy)
                        last.then_inc(turn_taken[m], 1)

                    def take_k(n, i, m, s):
                        a.wait_ge(turn_full[m], n + 1)
                        a.wait_ge(halo_made, n)
                        a.wait_ge(sc_full[1], earlier(n, i))
                        k = m - NCHK
                        a.activation(kt[s][:, k * PC:(k + 1) * PC, WINDOW:KW],
                                     tb[m % 2][:].rearrange("p (a t) -> p a t", a=PC), ACT.Copy).then_inc(turn_taken[m], 1)

                    def exps(n, b):
                        a.wait_ge(sc_taken[b], n + 1)
                        a.activation(ssx[b][:], ssx[b][:], ACT.Exp, scale=QK_SCALE).then_inc(exped[b], 1)

                    def take_pt(n, b):
                        a.wait_ge(pt_full[b], n + 1)
                        a.wait_ge(pv_full[3], n)
                        half = P // 2
                        for w in range(2):
                            rows = slice(w * half, (w + 1) * half)
                            last = a.activation(ptbd[rows, b * PC:(b + 1) * PC, :, w, :],
                                                ub[b][rows, :].rearrange("p (a g q) -> p a g q", a=PC, g=2), ACT.Copy)
                        last.then_inc(pt_taken[b], 1)

                    def take_o(n, u):
                        a.wait_ge(pv_full[u], n + 1)
                        a.wait_ge(wo_full, n)
                        half = P // 2
                        for h in range(2):
                            rows = slice(h * half, (h + 1) * half)
                            src = ub[u % 2][rows, :].rearrange("p (aw h q) -> p aw h q", h=2, q=2 * WINDOW)[:, :, h, :]
                            last = a.activation(ot[rows, 2 * u:2 * u + 2, :].rearrange("p a (w q) -> p (a w) q", w=2),
                                                src, ACT.Copy)
                        last.then_inc(pv_taken[u], 1)

                    def first(n, i, s):
                        for m in range(QKC):
                            square(n, m)
                        take_v(n, i, 0, s)
                        take_v(n, i, 1, s)
                        take_q(n, 0)
                        take_q(n, 1)
                        take_k(n, i, 2, s)
                        take_k(n, i, 3, s)

                    def both(n, i, s):
                        square(n + 1, 0)
                        square(n + 1, 1)
                        exps(n, 0)
                        exps(n, 1)
                        square(n + 1, 2)
                        square(n + 1, 3)
                        take_v(n + 1, i + 1, 0, 1 - s)
                        take_pt(n, 0)
                        take_pt(n, 1)
                        take_v(n + 1, i + 1, 1, 1 - s)
                        take_o(n, 0)
                        take_o(n, 1)
                        take_q(n + 1, 0)
                        take_q(n + 1, 1)
                        take_o(n, 2)
                        take_o(n, 3)
                        take_k(n + 1, i + 1, 2, 1 - s)
                        take_k(n + 1, i + 1, 3, 1 - s)

                    def second(n, i, s):
                        exps(n, 0)
                        exps(n, 1)
                        take_pt(n, 0)
                        take_pt(n, 1)
                        for u in range(4):
                            take_o(n, u)

                    def shift(l, n, c):
                        a.wait_ge(z_made, l * NT + ((NT if not isinstance(c, int) else 4 * c + 4) + 1))
                        half = P // 2
                        a.activation(sx[0:half, :], Z[0:half, bass.ds(c * BANK + 1, BANK)], ACT.Copy)
                        a.activation(sx[half:P, :], Z[half:P, bass.ds(c * BANK, BANK)], ACT.Copy).then_inc(f_shifted, 1)

                    def scale_rows(n):
                        a.wait_ge(f_back, n + 1)
                        a.activation(xn[:], tb[1][:], ACT.Identity, bias=b_col[:, 0:1],
                                     scale=g_col[:, 0:1]).then_inc(f_xn, 1)

                    def gelu(n, j):
                        a.wait_ge(gate_full[j], n + 1)
                        a.activation(gate[j][0:FW[j], :], fbank(j, 0)[0:FW[j], :], ACT.Gelu,
                                     bias=b1_col[0:FW[j], 1, j:j + 1]).then_inc(gated[j], 1)

                    start_ahead(a, "scalar")
                    a.wait_ge(inits, 4)
                    with loop(a, 0, DEPTH) as l:
                        def norm(n, c):
                            shift(l, n, c)
                            scale_rows(n)

                        def step(n, c):
                            gelu(n, 0)
                            shift(l, n + 1, c + 1)
                            gelu(n, 1)
                            gelu(n, 2)
                            a.wait_ge(val_full[NF - 1], n + 1)
                            scale_rows(n + 1)

                        def mlp(n, c):
                            for j in range(NF):
                                gelu(n, j)

                        run_tiles(a, l, first, both, second)
                        a.wait_ge(ffn_w, (l + 1) * (16 * 13))
                        run_chunks(a, l, norm, step, mlp)

                @block.tensor
                def _(pe):
                    def project(n, m, s, l0=None):
                        if m == 0:
                            pe.wait_ge(shifted, n + 1)
                        if m < 2:
                            pe.wait_ge(v_made[m], n)
                        else:
                            pe.wait_ge(normed[m - 2], n + 1)
                        pe.matmul(pj[m % 2][:], xs[s][:], wqkv_sb[:, m * BANK:(m + 1) * BANK], start=True,
                                  stop=True).then_inc(proj_full[m], 1)

                    def turn(n, m):
                        pe.wait_ge(cos_done[m], n + 1)
                        pe.wait_ge(sin_done[m], n + 1)
                        if m < 2:
                            pe.wait_ge(turn_taken[m + 2], n)
                        else:
                            pe.wait_ge(turn_taken[m - 2], n + 1)
                        for a in range(PC):
                            for k, src in enumerate((prod_c, prod_s)):
                                last = pe.matmul(tb[m % 2][:, a * P:(a + 1) * P],
                                                 src[m][:].rearrange("p h d -> p (h d)")[:, a * P:(a + 1) * P], ident[:],
                                                 start=(k == 0), stop=(k == 1), is_transpose=True, skip_group_check=True)
                        last.then_inc(turn_full[m], 1)

                    def scores(n, i, b, s):
                        pe.wait_ge(sc_taken[b], n)
                        for m in (b, b + 2):
                            pe.wait_ge(turn_taken[m], n + 1)
                        pe.wait_ge(halo_made, n + 1)
                        even = s == 0
                        which = (i // 2 if isinstance(i, int) else None) if even else 1
                        mask = wmask[:, which:which + 1, :] if which is not None else wmask[:, bass.ds(pair_index[0], 1), :]
                        pe.matmul(sb_[b][:], ident_bf[:], mask.broadcast_to([P, PC, P]), start=True, stop=False,
                                  skip_group_check=True)
                        for a in range(PC):
                            pair = b * PC + a
                            for g in range(2):
                                for w in range(2):
                                    win = 2 * w + g
                                    col = (2 * a + w) * 2 * WINDOW
                                    last = pe.matmul(sb_[b][64 * g:64 * g + 64, col:col + 2 * WINDOW],
                                                     qbd[:, pair, win, :, :].rearrange("p h q -> p (h q)"),
                                                     kt[s][:, pair, win * WINDOW:win * WINDOW + 2 * WINDOW],
                                                     start=False, stop=True, skip_group_check=True)
                        last.then_inc(sc_full[b], 1)

                    def turn_probs(n, b):
                        pe.wait_ge(prob_made[b], n + 1)
                        if b == 0:
                            pe.wait_ge(z_made, n)
                        else:
                            pe.wait_ge(pv_taken[3], n)
                        for a in range(PC):
                            last = pe.transpose(ub[b][:, a * P:(a + 1) * P],
                                                probs[b][:].rearrange("p g k -> p (g k)")[:, a * P:(a + 1) * P], ident[:])
                        last.then_inc(pt_full[b], 1)

                    def values(n, u, s):
                        pe.wait_ge(pt_taken[u // 2], n + 1)
                        if u < 2:
                            pe.wait_ge(pt_taken[u], n + 1)
                            if u == 0:
                                pe.wait_ge(odd_made, n * 32 + 32)
                                pe.wait_ge(v_made[1], n + 1)
                        else:
                            pe.wait_ge(pv_taken[u - 2], n + 1)
                        for a in range(2):
                            pair = 2 * u + a
                            for g in range(2):
                                vals = (v_odd if g == 0 else v_even)[s]
                                dst = ub[u % 2][:, a * 256:(a + 1) * 256].rearrange(
                                    "p (wh g q) -> p wh g q", g=2, q=WINDOW)[:, :, g, :]
                                last = pe.matmul(dst, vals[:, pair * P:(pair + 1) * P],
                                                 ptbd[:, pair, g, :, :].rearrange("p w (h q) -> p (w h) q", h=2),
                                                 start=True, stop=True, skip_group_check=True)
                        last.then_inc(pv_full[u], 1)

                    def project_out(n):
                        pe.wait_ge(pv_taken[2], n + 1)
                        pe.wait_ge(pv_taken[3], n + 1)
                        for pair in range(PAIRS):
                            last = pe.matmul(ub[0][:, 0:P], wo_sb[:, pair, :], ot[:, pair, :], start=(pair == 0),
                                             stop=(pair == PAIRS - 1))
                        last.then_inc(wo_full, 1)

                    def first(n, i, s):
                        for m in range(6):
                            project(n, m, s)
                        for m in range(QKC):
                            turn(n, m)

                    def both(n, i, s):
                        project(n + 1, 0, 1 - s)
                        project(n + 1, 1, 1 - s)
                        scores(n, i, 0, s)
                        scores(n, i, 1, s)
                        project(n + 1, 2, 1 - s)
                        project(n + 1, 3, 1 - s)
                        project(n + 1, 4, 1 - s)
                        turn_probs(n, 0)
                        turn_probs(n, 1)
                        project(n + 1, 5, 1 - s)
                        values(n, 0, s)
                        values(n, 1, s)
                        turn(n + 1, 0)
                        turn(n + 1, 1)
                        values(n, 2, s)
                        values(n, 3, s)
                        turn(n + 1, 2)
                        project_out(n)
                        turn(n + 1, 3)

                    def second(n, i, s):
                        scores(n, i, 0, s)
                        scores(n, i, 1, s)
                        turn_probs(n, 0)
                        turn_probs(n, 1)
                        for u in range(4):
                            values(n, u, s)
                        project_out(n)

                    pair_index = [None]

                    def turn_in(n):
                        pe.wait_ge(f_shifted, n + 1)
                        for k in range(4):
                            last = pe.transpose(tb[0][:, k * P:(k + 1) * P], sx[:, k * P:(k + 1) * P], ident[:])
                        last.then_inc(f_turned, 1)

                    def turn_back(n):
                        pe.wait_ge(f_rows, n + 1)
                        for k in range(4):
                            last = pe.transpose(tb[1][:, k * P:(k + 1) * P], xr[:, k, :], ident[:])
                        last.then_inc(f_back, 1)

                    def feature(n, j):
                        if j == 0:
                            pe.wait_ge(f_xn, n + 1)
                        if j == NF - 1:
                            pe.wait_ge(gated[0], n + 1)
                            pe.wait_ge(hid_made[0], n + 1)
                        else:
                            last_user = NF - 1 if j == 0 else j
                            pe.wait_ge(hid_made[last_user], n)
                        for k, full in ((0, gate_full), (1, val_full)):
                            col = (FF if k == 0 else 0) + FO[j]
                            pe.matmul(fbank(j, k)[0:FW[j], :], w1_sb[:, col:col + FW[j]], xn[:], start=True,
                                      stop=True).then_inc(full[j], 1)

                    def output(n):
                        for j in range(NF):
                            pe.wait_ge(hid_made[j], n + 1)
                        pe.wait_ge(y_made, n + NCH)
                        for j in range(NF):
                            last = pe.matmul(ub[0][:], w2_sb[0:FW[j], j, :], hid[j][0:FW[j], :], start=(j == 0),
                                             stop=(j == NF - 1))
                        last.then_inc(f_out, 1)

                    def norm(n, c):
                        turn_in(n)
                        turn_back(n)

                    def step(n, c):
                        feature(n, 0)
                        turn_in(n + 1)
                        feature(n, 1)
                        feature(n, 2)
                        turn_back(n + 1)
                        output(n)

                    def mlp(n, c):
                        for j in range(NF):
                            feature(n, j)
                        output(n)

                    start_ahead(pe, "tensor")
                    pe.wait_ge(mask_made, 1)
                    pe.wait_ge(inits, 4)
                    with loop(pe, 0, DEPTH) as l:
                        pe.wait_ge(attn_w, (l + 1) * (16 * 6))
                        base = l * NT + 1
                        first(base, 0, 0)
                        with loop(pe, 0, NT // 2 - 1) as it:
                            pair_index[0] = it
                            for s in range(2):
                                both(base + (it * 2 + s), it * 2 + s, s)
                        both(base + (NT - 2), NT - 2, 0)
                        second(base + (NT - 1), NT - 1, 1)
                        for b in range(2):
                            pe.wait_ge(v_made[b], base + NT)
                            pe.wait_ge(sc_taken[b], base + NT)
                            pe.wait_ge(turn_taken[2 + b], base + NT)
                        pe.wait_ge(z_made, base + NT)
                        pe.wait_ge(ffn_w, (l + 1) * (16 * 13))
                        run_chunks(pe, l, norm, step, mlp)
            clear_semaphores(ctx)

        with ExitStack() as ctx:
            sb, ps, sem1 = alloc(ctx)
            tbanks = [ps(f"fbank{b}", [P, BANK]) for b in range(2)]
            rows = sb("rows", [P, NT, P])
            t_full, t_free, out_made, stored = sem1("l_full"), sem1("l_free"), sem1("out_made"), sem1("stored")
            ln3 = norm_steps("ln3", yrow, rows)
            with nc.Block() as block:
                @block.tensor
                def _(pe):
                    for n in range(NT // 4):
                        if n >= 2:
                            pe.wait_ge(t_free, n - 1)
                        for j in range(4):
                            t = 4 * n + j
                            last = pe.transpose(tbanks[n % 2][:, j * P:(j + 1) * P], Y[:, 1 + t * P:1 + (t + 1) * P], ident[:])
                        last.then_inc(t_full, 1)

                @block.scalar
                def _(a):
                    for n in range(NT // 4):
                        a.wait_ge(t_full, n + 1)
                        a.activation(yrow[:, 4 * n:4 * n + 4, :], tbanks[n % 2][:].rearrange("p (n c) -> p n c", n=4),
                                     ACT.Copy).then_inc(t_free, 1)
                    ln3[1](a)

                @block.gpsimd
                def _(g):
                    ln3[2](g)

                @block.vector
                def _(v):
                    v.wait_ge(t_free, NT // 4)
                    ln3[0](v)
                    v.wait_ge(ln3[3], 1)
                    v.tensor_tensor(rows[:], rows[:], xin[:], ALU.add).then_inc(out_made, 1)

                @block.sync
                def _(sp):
                    sp.wait_ge(out_made, 1)
                    sp.dma_start(out.rearrange("a (n p) c -> p (a n) c", p=P), rows[:]).then_inc(stored, 16)
                    sp.wait_ge(stored, 16)


def shape_constants(T):
    import numpy as np
    half = np.arange(0, DIM_HEAD, 2, dtype=np.float32)
    inv_freq = np.float32(1.0) / np.float32(10000.0) ** (half / np.float32(DIM_HEAD))
    t = np.arange(T, dtype=np.float32)
    freqs = (t[:, None] * inv_freq[None, :]).astype(np.float64)
    base = (half.astype(np.float64) + 0.4 * DIM_HEAD) / (1.4 * DIM_HEAD)
    power = (np.arange(T) % P - P // 2) / (WINDOW // 2)
    scale = base[None, :] ** power[:, None]
    cos, sin = np.cos(freqs), np.sin(freqs)
    tables = []
    for sc in (scale, 1.0 / scale):
        tables += [cos * sc, cos * sc, sin * sc, -sin * sc]
    rot = np.concatenate(tables, 1).astype(np.float32)
    factor = np.tile(base ** (P / (WINDOW // 2)), 2 * 2).astype(np.float32)[:, None]
    p = np.arange(P)
    q, key = p[:, None, None] % WINDOW, np.arange(2 * WINDOW)[None, None, :]
    hidden = (key < q) | (key > q + WINDOW) | np.zeros((1, 2, 1), bool)
    before = (p[:, None, None] < P // 2) & (np.arange(2)[None, :, None] == 0) & (key < WINDOW)
    mask = np.stack([(hidden | before).reshape(P, P)] + [hidden.reshape(P, P)] * (T // P // 2 - 1), 1)
    return rot, factor, np.where(mask, np.float32(MASKED), np.float32(0.0))


_INS = ["L0_attn_x", "L0_attn_w_attn", "L0_attn_w_proj", "L0_ffn_Wqkv", "L0_ffn_q_scale", "L0_ffn_k_scale",
        "L0_ffn_Wo", "L0_ffn_ln_g", "L0_ffn_ln_b", "L0_ffn_W1", "L0_ffn_b1", "L0_ffn_W2", "L0_ffn_b2"]


def build(nc, inputs):
    import numpy as _np
    arrays = {f"in_{n}_dram": _np.ascontiguousarray(inputs[n]) for n in _INS}
    shape = arrays["in_L0_attn_x_dram"].shape
    for n, a in zip(("rot", "halo", "mask"), shape_constants(shape[1])):
        arrays[f"const_{n}_dram"] = _np.ascontiguousarray(a)
    args = [nc.dram_tensor(n, a.shape, mybir.dt.from_np(a.dtype), kind="ExternalInput").ap()
            for n, a in arrays.items()]
    out = nc.dram_tensor("out_0_dram", shape, F32, kind="ExternalOutput").ap()
    sandwich_kernel(nc, *args, out)
    return arrays, out


def kernel(**inputs):
    import concourse.bacc as _bacc
    from concourse.bass_utils import run_bass_kernel_spmd as _run

    nc = _bacc.Bacc("TRN2", target_bir_lowering=False, num_devices=1)
    arrays, _ = build(nc, inputs)
    r = _run(nc, [arrays], core_ids=[0])
    return r.results[0]["out_0_dram"]
```

```python
from contextlib import ExitStack

import concourse.bass as bass
from concourse import mybir

F32 = mybir.dt.float32
BF16 = mybir.dt.bfloat16
ALU = mybir.AluOpType
ACT = mybir.ActivationFunctionType
AX = mybir.AxisListType

P = 128
WINDOW = 32
DIM_HEAD = 64
QK_SCALE = 8.0
LN_EPS = 1e-5
NORM_EPS = 1e-12
MASKED = -1e30
LOWEST = -3e38
BANK = 512
PARTS = 3
HEADS1 = 16


def sandwich_kernel(nc, x_in, w_attn, w_proj, wqkv, q_scale, k_scale, wo, ln_g, ln_b, w1, b1, w2, b2,
                    rot_tables, halo_factor, window_mask, out):
    T, C = x_in.shape[1], x_in.shape[2]
    NT = T // P
    NCH = T // BANK
    DK = C // HEADS1
    DEPTH = wqkv.shape[0]
    INNER = wqkv.shape[2] // 3
    HEADS = INNER // DIM_HEAD
    PAIRS = HEADS // 2
    FF = w2.shape[1]
    NF = 3
    FW = [(FF + NF - 1) // NF] * (NF - 1)
    FW.append(FF - sum(FW))
    FO = [sum(FW[:j]) for j in range(NF)]
    NW = P // WINDOW
    assert C == P and NW == 4 and NT % 4 == 0 and PAIRS == 8 and DIM_HEAD == 64

    def loop(eng, start, end):
        return nc.Fori(start, end, engines=(eng.engine,), hint_back_edge=True)

    outer = ExitStack()
    phase_sems = {}

    def clear_semaphores(ctx):
        nums = sorted(s.num for s in phase_sems[ctx])
        with nc.Block() as block:
            @block.gpsimd
            def _(g):
                start = nums[0]
                for a, b in zip(nums, nums[1:] + [None]):
                    if b != a + 1:
                        g.sem_clear(range(start, a + 1))
                        start = b

    with outer:
        def alloc(ctx):
            def sb(name, shape, dt=F32):
                return ctx.enter_context(nc.sbuf_tensor(name, shape, dt))

            def ps(name, shape, dt=F32):
                return ctx.enter_context(nc.psum_tensor(name, shape, dt))

            def sem(name):
                made = ctx.enter_context(nc.semaphore(name))
                phase_sems.setdefault(ctx, []).append(made)
                return made
            return sb, ps, sem

        sb, ps, sem = alloc(outer)
        q_parts = nc.dram_tensor("q_parts", [PARTS, P, T], BF16, kind="Internal").ap()
        k_parts = nc.dram_tensor("k_parts", [PARTS, P, T], BF16, kind="Internal").ap()
        o_heads = nc.dram_tensor("o_heads", [HEADS1, DK + 1, T], F32, kind="Internal").ap()

        ident = sb("ident", [P, P])
        ident_bf = sb("ident_bf", [P, P], BF16)
        mask_qk = sb("mask_qk", [P, P], BF16)
        mask_kq = sb("mask_kq", [P, P], BF16)
        xin = sb("xin", [P, NT, P])
        yrow = sb("yrow", [P, NT, P])
        ln_mean = sb("ln_mean", [P, NT])
        ln_rstd = sb("ln_rstd", [P, NT])
        minus_half = sb("minus_half", [P, BANK // 8])
        Y = sb("Y", [P, T + 1])
        wproj_t = sb("wproj_t", [P, P])
        v_all = sb("v_all", [P, NT, P])

        const_made = sem("const_made")
        x_loaded = sem("x_loaded")

        def norm_steps(name, src, dst, ln_sq):
            s = {k: sem(f"{name}_{k}") for k in ("sum", "mean", "centred", "squared", "var", "eps", "rstd", "done")}

            def on_vector(v):
                v.tensor_reduce(ln_mean[:], src[:], AX.X, ALU.add).then_inc(s["sum"], 1)
                v.wait_ge(s["sum"], 1)
                v.tensor_scalar(ln_mean[:], ln_mean[:], 1.0 / C, None, ALU.mult).then_inc(s["mean"], 1)
                v.wait_ge(s["mean"], 1)
                v.tensor_tensor(dst[:], src[:], ln_mean[:].unsqueeze(2).broadcast_to([P, NT, C]),
                                ALU.subtract).then_inc(s["centred"], 1)
                v.wait_ge(s["squared"], 1)
                v.tensor_reduce(ln_rstd[:], ln_sq[:], AX.X, ALU.add).then_inc(s["var"], 1)
                v.wait_ge(s["var"], 1)
                v.tensor_scalar(ln_rstd[:], ln_rstd[:], 1.0 / C, LN_EPS, ALU.mult, ALU.add).then_inc(s["eps"], 1)
                v.wait_ge(s["rstd"], 1)
                v.tensor_tensor(dst[:], dst[:], ln_rstd[:].unsqueeze(2).broadcast_to([P, NT, C]),
                                ALU.mult).then_inc(s["done"], 1)

            def on_scalar(a):
                a.wait_ge(s["centred"], 1)
                a.activation(ln_sq[:], dst[:], ACT.Square).then_inc(s["squared"], 1)

            def on_gpsimd(g):
                g.wait_ge(s["eps"], 1)
                g.tensor_tensor(ln_rstd[:], ln_rstd[:], minus_half[:, 0:NT], ALU.pow).then_inc(s["rstd"], 1)
            return on_vector, on_scalar, on_gpsimd, s["done"]

        with ExitStack() as ctx:
            sb, ps, sem1 = alloc(ctx)
            w_rows = sb("w_rows", [P, 4, P])
            w_t = sb("w_t", [P, 3, P])
            xn_t = sb("xn_t", [P, T])
            part = [[sb(f"part{b}_{a}", [P, BANK], BF16) for a in range(PARTS)] for b in range(2)]
            rest = [sb(f"rest{b}", [P, BANK]) for b in range(2)]
            rest2 = [sb(f"rest2{b}", [P, BANK]) for b in range(2)]
            turned = [ps(f"turned{b}", [P, BANK]) for b in range(2)]
            proj = [ps(f"proj{b}", [P, BANK]) for b in range(2)]
            vproj = [ps(f"vproj{b}", [P, BANK]) for b in range(2)]
            turn_full, turn_free = sem1("turn_full"), sem1("turn_free")
            w_loaded = sem1("w_loaded")
            proj_full, proj_free = sem1("proj_full"), sem1("proj_free")
            p1_made, r1_made, p2_made, r2_made = (sem1(n) for n in ("p1_made", "r1_made", "p2_made", "r2_made"))
            parts_stored = [sem1(f"parts_stored{b}") for b in range(2)]
            v_full, v_free = sem1("v_full"), sem1("v_free")
            ln_vector, ln_scalar, ln_gpsimd, ln_done = norm_steps("ln0", xin, yrow, sb("ln_sq0", [P, NT, P]))
            NQK = 2 * NCH
            NTURN = (NT + 4) // 4

            with nc.Block() as block:
                @block.sync
                def _(sp):
                    sp.dma_start(xin[:], x_in.rearrange("a (n p) c -> p (a n) c", p=P)).then_inc(x_loaded, 16)
                    sp.dma_start(w_rows[:, 0:3, :], w_attn.rearrange("(n p) c -> p n c", p=P)).then_inc(w_loaded, 16)
                    sp.dma_start(w_rows[:, 3, :], w_proj).then_inc(w_loaded, 16)
                    for u in range(NQK):
                        dst = k_parts if u % 2 else q_parts
                        cols = slice(u // 2 * BANK, (u // 2 + 1) * BANK)
                        sp.wait_ge(r2_made, u + 1)
                        for a in range(PARTS):
                            sp.dma_start(dst[a, :, cols], part[u % 2][a][:]).then_inc(parts_stored[u % 2], 16)
                    for b in range(2):
                        sp.wait_ge(parts_stored[b], 16 * PARTS * NCH)

                @block.gpsimd
                def _(g):
                    g.memset(ident[:], 0.0).then_inc(const_made, 1)
                    g.memset(ident_bf[:], 0.0).then_inc(const_made, 1)
                    g.memset(mask_qk[:], 0.0).then_inc(const_made, 1)
                    g.memset(mask_kq[:], 0.0).then_inc(const_made, 1)
                    g.memset(minus_half[:], -0.5).then_inc(const_made, 1)
                    g.wait_ge(const_made, 5)
                    for t in (ident, ident_bf):
                        g.affine_select(out=t[:], in_=t[:], compare_op=ALU.not_equal, fill=1.0, base=0,
                                        pattern=[[-1, P]], channel_multiplier=1).then_inc(const_made, 1)
                    g.affine_select(out=mask_qk[:], in_=mask_qk[:], compare_op=ALU.is_ge, fill=MASKED, base=0,
                                    pattern=[[-1, P]], channel_multiplier=1).then_inc(const_made, 1)
                    g.affine_select(out=mask_kq[:], in_=mask_kq[:], compare_op=ALU.is_ge, fill=MASKED, base=0,
                                    pattern=[[1, P]], channel_multiplier=-1).then_inc(const_made, 1)
                    ln_gpsimd(g)

                @block.vector
                def _(v):
                    v.wait_ge(x_loaded, 16)
                    ln_vector(v)
                    for u in range(NQK):
                        b = u % 2
                        v.wait_ge(p1_made, u + 1)
                        v.tensor_tensor(rest[b][:], proj[b][:], part[b][0][:], ALU.subtract).then_inc(r1_made, 1)
                        v.wait_ge(r1_made, u + 1)
                        v.tensor_copy(part[b][1][:], rest[b][:]).then_inc(p2_made, 1)
                        v.wait_ge(p2_made, u + 1)
                        v.tensor_tensor(part[b][2][:], rest[b][:], part[b][1][:], ALU.subtract).then_inc(r2_made, 1)

                @block.scalar
                def _(a):
                    ln_scalar(a)
                    for n in range(NTURN):
                        a.wait_ge(turn_full, n + 1)
                        if n == 0:
                            a.activation(w_t[:], turned[0][:, 0:3 * P].rearrange("p (n c) -> p n c", n=3),
                                         ACT.Copy)
                            a.activation(wproj_t[:], turned[0][:, 3 * P:4 * P], ACT.Copy).then_inc(turn_free, 1)
                        else:
                            a.activation(xn_t[:, (n - 1) * BANK:n * BANK], turned[n % 2][:],
                                         ACT.Copy).then_inc(turn_free, 1)
                    for u in range(NQK):
                        a.wait_ge(proj_full, u + 1)
                        if u >= 2:
                            a.wait_ge(parts_stored[u % 2], 16 * PARTS * (u // 2))
                        a.activation(part[u % 2][0][:], proj[u % 2][:], ACT.Copy).then_inc(p1_made, 1)
                    for n in range(NT // 4):
                        a.wait_ge(v_full, n + 1)
                        a.activation(v_all[:, 4 * n:4 * n + 4, :],
                                     vproj[n % 2][:].rearrange("p (n c) -> p n c", n=4),
                                     ACT.Copy).then_inc(v_free, 1)

                @block.tensor
                def _(pe):
                    pe.wait_ge(const_made, 9)
                    pe.wait_ge(w_loaded, 32)
                    for n in range(NTURN):
                        if n == 1:
                            pe.wait_ge(ln_done, 1)
                        if n >= 2:
                            pe.wait_ge(turn_free, n - 1)
                        for j in range(4):
                            src = w_rows[:, j, :] if n == 0 else yrow[:, 4 * (n - 1) + j, :]
                            last = pe.transpose(turned[n % 2][:, j * P:(j + 1) * P], src, ident[:])
                        last.then_inc(turn_full, 1)
                    for u in range(NQK):
                        pe.wait_ge(turn_free, u // 2 + 2)
                        if u >= 2:
                            pe.wait_ge(r1_made, u - 1)
                        pe.matmul(proj[u % 2][:], w_t[:, u % 2, :], xn_t[:, u // 2 * BANK:(u // 2 + 1) * BANK],
                                  start=True, stop=True).then_inc(proj_full, 1)
                    for n in range(NT // 4):
                        if n >= 2:
                            pe.wait_ge(v_free, n - 1)
                        for j in range(4):
                            t = 4 * n + j
                            last = pe.matmul(vproj[n % 2][:, j * P:(j + 1) * P], xn_t[:, t * P:(t + 1) * P],
                                             w_t[:, 2, :], start=True, stop=True)
                        last.then_inc(v_full, 1)
            clear_semaphores(ctx)

        with ExitStack() as ctx:
            sb, ps, sem1 = alloc(ctx)
            ROWS = PARTS * PARTS * DK
            MROW = 96
            KROWS = MROW + PARTS
            Qh = [sb(f"Qh{s}", [P, T], BF16) for s in range(2)]
            Kh = [sb(f"Kh{s}", [P, T], BF16) for s in range(2)]
            Vh = [sb(f"Vh{s}", [P, NT, DK + 1]) for s in range(2)]
            mpart = [sb(f"mpart{s}", [P, NT, NCH]) for s in range(2)]
            mrow = [sb(f"mrow{s}", [P, NT]) for s in range(2)]
            nm = [sb(f"nm{s}", [NT, PARTS, P], BF16) for s in range(2)]
            nrest = [sb(f"nrest{s}", [NT, P]) for s in range(2)]
            probs = [sb(f"probs{r}", [P, BANK]) for r in range(4)]
            Oh = [sb(f"Oh{s}", [DK + 1, T]) for s in range(2)]
            sc_bank = [ps(f"sc{r}", [P, BANK]) for r in range(2)]
            st_bank = [ps(f"st{r}", [P, BANK]) for r in range(4)]
            o_bank = [ps(f"o{r}", [P, BANK]) for r in range(2)]
            m_bank = sc_bank[0]
            qk_loaded = sem1("qk_loaded")
            rows_set = sem1("rows_set")
            vh_made = sem1("vh_made")
            sc_full, sc_free = sem1("sc_full"), sem1("sc_free")
            m_made, m_turned = sem1("m_made"), sem1("m_turned")
            n1, n2, n3, n4 = (sem1(n) for n in ("n1_made", "nrest_made", "n2_made", "n3_made"))
            m_placed = sem1("m_placed")
            st_full, exp_done, pv_done = sem1("st_full"), sem1("exp_done"), sem1("pv_done")
            o_free = sem1("o_free")
            o_stored = [sem1(f"o_stored{s}") for s in range(2)]

            max_units = [(i, kc) for i in range(NT) for kc in range(i // 4 + 1)]
            pv_units = [(c, j) for c in range(NCH) for j in range(4 * c + 4)]
            U = len(pv_units)
            assert len(max_units) == U
            PV_LAG = 2
            SPAN = U // 2
            FIRST = U // 4
            assert U % 4 == 0

            with nc.Block() as block:
                @block.sync
                def _(sp):
                    for s in range(2):
                        sp.sem_inc(o_stored[s], 16)
                    sp.wait_ge(rows_set, 4)

                    def load(h, s, free=True):
                        if free:
                            sp.wait_ge(rows_set, 4)
                            sp.wait_ge(pv_done, U * (h - 1))
                        for b in range(PARTS):
                            r0 = b * PARTS * DK
                            sp.dma_start(Qh[s][r0:r0 + PARTS * DK, :],
                                         q_parts[:, bass.ds(h * DK, DK), :]).then_inc(qk_loaded, 16)
                            for a in range(PARTS):
                                sp.dma_start(Kh[s][r0 + a * DK:r0 + (a + 1) * DK, :],
                                             k_parts[b, bass.ds(h * DK, DK), :]).then_inc(qk_loaded, 16)

                    def place_max(h, s):
                        sp.wait_ge(n4, h + 1)
                        for a in range(PARTS):
                            sp.dma_start(Qh[s][MROW + a:MROW + a + 1, :],
                                         nm[s][:, a, :]).then_inc(m_placed, 16)

                    def store(h, s):
                        sp.wait_ge(o_free, NCH * (h + 1))
                        sp.dma_start(o_heads[bass.ds(h, 1), :, :].rearrange("a d t -> (a d) t"),
                                     Oh[s][:]).then_inc(o_stored[s], 16)

                    load(0, 0, False)
                    load(1, 1, False)
                    place_max(0, 0)
                    place_max(1, 1)
                    store(0, 0)
                    load(2, 0)
                    with loop(sp, 0, HEADS1 // 2 - 2) as it:
                        for r in range(2):
                            h = it * 2 + (1 + r)
                            place_max(h + 1, r)
                            store(h, 1 - r)
                            load(h + 2, 1 - r)
                    h = HEADS1 - 3
                    place_max(h + 1, 0)
                    store(h, 1)
                    load(h + 2, 1)
                    place_max(h + 2, 1)
                    store(h + 1, 0)
                    store(h + 2, 1)
                    for s in range(2):
                        sp.wait_ge(o_stored[s], 16 * (HEADS1 // 2 + 1))

                @block.gpsimd
                def _(g):
                    g.memset(Vh[0][:], 1.0).then_inc(vh_made, 1)
                    g.memset(Vh[1][:], 1.0).then_inc(vh_made, 1)
                    g.wait_ge(vh_made, 2)
                    for s in range(2):
                        g.tensor_copy(Vh[s][:, :, 0:DK], v_all[:, :, s * DK:(s + 1) * DK]).then_inc(vh_made, 1)
                    with loop(g, 0, HEADS1 // 2 - 1) as it:
                        for s in range(2):
                            h = it * 2 + s
                            g.wait_ge(pv_done, U * (h + 1))
                            g.tensor_copy(Vh[s][:, :, 0:DK],
                                          v_all[:, :, bass.ds((h + 2) * DK, DK)]).then_inc(vh_made, 1)

                @block.vector
                def _(v):
                    for s in range(2):
                        v.memset(Qh[s][64:P, :], 0.0).then_inc(rows_set, 1)
                        v.memset(Kh[s][64:96, :], 0.0)
                        v.memset(Kh[s][96:P, :], 1.0).then_inc(rows_set, 1)
                        v.memset(mpart[s][:], LOWEST)

                    def maxima(h, s, u):
                        i, kc = max_units[u]
                        n = BANK if kc < i // 4 else P * (i % 4 + 1)
                        v.wait_ge(sc_full, h * U + (u + 1))
                        v.tensor_reduce(mpart[s][:, i, kc:kc + 1], sc_bank[u % 2][:, 0:n], AX.X,
                                        ALU.max).then_inc(sc_free, 1)

                    def row_max(h, s):
                        v.wait_ge(sc_free, (h + 1) * U)
                        if not isinstance(h, int) or h >= 2:
                            v.wait_ge(m_turned, h - 1)
                        v.tensor_reduce(mrow[s][:], mpart[s][:], AX.X, ALU.max).then_inc(m_made, 1)

                    def split_max(h, s):
                        mt = m_bank[0:NT, 0:P]
                        v.wait_ge(m_turned, h + 1)
                        if not isinstance(h, int) or h >= 2:
                            v.wait_ge(m_placed, 16 * PARTS * (h - 1))
                        v.tensor_scalar(nm[s][:, 0, :], mt, -1.0, None, ALU.mult).then_inc(n1, 1)
                        v.wait_ge(n1, h + 1)
                        v.scalar_tensor_tensor(out=nrest[s][:], in0=mt, scalar=-1.0, in1=nm[s][:, 0, :],
                                               op0=ALU.mult, op1=ALU.subtract).then_inc(n2, 1)
                        v.wait_ge(n2, h + 1)
                        v.tensor_copy(nm[s][:, 1, :], nrest[s][:]).then_inc(n3, 1)
                        v.wait_ge(n3, h + 1)
                        v.tensor_tensor(nm[s][:, 2, :], nrest[s][:], nm[s][:, 1, :],
                                        ALU.subtract).then_inc(n4, 1)

                    def take_out(h, s, c, before):
                        last = pv_units.index((c, 4 * c + 3))
                        v.wait_ge(pv_done, h * U + (last + 1))
                        if c == 0 and (not isinstance(h, int) or h >= 2):
                            v.wait_ge(o_stored[s], 16 * before + 16)
                        v.tensor_copy(Oh[s][:, c * BANK:(c + 1) * BANK],
                                      o_bank[c % 2][0:DK + 1, :]).then_inc(o_free, 1)

                    def step(h, s, with_max, with_pv, before=0):
                        for u in range(U):
                            if with_max and FIRST <= u < FIRST + SPAN:
                                for k in range(2):
                                    maxima(h + 1, 1 - s, 2 * (u - FIRST) + k)
                            if with_max and u == FIRST + SPAN:
                                row_max(h + 1, 1 - s)
                                split_max(h + 1, 1 - s)
                            if with_pv and pv_units[u][0] > 0 and pv_units[u][1] == 3:
                                take_out(h, s, pv_units[u][0] - 1, before)
                        if with_pv:
                            take_out(h, s, NCH - 1, before)

                    step(-1, 1, True, False)
                    step(0, 0, True, True)
                    with loop(v, 0, HEADS1 // 2 - 1) as it:
                        for r in range(2):
                            step(it * 2 + (1 + r), 1 - r, True, True, it + r if r else it)
                    step(HEADS1 - 1, 1, False, True, HEADS1 // 2 - 1)

                @block.scalar
                def _(a):
                    def head(h, s):
                        for u, (c, j) in enumerate(pv_units):
                            off = max(0, j - 4 * c) * P
                            a.wait_ge(st_full, h * U + (u + 1))
                            if not isinstance(h, int) or h * U + u >= len(probs):
                                a.wait_ge(pv_done, h * U + (u + 1 - len(probs)))
                            a.activation(probs[u % 4][:, off:BANK], st_bank[u % 4][:, off:BANK],
                                         ACT.Exp, scale=float(DK) ** -0.5).then_inc(exp_done, 1)
                    head(0, 0)
                    head(1, 1)
                    with loop(a, 1, HEADS1 // 2) as it:
                        for s in range(2):
                            head(it * 2 + s, s)

                @block.tensor
                def _(pe):
                    def scores_qk(h, s, u):
                        i, kc = max_units[u]
                        n = BANK if kc < i // 4 else P * (i % 4 + 1)
                        if not isinstance(h, int) or h * U + u >= 2:
                            pe.wait_ge(sc_free, h * U + (u - 1))
                        if u == 0 and (not isinstance(h, int) or h >= 1):
                            pe.wait_ge(n2, h)
                        last = kc == i // 4
                        mm = pe.matmul(sc_bank[u % 2][:, 0:n], Qh[s][0:MROW, i * P:(i + 1) * P],
                                       Kh[s][0:MROW, kc * BANK:kc * BANK + n], start=True, stop=not last,
                                       skip_group_check=True)
                        if last:
                            mm = pe.matmul(sc_bank[u % 2][:, n - P:n], ident_bf[:], mask_qk[:], start=False,
                                           stop=True, skip_group_check=True)
                        mm.then_inc(sc_full, 1)

                    def turn_max(h, s):
                        pe.wait_ge(m_made, h + 1)
                        pe.transpose(m_bank[0:NT, 0:P], mrow[s][:], ident[:]).then_inc(m_turned, 1)

                    def scores_kq(h, s, u):
                        c, j = pv_units[u]
                        off = max(0, j - 4 * c) * P
                        st = st_bank[u % 4]
                        lag = len(st_bank)
                        if not isinstance(h, int) or h * U + u >= lag:
                            pe.wait_ge(exp_done, h * U + (u + 1 - lag))
                        diag = j >= 4 * c
                        mm = pe.matmul(st[:, off:BANK], Kh[s][0:KROWS, j * P:(j + 1) * P],
                                       Qh[s][0:KROWS, c * BANK + off:(c + 1) * BANK], start=True, stop=not diag,
                                       skip_group_check=True)
                        if diag:
                            mm = pe.matmul(st[:, off:off + P], ident_bf[:], mask_kq[:], start=False, stop=True,
                                           skip_group_check=True)
                        mm.then_inc(st_full, 1)

                    def values(h, s, u):
                        c, j = pv_units[u]
                        off = max(0, j - 4 * c) * P
                        pe.wait_ge(exp_done, h * U + (u + 1))
                        if j == 0 and (not isinstance(h, int) or NCH * h + c >= 2):
                            pe.wait_ge(o_free, NCH * h + (c - 1))
                        mm = pe.matmul(o_bank[c % 2][0:DK + 1, off:BANK], Vh[s][:, j, :], probs[u % 4][:, off:BANK],
                                       start=(j == 0), stop=(j == 4 * c + 3), skip_group_check=True)
                        mm.then_inc(pv_done, 1)

                    def step(h, s, with_max, with_pv):
                        if with_pv:
                            pe.wait_ge(m_placed, 16 * PARTS * (h + 1))
                            pe.wait_ge(vh_made, h + 3)
                        for u in range(U + PV_LAG):
                            if with_max and u == FIRST:
                                loads = 2 if isinstance(h, int) and h < 0 else h + 2
                                pe.wait_ge(qk_loaded, 16 * 12 * loads)
                            if with_max and FIRST <= u < FIRST + SPAN:
                                for k in range(2):
                                    scores_qk(h + 1, 1 - s, 2 * (u - FIRST) + k)
                            if with_max and u == FIRST + SPAN + 1:
                                turn_max(h + 1, 1 - s)
                            if with_pv and u < U:
                                scores_kq(h, s, u)
                            if with_pv and u >= PV_LAG:
                                values(h, s, u - PV_LAG)

                    pe.wait_ge(rows_set, 4)
                    step(-1, 1, True, False)
                    step(0, 0, True, True)
                    with loop(pe, 0, HEADS1 // 2 - 1) as it:
                        for r in range(2):
                            step(it * 2 + (1 + r), 1 - r, True, True)
                    step(HEADS1 - 1, 1, False, True)
            clear_semaphores(ctx)

        with ExitStack() as ctx:
            sb, ps, sem1 = alloc(ctx)
            o_t = sb("o_t", [P, T])
            den = sb("den", [P, T])
            rden = sb("rden", [P, T])
            att = sb("att", [P, NT, P])
            banks = [ps(f"pbank{b}", [P, BANK]) for b in range(2)]
            tbanks = [ps(f"tbank{b}", [P, BANK]) for b in range(2)]
            o_loaded, r_made, on_made = sem1("o_loaded"), sem1("r_made"), sem1("on_made")
            a_full, a_free = sem1("a_full"), sem1("a_free")
            x1_made, t_full, t_free = sem1("x1_made"), sem1("t_full"), sem1("t_free")
            ln_sq = sb("ln_sq", [P, NT, P])
            ln1 = norm_steps("ln1", att, yrow, ln_sq)
            ln2 = norm_steps("ln2", xin, yrow, ln_sq)
            with nc.Block() as block:
                @block.sync
                def _(sp):
                    for h in range(HEADS1):
                        sp.dma_start(o_t[h * DK:(h + 1) * DK, :], o_heads[h, 0:DK, :]).then_inc(o_loaded, 16)
                        sp.dma_start(den[h * DK:(h + 1) * DK, :],
                                     o_heads[h, DK:DK + 1, :].broadcast_to([DK, T])).then_inc(o_loaded, 16)

                @block.gpsimd
                def _(g):
                    ln1[2](g)
                    ln2[2](g)

                @block.vector
                def _(v):
                    v.memset(Y[:, 0:1], 0.0)
                    v.wait_ge(o_loaded, 16 * 2 * HEADS1)
                    v.reciprocal(rden[:], den[:]).then_inc(r_made, 1)
                    v.wait_ge(r_made, 1)
                    v.tensor_tensor(o_t[:], o_t[:], rden[:], ALU.mult).then_inc(on_made, 1)
                    v.wait_ge(a_free, NT // 4)
                    ln1[0](v)
                    v.wait_ge(ln1[3], 1)
                    v.tensor_tensor(xin[:], xin[:], yrow[:], ALU.add).then_inc(x1_made, 1)
                    v.wait_ge(x1_made, 1)
                    ln2[0](v)

                @block.scalar
                def _(a):
                    for n in range(NT // 4):
                        a.wait_ge(a_full, n + 1)
                        a.activation(att[:, 4 * n:4 * n + 4, :], banks[n % 2][:].rearrange("p (n c) -> p n c", n=4),
                                     ACT.Copy).then_inc(a_free, 1)
                    ln1[1](a)
                    ln2[1](a)
                    for n in range(NT // 4):
                        a.wait_ge(t_full, n + 1)
                        a.activation(Y[:, 1 + n * BANK:1 + (n + 1) * BANK], tbanks[n % 2][:],
                                     ACT.Copy).then_inc(t_free, 1)

                @block.tensor
                def _(pe):
                    pe.wait_ge(on_made, 1)
                    for n in range(NT // 4):
                        if n >= 2:
                            pe.wait_ge(a_free, n - 1)
                        for j in range(4):
                            t = 4 * n + j
                            last = pe.matmul(banks[n % 2][:, j * P:(j + 1) * P], o_t[:, t * P:(t + 1) * P],
                                             wproj_t[:], start=True, stop=True)
                        last.then_inc(a_full, 1)
                    pe.wait_ge(ln2[3], 1)
                    for n in range(NT // 4):
                        if n >= 2:
                            pe.wait_ge(t_free, n - 1)
                        for j in range(4):
                            last = pe.transpose(tbanks[n % 2][:, j * P:(j + 1) * P], yrow[:, 4 * n + j, :],
                                                ident[:])
                        last.then_inc(t_full, 1)
            clear_semaphores(ctx)

        with ExitStack() as ctx:
            sb, ps, sem2 = alloc(ctx)
            NCHK = INNER // BANK
            HC = BANK // DIM_HEAD
            PC = PAIRS // NCHK
            QKC = 2 * NCHK
            SIN_ON_GPSIMD = ()
            CONSTS = 7
            FFN_LOADS = 4 + 3 * NF
            KW = WINDOW + P

            wqkv_sb = sb("wqkv_sb", [P, 3 * INNER])
            wo_sb = sb("wo_sb", [P, PAIRS, P])
            w1_sb = sb("w1_sb", [P, 2 * FF])
            w2_sb = sb("w2_sb", [FW[0], NF, P])
            g_col, b_col, b2_col = sb("g_col", [P, 1]), sb("b_col", [P, 1]), sb("b2_col", [P, 1])
            b1_col = sb("b1_col", [FW[0], 2, NF])
            rot = sb("rot", [P, NT, 4, DIM_HEAD])
            qk_scales = sb("qk_scales", [P, DEPTH, 4, DIM_HEAD])
            halo_col = sb("halo_col", [P, 1])
            wmask = sb("wmask", [P, 2, P], BF16)
            wmask_f = sb("wmask_f", [P, 2, P])
            Z = sb("Z", [P, T + 1])
            xs = [sb(f"xs{s}", [P, P]) for s in range(2)]
            tab = [sb(f"tab{s}", [P, 4, DIM_HEAD]) for s in range(2)]
            squares = [sb(f"squares{m}", [P, HC, DIM_HEAD]) for m in range(QKC)]
            ssum = [sb(f"ssum{m}", [P, HC]) for m in range(QKC)]
            rnorm = [sb(f"rnorm{m}", [P, HC]) for m in range(QKC)]
            raw = [sb(f"raw{m}", [P, HC, DIM_HEAD]) for m in range(QKC)]
            qk_n = [sb(f"qk_n{m}", [P, HC, DIM_HEAD]) for m in range(QKC)]
            prod_c = [sb(f"prod_c{m}", [P, HC, DIM_HEAD]) for m in range(QKC)]
            prod_s = [sb(f"prod_s{m}", [P, HC, DIM_HEAD]) for m in range(QKC)]
            qbd = sb("qbd", [P, PAIRS, NW, 2, WINDOW])
            kt = [sb(f"kt{s}", [P, PAIRS, KW]) for s in range(2)]
            v_even = [sb(f"v_even{s}", [P, INNER]) for s in range(2)]
            v_odd = [sb(f"v_odd{s}", [P, INNER]) for s in range(2)]
            G = PC * 2
            smax = [sb(f"smax{b}", [P, G]) for b in range(2)]
            ssx = [sb(f"ssx{b}", [P, G, 2 * WINDOW]) for b in range(2)]
            den = [sb(f"wden{b}", [P, G]) for b in range(2)]
            rden = [sb(f"wrden{b}", [P, G]) for b in range(2)]
            probs = [sb(f"wprobs{b}", [P, G, 2 * WINDOW]) for b in range(2)]
            ptbd = sb("ptbd", [P, PAIRS, 2, 2, 2 * WINDOW])
            ot = sb("ot", [P, PAIRS, P])
            sx = sb("sx", [P, BANK])
            stats = sb("stats", [P, 4, 6])
            mv = sb("mv", [P, 4, 2])
            frstd = sb("frstd", [P, 4])
            xr = sb("xr", [P, 4, P])
            xn = sb("xn", [P, BANK])
            gate = [sb(f"gate{j}", [FW[0], BANK]) for j in range(NF)]
            hid = [sb(f"hid{j}", [FW[0], BANK]) for j in range(NF)]

            pj = [ps(f"pj{b}", [P, BANK]) for b in range(2)]
            tb = [ps(f"tb{b}", [P, BANK]) for b in range(2)]
            sb_ = [ps(f"sb{b}", [P, BANK]) for b in range(2)]
            ub = [ps(f"ub{b}", [P, BANK]) for b in range(2)]

            def per(name, count):
                return [sem2(f"{name}{m}") for m in range(count)]
            inits = sem2("inits")
            consts_loaded = sem2("consts_loaded")
            mask_made = sem2("mask_made")
            wqk_loaded, wv_loaded, wo_loaded, ffn_loaded = (
                sem2(x) for x in ("wqk_loaded", "wv_loaded", "wo_loaded", "ffn_loaded"))
            shifted, tabled = sem2("shifted"), sem2("tabled")
            proj_full = per("wproj_full", 6)
            squared, copied, summed, clamped, rsqrted, normed = (
                per(x, QKC) for x in ("squared", "copied", "summed", "clamped", "rsqrted", "normed"))
            v_made = per("v_made", 2)
            cos_done, sin_done = per("cos_done", QKC), per("sin_done", QKC)
            turn_full, turn_taken = per("wturn_full", QKC), per("wturn_taken", QKC)
            halo_made, odd_made = sem2("halo_made"), sem2("odd_made")
            sc_full, sc_max, sc_taken, exped, den_made, rden_made, prob_made = (
                per(x, 2) for x in ("wsc_full", "sc_max", "sc_taken", "exped", "den_made", "rden_made", "prob_made"))
            pt_full, pt_taken = per("pt_full", 2), per("pt_taken", 2)
            pv_full, pv_taken = per("pv_full", 4), per("pv_taken", 4)
            wo_full, z_made = sem2("wo_full"), sem2("z_made")
            y_made = sem2("y_made")
            f_shifted, f_turned, f_stats, f_mv, f_eps, f_rstd, f_rows, f_back, f_xn = (
                sem2(x) for x in ("f_shifted", "f_turned", "f_stats", "f_mv", "f_eps", "f_rstd", "f_rows",
                                  "f_back", "f_xn"))
            gate_full, val_full, gated, hid_made = (per(x, NF) for x in ("gate_full", "val_full", "gated", "hid_made"))
            f_out = sem2("f_out")

            COUNT0 = 2
            ahead = {
                "gpsimd": (tabled, *rsqrted, *[sin_done[m] for m in SIN_ON_GPSIMD], f_rstd),
                "vector": (*summed, *clamped, *normed, *cos_done,
                           *[sin_done[m] for m in range(QKC) if m not in SIN_ON_GPSIMD], halo_made, *sc_max,
                           *sc_taken, *den_made, *rden_made, *prob_made, z_made, f_stats, f_mv, f_eps, f_rows,
                           *hid_made),
                "scalar": (shifted, *squared, *copied, *v_made, *turn_taken, *exped, *pt_taken, *pv_taken,
                           f_shifted, f_xn, *gated),
                "tensor": (*proj_full, *turn_full, *sc_full, *pt_full, *pv_full, wo_full,
                           f_turned, f_back, *gate_full, *val_full, f_out),
            }

            def start_ahead(eng, name):
                for q in ahead[name]:
                    eng.sem_inc(q, COUNT0)

            def done(n):
                return n + 1

            def odd_done(n):
                return 32 * (n + 1)

            def chunk_done(f):
                return f + 1 + NCH

            SLOTS = BANK // P
            ALL = ("qk", "turn", "attend", "out", "ffn")

            def run_slots(eng, chunk):
                everything = [ALL] * SLOTS
                chunk(0, 0, [ALL[:k + 1] for k in range(SLOTS)])
                with loop(eng, 0, DEPTH - 1) as l:
                    with loop(eng, 1, NCH) as c:
                        chunk(l, c, everything)
                    chunk(l + 1, 0, everything)
                with loop(eng, 1, NCH) as c:
                    chunk(DEPTH - 1, c, everything)
                chunk(DEPTH, 0, [ALL[1:], ALL[2:], ALL[3:], ALL[4:]])

            def count_of(l, c, k):
                return l * NT + c * SLOTS + (k + COUNT0)

            def layer_start(c):
                return isinstance(c, int) and c == 0

            def tile_at(c, k):
                return (NT + k if k < 0 else k) if layer_start(c) else c * SLOTS + k

            def ffn_chunk(l, c):
                return l * NCH + c + (COUNT0 - 1), (NCH - 1 if layer_start(c) else c - 1)

            def ffn_layers(l, c):
                return l if layer_start(c) else l + 1

            def sine_product(eng, m, s):
                k = 2 * (m // NCHK) + 1
                table = tab[s][:, k, :].rearrange("p (t d) -> p t d", t=2).unsqueeze(1)
                src = qk_n[m][:].rearrange("p h (t d) -> p h t d", t=2)
                dst = prod_s[m][:].rearrange("p h (t d) -> p h t d", t=2)
                eng.tensor_tensor(dst[:, :, ::-1, :], src, table.broadcast_to([P, HC, 2, DIM_HEAD // 2]),
                                  ALU.mult).then_inc(sin_done[m], 1)

            with nc.Block() as block:
                @block.sync
                def _(sp):
                    sp.sem_inc(odd_made, 32 * COUNT0)
                    sp.dma_start(rot[:], rot_tables.rearrange("(n p) (k d) -> p n k d", p=P, k=4)).then_inc(consts_loaded, 16)
                    sp.dma_start(halo_col[:], halo_factor).then_inc(consts_loaded, 16)
                    sp.dma_start(wmask_f[:], window_mask).then_inc(consts_loaded, 16)
                    for k, src in enumerate((q_scale, q_scale, k_scale, k_scale)):
                        sp.dma_start(qk_scales[:, :, k, :], src.unsqueeze(0).broadcast_to([P, DEPTH, DIM_HEAD])
                                     ).then_inc(consts_loaded, 16)

                    def shift_values(n, s):
                        sp.wait_ge(v_made[0], done(n))
                        sp.wait_ge(v_made[1], done(n))
                        sp.dma_start(v_odd[s][WINDOW:P, :], v_even[s][0:P - WINDOW, :]).then_inc(odd_made, 16)
                        sp.dma_start(v_odd[s][0:WINDOW, :], v_even[1 - s][P - WINDOW:P, :]).then_inc(odd_made, 16)

                    def load_projection(l, m, loaded):
                        sp.wait_ge(consts_loaded, 16 * CONSTS)
                        sp.wait_ge(proj_full[m], l * NT + COUNT0)
                        cols = slice(m * BANK, (m + 1) * BANK)
                        sp.dma_start(wqkv_sb[:, cols],
                                     wqkv[bass.ds(l, 1), :, cols].rearrange("a c n -> (a c) n")).then_inc(loaded, 16)

                    def load_out_weights(l):
                        sp.wait_ge(consts_loaded, 16 * CONSTS)
                        sp.wait_ge(wo_full, l * NT + COUNT0)
                        sp.dma_start(wo_sb[:], wo[bass.ds(l, 1), :, :].rearrange("a (n p) c -> p (a n) c", p=P)
                                     ).then_inc(wo_loaded, 16)

                    def load_ffn(l):
                        sp.wait_ge(consts_loaded, 16 * CONSTS)
                        sp.wait_ge(y_made, l * NCH + (NCH + COUNT0))
                        wl = bass.ds(l, 1)
                        for dst, src in ((g_col, ln_g), (b_col, ln_b), (b2_col, b2)):
                            sp.dma_start(dst[:], src[wl, :].rearrange("a p -> p a")).then_inc(ffn_loaded, 16)
                        for k in range(2):
                            for j in range(NF):
                                sp.dma_start(b1_col[0:FW[j], k, j:j + 1],
                                             b1[wl, k * FF + FO[j]:k * FF + FO[j] + FW[j]].rearrange("a p -> p a")
                                             ).then_inc(ffn_loaded, 16)
                        sp.dma_start(w1_sb[:], w1[wl, :, :].rearrange("a c n -> (a c) n")).then_inc(ffn_loaded, 16)
                        for j in range(NF):
                            sp.dma_start(w2_sb[0:FW[j], j, :],
                                         w2[wl, FO[j]:FO[j] + FW[j], :].rearrange("a c n -> (a c) n")
                                         ).then_inc(ffn_loaded, 16)

                    def chunk(l, c, slots):
                        loads = layer_start(c) and not (isinstance(l, int) and l == DEPTH)
                        if loads:
                            for m in range(QKC):
                                load_projection(l, m, wqk_loaded)
                        for k, stages in enumerate(slots):
                            if k == 2 and loads:
                                load_out_weights(l)
                            if "turn" in stages:
                                shift_values(count_of(l, c, k) - 1, (k + 1) % 2)
                            if k == 0 and loads:
                                load_projection(l, QKC, wv_loaded)
                                load_projection(l, QKC + 1, wv_loaded)
                        if loads:
                            load_ffn(l)

                    run_slots(sp, chunk)
                    for q, count in ((consts_loaded, CONSTS), (wqk_loaded, QKC * DEPTH), (wv_loaded, 2 * DEPTH),
                                     (wo_loaded, DEPTH), (ffn_loaded, FFN_LOADS * DEPTH),
                                     (odd_made, 2 * (NT * DEPTH + COUNT0))):
                        sp.wait_ge(q, 16 * count)

                @block.gpsimd
                def _(g):
                    start_ahead(g, "gpsimd")
                    g.memset(kt[1][:], 0.0).then_inc(inits, 1)
                    g.memset(v_even[1][:], 0.0).then_inc(inits, 1)
                    g.memset(qbd[:], 0.0).then_inc(inits, 1)
                    g.memset(ptbd[:], 0.0).then_inc(inits, 1)

                    def make_table(n, l, i, s):
                        g.wait_ge(consts_loaded, 16 * CONSTS)
                        g.wait_ge(cos_done[QKC - 1], done(n - 2))
                        g.wait_ge(sin_done[QKC - 1], done(n - 2))
                        scales = qk_scales[:, bass.ds(l, 1), :, :].rearrange("p a k d -> p (a k) d")
                        g.tensor_tensor(tab[s][:], rot[:, bass.ds(i, 1), :, :].rearrange("p a k d -> p (a k) d"),
                                        scales, ALU.mult).then_inc(tabled, 1)

                    def power(n, m):
                        g.wait_ge(clamped[m], done(n))
                        g.wait_ge(normed[m], done(n - 1))
                        g.tensor_tensor(rnorm[m][:], ssum[m][:], minus_half[:, 0:HC], ALU.pow).then_inc(rsqrted[m], 1)

                    def sines(n, m, s):
                        g.wait_ge(normed[m], done(n))
                        g.wait_ge(tabled, done(n))
                        g.wait_ge(turn_full[m], done(n - 1))
                        sine_product(g, m, s)

                    def ffn_power(f):
                        g.wait_ge(f_eps, done(f))
                        g.tensor_tensor(frstd[:], frstd[:], minus_half[:, 0:4], ALU.pow).then_inc(f_rstd, 1)

                    def chunk(l, c, slots):
                        f, _ = ffn_chunk(l, c)
                        for k, stages in enumerate(slots):
                            n, s = count_of(l, c, k), k % 2
                            if "turn" in stages:
                                for m in SIN_ON_GPSIMD:
                                    sines(n - 1, m, 1 - s)
                            if "qk" in stages:
                                make_table(n, l, tile_at(c, k), s)
                            if "qk" in stages:
                                power(n, 0)
                                power(n, 1)
                            if "ffn" in stages and k == 2:
                                ffn_power(f)
                            if "qk" in stages:
                                power(n, 2)
                                power(n, 3)

                    g.wait_ge(consts_loaded, 16 * CONSTS)
                    run_slots(g, chunk)

                @block.vector
                def _(v):
                    start_ahead(v, "vector")
                    v.sem_inc(y_made, COUNT0 + NCH)
                    v.memset(Z[:, 0:1], 0.0)
                    v.wait_ge(consts_loaded, 16 * CONSTS)
                    v.tensor_copy(wmask[:], wmask_f[:]).then_inc(mask_made, 1)

                    def sums(n, m):
                        v.wait_ge(squared[m], done(n))
                        v.tensor_reduce(ssum[m][:], squares[m][:], AX.X, ALU.add).then_inc(summed[m], 1)
                        v.wait_ge(summed[m], done(n))
                        v.tensor_scalar(ssum[m][:], ssum[m][:], NORM_EPS ** 2, None, ALU.max).then_inc(clamped[m], 1)

                    def rotate(n, m, s):
                        v.wait_ge(copied[m], done(n))
                        v.wait_ge(rsqrted[m], done(n))
                        v.wait_ge(sin_done[m], done(n - 1))
                        v.tensor_tensor(qk_n[m][:], raw[m][:], rnorm[m][:].unsqueeze(2).broadcast_to([P, HC, DIM_HEAD]),
                                        ALU.mult).then_inc(normed[m], 1)
                        v.wait_ge(normed[m], done(n))
                        v.wait_ge(turn_full[m], done(n - 1))
                        v.wait_ge(tabled, done(n))
                        k = 2 * (m // NCHK)
                        v.tensor_tensor(prod_c[m][:], qk_n[m][:],
                                        tab[s][:, k, :].unsqueeze(1).broadcast_to([P, HC, DIM_HEAD]),
                                        ALU.mult).then_inc(cos_done[m], 1)
                        if m not in SIN_ON_GPSIMD:
                            sine_product(v, m, s)

                    def halo(n, s):
                        for m in range(NCHK, QKC):
                            v.wait_ge(turn_taken[m], done(n - 1))
                        v.wait_ge(sc_full[1], done(n - 2))
                        v.tensor_scalar(kt[s][:, :, 0:WINDOW], kt[1 - s][:, :, P:KW], halo_col[:, 0:1], None,
                                        ALU.mult).then_inc(halo_made, 1)

                    def soft_in(n, b):
                        v.wait_ge(sc_full[b], done(n))
                        src = sb_[b][:].rearrange("p (g k) -> p g k", g=G)
                        v.tensor_reduce(smax[b][:], src, AX.X, ALU.max).then_inc(sc_max[b], 1)
                        v.wait_ge(sc_max[b], done(n))
                        v.wait_ge(prob_made[b], done(n - 1))
                        v.tensor_tensor(ssx[b][:], src, smax[b][:].unsqueeze(2).broadcast_to([P, G, 2 * WINDOW]),
                                        ALU.subtract).then_inc(sc_taken[b], 1)

                    def soft_out(n, b):
                        v.wait_ge(exped[b], done(n))
                        v.tensor_reduce(den[b][:], ssx[b][:], AX.X, ALU.add).then_inc(den_made[b], 1)
                        v.wait_ge(den_made[b], done(n))
                        v.reciprocal(rden[b][:], den[b][:]).then_inc(rden_made[b], 1)
                        v.wait_ge(rden_made[b], done(n))
                        v.wait_ge(pt_full[b], done(n - 1))
                        v.tensor_tensor(probs[b][:], ssx[b][:],
                                        rden[b][:].unsqueeze(2).broadcast_to([P, G, 2 * WINDOW]),
                                        ALU.mult).then_inc(prob_made[b], 1)

                    def add_stream(n, i):
                        v.wait_ge(wo_full, done(n))
                        v.tensor_tensor(Z[:, bass.ds(i * P + 1, P)], ub[0][:, 0:P], Y[:, bass.ds(i * P + 1, P)],
                                        ALU.add).then_inc(z_made, 1)

                    def ffn_stats(f):
                        v.wait_ge(f_turned, done(f))
                        for k in range(4):
                            last = v.bn_stats(stats[:, k, :], tb[0][:, k * P:(k + 1) * P])
                        last.then_inc(f_stats, 1)
                        v.wait_ge(consts_loaded, 16 * CONSTS)
                        v.wait_ge(f_stats, done(f))
                        for k in range(4):
                            last = v.bn_aggr(mv[:, k, :], stats[:, k, :])
                        last.then_inc(f_mv, 1)
                        v.wait_ge(f_mv, done(f))
                        v.tensor_scalar(frstd[:], mv[:, :, 1], LN_EPS, None, ALU.add).then_inc(f_eps, 1)

                    def ffn_rows(f):
                        v.wait_ge(f_rstd, done(f))
                        for k in range(4):
                            last = v.tensor_scalar(xr[:, k, :], tb[0][:, k * P:(k + 1) * P], mv[:, k, 0:1],
                                                   frstd[:, k:k + 1], ALU.subtract, ALU.mult)
                        last.then_inc(f_rows, 1)

                    def hidden(f, j):
                        v.wait_ge(val_full[j], done(f))
                        v.wait_ge(gated[j], done(f))
                        v.wait_ge(f_out, done(f - 1))
                        v.scalar_tensor_tensor(out=hid[j][0:FW[j], :], in0=pj[1][0:FW[j], :],
                                               scalar=b1_col[0:FW[j], 0, j:j + 1], in1=gate[j][0:FW[j], :],
                                               op0=ALU.add, op1=ALU.mult).then_inc(hid_made[j], 1)

                    def add_ffn(f, place):
                        v.wait_ge(f_out, done(f))
                        cols = bass.ds(place * BANK + 1, BANK)
                        v.scalar_tensor_tensor(out=Y[:, cols], in0=tb[0][:], scalar=b2_col[:, 0:1], in1=Z[:, cols],
                                               op0=ALU.add, op1=ALU.add).then_inc(y_made, 1)

                    def chunk(l, c, slots):
                        f, place = ffn_chunk(l, c)
                        for k, stages in enumerate(slots):
                            n, s = count_of(l, c, k), k % 2
                            qk, turn, attend = (x in stages for x in ALL[:3])
                            norm, mlp = ("ffn" in stages and k == x for x in (2, 3))
                            if attend:
                                soft_in(n - 2, 0)
                                soft_in(n - 2, 1)
                                soft_out(n - 2, 0)
                            if turn:
                                rotate(n - 1, 2, 1 - s)
                            if "out" in stages:
                                add_stream(n - 3, tile_at(c, k - 3))
                            if turn:
                                rotate(n - 1, 3, 1 - s)
                            if attend:
                                soft_out(n - 2, 1)
                            if qk:
                                sums(n, 0)
                                sums(n, 1)
                            if mlp:
                                v.wait_ge(ffn_loaded, 16 * FFN_LOADS * ffn_layers(l, c))
                                hidden(f, 0)
                            if turn:
                                halo(n - 1, 1 - s)
                            if norm:
                                ffn_stats(f)
                            if mlp:
                                hidden(f, 1)
                            if qk:
                                rotate(n, 0, s)
                            if norm:
                                ffn_rows(f)
                            if mlp:
                                hidden(f, 2)
                            if qk:
                                sums(n, 2)
                                rotate(n, 1, s)
                                sums(n, 3)
                            if mlp:
                                add_ffn(f, place)

                    run_slots(v, chunk)

                @block.scalar
                def _(a):
                    half = P // 2

                    def shift_tile(n, l, c, i, s):
                        a.wait_ge(y_made, l * NCH + c + (COUNT0 + 1))
                        a.wait_ge(proj_full[5], done(n - 2))
                        a.activation(xs[s][0:half, :], Y[0:half, bass.ds(i * P + 1, P)], ACT.Copy)
                        a.activation(xs[s][half:P, :], Y[half:P, bass.ds(i * P, P)], ACT.Copy).then_inc(shifted, 1)

                    def take_qk(n, m):
                        a.wait_ge(proj_full[m], done(n))
                        a.wait_ge(summed[m], done(n - 1))
                        a.activation(squares[m][:], pj[m % 2][:].rearrange("p (h d) -> p h d", h=HC),
                                     ACT.Square).then_inc(squared[m], 1)
                        a.wait_ge(normed[m], done(n - 1))
                        a.activation(raw[m][:], pj[m % 2][:].rearrange("p (h d) -> p h d", h=HC),
                                     ACT.Copy).then_inc(copied[m], 1)

                    def take_v(n, k, s):
                        a.wait_ge(proj_full[QKC + k], done(n))
                        a.wait_ge(pv_full[3], done(n - 2))
                        a.wait_ge(odd_made, odd_done(n - 1))
                        a.activation(v_even[s][:, k * BANK:(k + 1) * BANK], pj[k][:], ACT.Copy).then_inc(v_made[k], 1)

                    def take_q(n, m):
                        a.wait_ge(turn_full[m], done(n))
                        a.wait_ge(sc_full[1], done(n - 1))
                        for h in range(2):
                            rows = slice(h * half, (h + 1) * half)
                            last = a.activation(qbd[rows, m * PC:(m + 1) * PC, :, h, :],
                                                tb[m % 2][rows, :].rearrange("p (a w q) -> p a w q", a=PC, w=NW), ACT.Copy)
                        last.then_inc(turn_taken[m], 1)

                    def take_k(n, m, s):
                        a.wait_ge(turn_full[m], done(n))
                        a.wait_ge(halo_made, done(n - 1))
                        a.wait_ge(sc_full[1], done(n - 2))
                        k = m - NCHK
                        a.activation(kt[s][:, k * PC:(k + 1) * PC, WINDOW:KW],
                                     tb[m % 2][:].rearrange("p (a t) -> p a t", a=PC), ACT.Copy).then_inc(turn_taken[m], 1)

                    def exps(n, b):
                        a.wait_ge(sc_taken[b], done(n))
                        a.activation(ssx[b][:], ssx[b][:], ACT.Exp, scale=QK_SCALE).then_inc(exped[b], 1)

                    def take_pt(n, b):
                        a.wait_ge(pt_full[b], done(n))
                        a.wait_ge(pv_full[3], done(n - 1))
                        for w in range(2):
                            rows = slice(w * half, (w + 1) * half)
                            last = a.activation(ptbd[rows, b * PC:(b + 1) * PC, :, w, :],
                                                ub[b][rows, :].rearrange("p (a g q) -> p a g q", a=PC, g=2), ACT.Copy)
                        last.then_inc(pt_taken[b], 1)

                    def take_o(n, u):
                        a.wait_ge(pv_full[u], done(n))
                        a.wait_ge(wo_full, done(n - 1))
                        for h in range(2):
                            rows = slice(h * half, (h + 1) * half)
                            src = ub[u % 2][rows, :].rearrange("p (aw h q) -> p aw h q", h=2, q=2 * WINDOW)[:, :, h, :]
                            last = a.activation(ot[rows, 2 * u:2 * u + 2, :].rearrange("p a (w q) -> p (a w) q", w=2),
                                                src, ACT.Copy)
                        last.then_inc(pv_taken[u], 1)

                    def ffn_shift(n, f, place):
                        a.wait_ge(z_made, done(n))
                        a.wait_ge(f_turned, done(f - 1))
                        a.activation(sx[0:half, :], Z[0:half, bass.ds(place * BANK + 1, BANK)], ACT.Copy)
                        a.activation(sx[half:P, :], Z[half:P, bass.ds(place * BANK, BANK)],
                                     ACT.Copy).then_inc(f_shifted, 1)

                    def ffn_scale(f):
                        a.wait_ge(f_back, done(f))
                        a.wait_ge(val_full[NF - 1], done(f - 1))
                        a.activation(xn[:], tb[1][:], ACT.Identity, bias=b_col[:, 0:1],
                                     scale=g_col[:, 0:1]).then_inc(f_xn, 1)

                    def gelu(f, j):
                        a.wait_ge(gate_full[j], done(f))
                        a.wait_ge(hid_made[j], done(f - 1))
                        a.activation(gate[j][0:FW[j], :], pj[0][0:FW[j], :], ACT.Gelu,
                                     bias=b1_col[0:FW[j], 1, j:j + 1]).then_inc(gated[j], 1)

                    def chunk(l, c, slots):
                        f, place = ffn_chunk(l, c)
                        for k, stages in enumerate(slots):
                            n, s = count_of(l, c, k), k % 2
                            qk, turn, attend = (x in stages for x in ALL[:3])
                            norm, mlp = ("ffn" in stages and k == x for x in (2, 3))
                            if qk:
                                shift_tile(n, l, c, tile_at(c, k), s)
                            if attend:
                                exps(n - 2, 0)
                            if qk:
                                take_qk(n, 0)
                            if attend:
                                exps(n - 2, 1)
                            if qk:
                                take_qk(n, 1)
                            if mlp:
                                a.wait_ge(ffn_loaded, 16 * FFN_LOADS * ffn_layers(l, c))
                                ffn_scale(f)
                                if turn:
                                    take_v(n - 1, 0, 1 - s)
                                    take_v(n - 1, 1, 1 - s)
                                    take_q(n - 1, 0)
                                    take_q(n - 1, 1)
                                gelu(f, 0)
                                if turn:
                                    take_k(n - 1, 2, 1 - s)
                                    take_k(n - 1, 3, 1 - s)
                                if attend:
                                    take_pt(n - 2, 0)
                                    take_pt(n - 2, 1)
                                gelu(f, 1)
                                if attend:
                                    take_o(n - 2, 0)
                                    take_o(n - 2, 1)
                                gelu(f, 2)
                                if attend:
                                    take_o(n - 2, 2)
                                    take_o(n - 2, 3)
                                if qk:
                                    take_qk(n, 2)
                                    take_qk(n, 3)
                                continue
                            if turn:
                                take_q(n - 1, 0)
                                take_q(n - 1, 1)
                                take_v(n - 1, 0, 1 - s)
                                take_v(n - 1, 1, 1 - s)
                            if norm:
                                ffn_shift(n - 3, f, place)
                            if turn:
                                take_k(n - 1, 2, 1 - s)
                                take_k(n - 1, 3, 1 - s)
                            if attend:
                                take_pt(n - 2, 0)
                                take_pt(n - 2, 1)
                            if qk:
                                take_qk(n, 2)
                            if attend:
                                take_o(n - 2, 0)
                                take_o(n - 2, 1)
                            if qk:
                                take_qk(n, 3)
                            if attend:
                                take_o(n - 2, 2)
                                take_o(n - 2, 3)

                    start_ahead(a, "scalar")
                    a.wait_ge(inits, 4)
                    run_slots(a, chunk)

                @block.tensor
                def _(pe):
                    def project(n, m, s, ffn_f=None, alone=False):
                        if m == 0:
                            pe.wait_ge(shifted, done(n))
                        if ffn_f is not None and m % 2 == 0:
                            pe.wait_ge(gated[NF - 1], done(ffn_f))
                            pe.wait_ge(hid_made[NF - 1], done(ffn_f))
                        if m < 2:
                            pe.wait_ge(copied[m + 2], done(n - 1))
                        elif m < QKC:
                            pe.wait_ge(*((copied[m - 2], done(n)) if alone else (v_made[m - 2], done(n - 1))))
                        else:
                            pe.wait_ge(*((copied[m - 2], done(n)) if alone else (copied[m - QKC], done(n + 1))))
                        pe.matmul(pj[m % 2][:], xs[s][:], wqkv_sb[:, m * BANK:(m + 1) * BANK], start=True,
                                  stop=True).then_inc(proj_full[m], 1)

                    def turn_qk(n, m, out_f, norm_f):
                        pe.wait_ge(cos_done[m], done(n))
                        pe.wait_ge(sin_done[m], done(n))
                        if m < 2:
                            pe.wait_ge(turn_taken[m + 2], done(n - 1))
                            if out_f is not None and m == 0:
                                pe.wait_ge(y_made, chunk_done(out_f))
                            if norm_f is not None and m == 1:
                                pe.wait_ge(f_xn, done(norm_f))
                        else:
                            pe.wait_ge(turn_taken[m - 2], done(n))
                        for a in range(PC):
                            for k, src in enumerate((prod_c, prod_s)):
                                last = pe.matmul(tb[m % 2][:, a * P:(a + 1) * P],
                                                 src[m][:].rearrange("p h d -> p (h d)")[:, a * P:(a + 1) * P], ident[:],
                                                 start=(k == 0), stop=(k == 1), is_transpose=True, skip_group_check=True)
                        last.then_inc(turn_full[m], 1)

                    def scores(n, first, b, s):
                        pe.wait_ge(sc_taken[b], done(n - 1))
                        for m in (b, b + 2):
                            pe.wait_ge(turn_taken[m], done(n))
                        pe.wait_ge(halo_made, done(n))
                        which = 0 if first else 1
                        pe.matmul(sb_[b][:], ident_bf[:], wmask[:, which:which + 1, :].broadcast_to([P, PC, P]),
                                  start=True, stop=False, skip_group_check=True)
                        for a in range(PC):
                            pair = b * PC + a
                            for g in range(2):
                                for w in range(2):
                                    win = 2 * w + g
                                    col = (2 * a + w) * 2 * WINDOW
                                    last = pe.matmul(sb_[b][64 * g:64 * g + 64, col:col + 2 * WINDOW],
                                                     qbd[:, pair, win, :, :].rearrange("p h q -> p (h q)"),
                                                     kt[s][:, pair, win * WINDOW:win * WINDOW + 2 * WINDOW],
                                                     start=False, stop=True, skip_group_check=True)
                        last.then_inc(sc_full[b], 1)

                    def turn_probs(n, b):
                        pe.wait_ge(prob_made[b], done(n))
                        if b == 0:
                            pe.wait_ge(z_made, done(n - 1))
                        else:
                            pe.wait_ge(pv_taken[3], done(n - 1))
                        for a in range(PC):
                            last = pe.transpose(ub[b][:, a * P:(a + 1) * P],
                                                probs[b][:].rearrange("p g k -> p (g k)")[:, a * P:(a + 1) * P], ident[:])
                        last.then_inc(pt_full[b], 1)

                    def values(n, u, s):
                        pe.wait_ge(pt_taken[u // 2], done(n))
                        if u < 2:
                            pe.wait_ge(pt_taken[u], done(n))
                            if u == 0:
                                pe.wait_ge(odd_made, odd_done(n))
                                pe.wait_ge(v_made[1], done(n))
                        else:
                            pe.wait_ge(pv_taken[u - 2], done(n))
                        for a in range(2):
                            pair = 2 * u + a
                            for g in range(2):
                                vals = (v_odd if g == 0 else v_even)[s]
                                dst = ub[u % 2][:, a * 256:(a + 1) * 256].rearrange(
                                    "p (wh g q) -> p wh g q", g=2, q=WINDOW)[:, :, g, :]
                                last = pe.matmul(dst, vals[:, pair * P:(pair + 1) * P],
                                                 ptbd[:, pair, g, :, :].rearrange("p w (h q) -> p (w h) q", h=2),
                                                 start=True, stop=True, skip_group_check=True)
                        last.then_inc(pv_full[u], 1)

                    def project_out(n):
                        pe.wait_ge(pv_taken[2], done(n))
                        pe.wait_ge(pv_taken[3], done(n))
                        for pair in range(PAIRS):
                            last = pe.matmul(ub[0][:, 0:P], wo_sb[:, pair, :], ot[:, pair, :], start=(pair == 0),
                                             stop=(pair == PAIRS - 1))
                        last.then_inc(wo_full, 1)

                    def ffn_turn(n, f, turned):
                        pe.wait_ge(f_shifted, done(f))
                        if turned:
                            pe.wait_ge(turn_taken[2], done(n))
                        for k in range(4):
                            last = pe.transpose(tb[0][:, k * P:(k + 1) * P], sx[:, k * P:(k + 1) * P], ident[:])
                        last.then_inc(f_turned, 1)

                    def ffn_turn_back(f):
                        pe.wait_ge(f_rows, done(f))
                        for k in range(4):
                            last = pe.transpose(tb[1][:, k * P:(k + 1) * P], xr[:, k, :], ident[:])
                        last.then_inc(f_back, 1)

                    def feature(n, f, j, turned):
                        if j == 0:
                            pe.wait_ge(f_xn, done(f))
                            for q in v_made:
                                pe.wait_ge(q, done(n - 1 if turned else n - 4))
                        else:
                            pe.wait_ge(gated[j - 1], done(f))
                            pe.wait_ge(hid_made[j - 1], done(f))
                        for k, full in ((0, gate_full), (1, val_full)):
                            col = (FF if k == 0 else 0) + FO[j]
                            pe.matmul(pj[k][0:FW[j], :], w1_sb[:, col:col + FW[j]], xn[:], start=True,
                                      stop=True).then_inc(full[j], 1)

                    def ffn_out(f):
                        for j in range(NF):
                            pe.wait_ge(hid_made[j], done(f))
                        for j in range(NF):
                            last = pe.matmul(tb[0][:], w2_sb[0:FW[j], j, :], hid[j][0:FW[j], :], start=(j == 0),
                                             stop=(j == NF - 1))
                        last.then_inc(f_out, 1)

                    def chunk(l, c, slots):
                        f, _ = ffn_chunk(l, c)
                        for k, stages in enumerate(slots):
                            n, s = count_of(l, c, k), k % 2
                            qk, turn, attend = (x in stages for x in ALL[:3])
                            norm, mlp = ("ffn" in stages and k == x for x in (2, 3))
                            after = f - 1 if k == 0 else None
                            if attend:
                                scores(n - 2, layer_start(c) and k == 2, 0, s)
                                scores(n - 2, layer_start(c) and k == 2, 1, s)
                            if mlp:
                                ffn_turn_back(f)
                            if qk:
                                if k == 0 and layer_start(c):
                                    pe.wait_ge(wqk_loaded, (l + 1) * (16 * QKC))
                                project(n, 0, s)
                                project(n, 1, s)
                            if "out" in stages:
                                if k == 3 and layer_start(c):
                                    pe.wait_ge(wo_loaded, (l + 1) * 16)
                                project_out(n - 3)
                            if mlp:
                                pe.wait_ge(ffn_loaded, 16 * FFN_LOADS * ffn_layers(l, c))
                                if turn:
                                    project(n - 1, 4, 1 - s)
                                    project(n - 1, 5, 1 - s)
                                    turn_qk(n - 1, 0, None, f)
                                    turn_qk(n - 1, 1, None, f)
                                feature(n, f, 0, turn)
                                if turn:
                                    turn_qk(n - 1, 2, None, f)
                                    turn_qk(n - 1, 3, None, f)
                                if attend:
                                    turn_probs(n - 2, 0)
                                    turn_probs(n - 2, 1)
                                feature(n, f, 1, turn)
                                if attend:
                                    values(n - 2, 0, s)
                                    values(n - 2, 1, s)
                                feature(n, f, 2, turn)
                                if attend:
                                    values(n - 2, 2, s)
                                    values(n - 2, 3, s)
                                if qk:
                                    project(n, 2, s, f)
                                    project(n, 3, s, f)
                                ffn_out(f)
                                continue
                            if turn:
                                turn_qk(n - 1, 0, after, None)
                                turn_qk(n - 1, 1, after, None)
                                if k == 1 and layer_start(c):
                                    pe.wait_ge(wv_loaded, (l + 1) * (16 * 2))
                                project(n - 1, 4, 1 - s, None, not qk)
                                project(n - 1, 5, 1 - s, None, not qk)
                                turn_qk(n - 1, 2, after, None)
                                turn_qk(n - 1, 3, after, None)
                            if attend:
                                turn_probs(n - 2, 0)
                                turn_probs(n - 2, 1)
                            if norm:
                                ffn_turn(n - 1, f, turn)
                            if qk:
                                project(n, 2, s, None, not turn)
                                project(n, 3, s, None, not turn)
                            if attend:
                                for u in range(4):
                                    values(n - 2, u, s)

                    start_ahead(pe, "tensor")
                    pe.wait_ge(mask_made, 1)
                    pe.wait_ge(inits, 4)
                    run_slots(pe, chunk)
            clear_semaphores(ctx)

        with ExitStack() as ctx:
            sb, ps, sem1 = alloc(ctx)
            tbanks = [ps(f"fbank{b}", [P, BANK]) for b in range(2)]
            rows = sb("rows", [P, NT, P])
            t_full, t_free, out_made, stored = sem1("l_full"), sem1("l_free"), sem1("out_made"), sem1("stored")
            ln3 = norm_steps("ln3", yrow, rows, sb("ln_sq3", [P, NT, P]))
            with nc.Block() as block:
                @block.tensor
                def _(pe):
                    for n in range(NT // 4):
                        if n >= 2:
                            pe.wait_ge(t_free, n - 1)
                        for j in range(4):
                            t = 4 * n + j
                            last = pe.transpose(tbanks[n % 2][:, j * P:(j + 1) * P], Y[:, 1 + t * P:1 + (t + 1) * P], ident[:])
                        last.then_inc(t_full, 1)

                @block.scalar
                def _(a):
                    for n in range(NT // 4):
                        a.wait_ge(t_full, n + 1)
                        a.activation(yrow[:, 4 * n:4 * n + 4, :], tbanks[n % 2][:].rearrange("p (n c) -> p n c", n=4),
                                     ACT.Copy).then_inc(t_free, 1)
                    ln3[1](a)

                @block.gpsimd
                def _(g):
                    ln3[2](g)

                @block.vector
                def _(v):
                    v.wait_ge(t_free, NT // 4)
                    ln3[0](v)
                    v.wait_ge(ln3[3], 1)
                    v.tensor_tensor(rows[:], rows[:], xin[:], ALU.add).then_inc(out_made, 1)

                @block.sync
                def _(sp):
                    sp.wait_ge(out_made, 1)
                    sp.dma_start(out.rearrange("a (n p) c -> p (a n) c", p=P), rows[:]).then_inc(stored, 16)
                    sp.wait_ge(stored, 16)


def shape_constants(T):
    import numpy as np
    half = np.arange(0, DIM_HEAD, 2, dtype=np.float32)
    inv_freq = np.float32(1.0) / np.float32(10000.0) ** (half / np.float32(DIM_HEAD))
    t = np.arange(T, dtype=np.float32)
    freqs = (t[:, None] * inv_freq[None, :]).astype(np.float64)
    base = (half.astype(np.float64) + 0.4 * DIM_HEAD) / (1.4 * DIM_HEAD)
    power = (np.arange(T) % P - P // 2) / (WINDOW // 2)
    scale = base[None, :] ** power[:, None]
    cos, sin = np.cos(freqs), np.sin(freqs)
    tables = []
    for sc in (scale, 1.0 / scale):
        tables += [cos * sc, cos * sc, sin * sc, -sin * sc]
    rot = np.concatenate(tables, 1).astype(np.float32)
    factor = np.tile(base ** (P / (WINDOW // 2)), 2 * 2).astype(np.float32)[:, None]
    p = np.arange(P)
    q, key = p[:, None, None] % WINDOW, np.arange(2 * WINDOW)[None, None, :]
    hidden = (key < q) | (key > q + WINDOW) | np.zeros((1, 2, 1), bool)
    before = (p[:, None, None] < P // 2) & (np.arange(2)[None, :, None] == 0) & (key < WINDOW)
    mask = np.stack([(hidden | before).reshape(P, P), hidden.reshape(P, P)], 1)
    return rot, factor, np.where(mask, np.float32(MASKED), np.float32(0.0))


_INS = ["L0_attn_x", "L0_attn_w_attn", "L0_attn_w_proj", "L0_ffn_Wqkv", "L0_ffn_q_scale", "L0_ffn_k_scale",
        "L0_ffn_Wo", "L0_ffn_ln_g", "L0_ffn_ln_b", "L0_ffn_W1", "L0_ffn_b1", "L0_ffn_W2", "L0_ffn_b2"]


def build(nc, inputs):
    import numpy as _np
    arrays = {f"in_{n}_dram": _np.ascontiguousarray(inputs[n]) for n in _INS}
    shape = arrays["in_L0_attn_x_dram"].shape
    for n, a in zip(("rot", "halo", "mask"), shape_constants(shape[1])):
        arrays[f"const_{n}_dram"] = _np.ascontiguousarray(a)
    args = [nc.dram_tensor(n, a.shape, mybir.dt.from_np(a.dtype), kind="ExternalInput").ap()
            for n, a in arrays.items()]
    out = nc.dram_tensor("out_0_dram", shape, F32, kind="ExternalOutput").ap()
    sandwich_kernel(nc, *args, out)
    return arrays, out


def kernel(**inputs):
    import concourse.bacc as _bacc
    from concourse.bass_utils import run_bass_kernel_spmd as _run

    nc = _bacc.Bacc("TRN2", target_bir_lowering=False, num_devices=1)
    arrays, _ = build(nc, inputs)
    r = _run(nc, [arrays], core_ids=[0])
    return r.results[0]["out_0_dram"]
```

```python
from contextlib import ExitStack

import concourse.bass as bass
from concourse import mybir

F32 = mybir.dt.float32
BF16 = mybir.dt.bfloat16
ALU = mybir.AluOpType
ACT = mybir.ActivationFunctionType
AX = mybir.AxisListType

P = 128
WINDOW = 32
DIM_HEAD = 64
QK_SCALE = 8.0
LN_EPS = 1e-5
NORM_EPS = 1e-12
MASKED = -1e30
LOWEST = -3e38
BANK = 512
PARTS = 3
HEADS1 = 16


def sandwich_kernel(nc, x_in, w_attn, w_proj, wqkv, q_scale, k_scale, wo, ln_g, ln_b, w1, b1, w2, b2,
                    rot_tables, halo_factor, window_mask, out):
    T, C = x_in.shape[1], x_in.shape[2]
    NT = T // P
    NCH = T // BANK
    DK = C // HEADS1
    DEPTH = wqkv.shape[0]
    INNER = wqkv.shape[2] // 3
    HEADS = INNER // DIM_HEAD
    PAIRS = HEADS // 2
    FF = w2.shape[1]
    NF = 3
    FW = [(FF + NF - 1) // NF] * (NF - 1)
    FW.append(FF - sum(FW))
    FO = [sum(FW[:j]) for j in range(NF)]
    NW = P // WINDOW
    assert C == P and NW == 4 and NT % 4 == 0 and PAIRS == 8 and DIM_HEAD == 64

    def loop(eng, start, end):
        return nc.Fori(start, end, engines=(eng.engine,), hint_back_edge=True)

    outer = ExitStack()
    phase_sems = {}

    def clear_semaphores(ctx):
        nums = sorted(s.num for s in phase_sems[ctx])
        with nc.Block() as block:
            @block.gpsimd
            def _(g):
                start = nums[0]
                for a, b in zip(nums, nums[1:] + [None]):
                    if b != a + 1:
                        g.sem_clear(range(start, a + 1))
                        start = b

    with outer:
        def alloc(ctx):
            def sb(name, shape, dt=F32):
                return ctx.enter_context(nc.sbuf_tensor(name, shape, dt))

            def ps(name, shape, dt=F32):
                return ctx.enter_context(nc.psum_tensor(name, shape, dt))

            def sem(name):
                made = ctx.enter_context(nc.semaphore(name))
                phase_sems.setdefault(ctx, []).append(made)
                return made
            return sb, ps, sem

        sb, ps, sem = alloc(outer)
        outer_sb = sb
        q_parts = nc.dram_tensor("q_parts", [PARTS, P, T], BF16, kind="Internal").ap()
        k_parts = nc.dram_tensor("k_parts", [PARTS, P, T], BF16, kind="Internal").ap()
        o_sums = nc.dram_tensor("o_sums", [P, T], F32, kind="Internal").ap()
        o_dens = nc.dram_tensor("o_dens", [HEADS1, T], F32, kind="Internal").ap()

        ident = sb("ident", [P, P])
        ident_bf = sb("ident_bf", [P, P], BF16)
        mask_qk = sb("mask_qk", [P, P], BF16)
        mask_kq = sb("mask_kq", [P, P], BF16)
        xin = sb("xin", [P, NT, P])
        yrow = sb("yrow", [P, NT, P])
        minus_half = sb("minus_half", [P, BANK // 8])
        Y = sb("Y", [P, T + 1])
        wproj_t = sb("wproj_t", [P, P])
        v_all = sb("v_all", [P, NT, P])

        const_made = sem("const_made")

        def group_norm(name, sb):
            stats, mv = sb(f"{name}_stats", [P, NT, 6]), sb(f"{name}_mv", [P, NT, 2])
            rstd = sb(f"{name}_rstd", [P, NT])
            shift = sb(f"{name}_shift", [P, NT])
            s = {k: sem(f"{name}_{k}") for k in ("stats", "mv", "eps", "rstd", "shift")}

            def statistics(v, g, rows):
                for k in range(4):
                    last = v.bn_stats(stats[:, 4 * g + k, :], rows[k])
                last.then_inc(s["stats"], 1)
                v.wait_ge(s["stats"], g + 1)
                for k in range(4):
                    last = v.bn_aggr(mv[:, 4 * g + k, :], stats[:, 4 * g + k, :])
                last.then_inc(s["mv"], 1)
                v.wait_ge(s["mv"], g + 1)
                v.tensor_scalar(rstd[:, 4 * g:4 * g + 4], mv[:, 4 * g:4 * g + 4, 1], LN_EPS, None,
                                ALU.add).then_inc(s["eps"], 1)

            def power(g_, g):
                g_.wait_ge(s["eps"], g + 1)
                cols = slice(4 * g, 4 * g + 4)
                g_.tensor_tensor(rstd[:, cols], rstd[:, cols], minus_half[:, 0:4], ALU.pow).then_inc(s["rstd"], 1)

            def apply(v, g, dst, rows):
                v.wait_ge(s["rstd"], g + 1)
                for k in range(4):
                    t = 4 * g + k
                    last = v.tensor_scalar(dst[k], rows[k], mv[:, t, 0:1], rstd[:, t:t + 1], ALU.subtract, ALU.mult)
                return last

            def offset(v, g):
                v.wait_ge(s["rstd"], g + 1)
                cols = slice(4 * g, 4 * g + 4)
                v.scalar_tensor_tensor(out=shift[:, cols], in0=mv[:, cols, 0], scalar=-1.0, in1=rstd[:, cols],
                                       op0=ALU.mult, op1=ALU.mult).then_inc(s["shift"], 1)

            def scaled(a, g, dst, rows):
                a.wait_ge(s["shift"], g + 1)
                for k in range(4):
                    t = 4 * g + k
                    last = a.activation(dst[k], rows[k], ACT.Identity, bias=shift[:, t:t + 1], scale=rstd[:, t:t + 1])
                return last
            return statistics, power, apply, offset, scaled

        def tiles_of(bank):
            return [bank[:, k * P:(k + 1) * P] for k in range(4)]

        def xin_tiles(g):
            return [xin[:, 4 * g + k, :] for k in range(4)]

        def yrow_tiles(g):
            return [yrow[:, 4 * g + k, :] for k in range(4)]

        heads_stack = ExitStack()
        heads_sb = alloc(heads_stack)[0]
        ROWS = PARTS * PARTS * DK
        MROW = 96
        KROWS = MROW + PARTS
        Qh = [heads_sb(f"Qh{s}", [P, T], BF16) for s in range(2)]
        Kh = [heads_sb(f"Kh{s}", [P, T], BF16) for s in range(2)]
        Vh = [heads_sb(f"Vh{s}", [P, NT, DK + 1]) for s in range(2)]
        with ExitStack() as ctx:
            sb, ps, sem1 = alloc(ctx)
            NG = NT // 4
            NB = 4
            w_rows = sb("w_rows", [P, 4, P])
            w_t = sb("w_t", [P, 3, P])
            xn_t = sb("xn_t", [P, T])
            part = [sb(f"part{b}", [P, PARTS, BANK], BF16) for b in range(NB)]
            rest = [sb(f"rest{b}", [P, BANK]) for b in range(2)]
            turned = [ps(f"turned{b}", [P, BANK]) for b in range(2)]
            proj = [ps(f"proj{b}", [P, BANK]) for b in range(2)]
            vproj = [ps(f"vproj{b}", [P, BANK]) for b in range(2)]
            x_loaded = [sem1(f"x_loaded{g}") for g in range(NG)]
            w_loaded, rows_normed = sem1("w_loaded"), sem1("rows_normed")
            turn_full, turn_free = sem1("turn_full"), sem1("turn_free")
            proj_full = sem1("proj_full")
            p1_made, r1_made, p2_made, r2_made = (sem1(n) for n in ("p1_made", "r1_made", "p2_made", "r2_made"))
            parts_stored = [sem1(f"parts_stored{b}") for b in range(NB)]
            v_full, v_free = sem1("v_full"), sem1("v_free")
            stats0, power0, apply0, _, _ = group_norm("ln0", sb)
            NQK = 2 * NCH

            with nc.Block() as block:
                @block.sync
                def _(sp):
                    for g in range(NG):
                        sp.dma_start(xin[:, 4 * g:4 * g + 4, :],
                                     x_in[:, g * BANK:(g + 1) * BANK, :].rearrange("a (n p) c -> p (a n) c", p=P)
                                     ).then_inc(x_loaded[g], 16)
                        if g == 0:
                            sp.dma_start(w_rows[:, 0:3, :], w_attn.rearrange("(n p) c -> p n c", p=P)).then_inc(w_loaded, 16)
                            sp.dma_start(w_rows[:, 3, :], w_proj).then_inc(w_loaded, 16)
                    for u in range(NQK):
                        dst = k_parts if u % 2 else q_parts
                        sp.wait_ge(r2_made, u + 1)
                        sp.dma_start(dst[:, :, u // 2 * BANK:(u // 2 + 1) * BANK].rearrange("a p c -> p a c"),
                                     part[u % NB][:]).then_inc(parts_stored[u % NB], 16)
                    for b in range(NB):
                        sp.wait_ge(parts_stored[b], 16 * len(range(b, NQK, NB)))

                @block.gpsimd
                def _(g):
                    g.memset(minus_half[:], -0.5).then_inc(const_made, 1)
                    g.memset(ident[:], 0.0).then_inc(const_made, 1)
                    g.memset(ident_bf[:], 0.0).then_inc(const_made, 1)
                    g.memset(mask_qk[:], 0.0).then_inc(const_made, 1)
                    g.memset(mask_kq[:], 0.0).then_inc(const_made, 1)
                    g.wait_ge(const_made, 5)
                    for t in (ident, ident_bf):
                        g.affine_select(out=t[:], in_=t[:], compare_op=ALU.not_equal, fill=1.0, base=0,
                                        pattern=[[-1, P]], channel_multiplier=1).then_inc(const_made, 1)
                    g.affine_select(out=mask_qk[:], in_=mask_qk[:], compare_op=ALU.is_ge, fill=MASKED, base=0,
                                    pattern=[[-1, P]], channel_multiplier=1).then_inc(const_made, 1)
                    g.affine_select(out=mask_kq[:], in_=mask_kq[:], compare_op=ALU.is_ge, fill=MASKED, base=0,
                                    pattern=[[1, P]], channel_multiplier=-1).then_inc(const_made, 1)
                    for n in range(NG):
                        power0(g, n)
                    for s in range(2):
                        g.memset(Qh[s][:], 0.0)
                        g.memset(Kh[s][:], 1.0)
                        g.memset(Vh[s][:], 1.0)

                @block.vector
                def _(v):
                    def split(u):
                        b, r = part[u % NB], rest[u % 2]
                        v.wait_ge(p1_made, u + 1)
                        v.tensor_tensor(r[:], proj[u % 2][:], b[:, 0, :], ALU.subtract).then_inc(r1_made, 1)
                        v.wait_ge(r1_made, u + 1)
                        v.tensor_copy(b[:, 1, :], r[:]).then_inc(p2_made, 1)
                        v.wait_ge(p2_made, u + 1)
                        v.tensor_tensor(b[:, 2, :], r[:], b[:, 1, :], ALU.subtract).then_inc(r2_made, 1)

                    def normalise(n):
                        apply0(v, n, yrow_tiles(n), xin_tiles(n)).then_inc(rows_normed, 1)

                    for n in range(NG):
                        v.wait_ge(x_loaded[n], 16)
                        stats0(v, n, xin_tiles(n))
                        if n >= 1:
                            normalise(n - 1)
                        if n >= 3:
                            split(2 * n - 6)
                            split(2 * n - 5)
                    normalise(NG - 1)
                    for u in range(max(0, NQK - 6), NQK):
                        split(u)

                @block.scalar
                def _(a):
                    def take_turned(n):
                        a.wait_ge(turn_full, n + 1)
                        if n == 0:
                            a.activation(w_t[:], turned[0][:, 0:3 * P].rearrange("p (n c) -> p n c", n=3),
                                         ACT.Copy)
                            a.activation(wproj_t[:], turned[0][:, 3 * P:4 * P], ACT.Copy).then_inc(turn_free, 1)
                        else:
                            a.activation(xn_t[:, (n - 1) * BANK:n * BANK], turned[n % 2][:],
                                         ACT.Copy).then_inc(turn_free, 1)

                    take_turned(0)
                    take_turned(1)
                    for n in range(NG):
                        if n + 2 <= NG:
                            take_turned(n + 2)
                        for u in (2 * n, 2 * n + 1):
                            a.wait_ge(proj_full, u + 1)
                            if u >= NB:
                                a.wait_ge(parts_stored[u % NB], 16 * (u // NB))
                            a.activation(part[u % NB][:, 0, :], proj[u % 2][:], ACT.Copy).then_inc(p1_made, 1)
                    for n in range(NG):
                        a.wait_ge(v_full, n + 1)
                        a.activation(v_all[:, 4 * n:4 * n + 4, :],
                                     vproj[n % 2][:].rearrange("p (n c) -> p n c", n=4),
                                     ACT.Copy).then_inc(v_free, 1)

                @block.tensor
                def _(pe):
                    def turn_tiles(n):
                        if n >= 1:
                            pe.wait_ge(rows_normed, n)
                        if n >= 2:
                            pe.wait_ge(turn_free, n - 1)
                        for j in range(4):
                            src = w_rows[:, j, :] if n == 0 else yrow[:, 4 * (n - 1) + j, :]
                            last = pe.transpose(turned[n % 2][:, j * P:(j + 1) * P], src, ident[:])
                        last.then_inc(turn_full, 1)

                    pe.wait_ge(const_made, 9)
                    pe.wait_ge(w_loaded, 32)
                    turn_tiles(0)
                    turn_tiles(1)
                    for n in range(NG):
                        if n + 2 <= NG:
                            turn_tiles(n + 2)
                        pe.wait_ge(turn_free, n + 2)
                        for u in (2 * n, 2 * n + 1):
                            if u >= 2:
                                pe.wait_ge(r1_made, u - 1)
                            pe.matmul(proj[u % 2][:], w_t[:, u % 2, :], xn_t[:, n * BANK:(n + 1) * BANK],
                                      start=True, stop=True).then_inc(proj_full, 1)
                    for n in range(NG):
                        if n >= 2:
                            pe.wait_ge(v_free, n - 1)
                        for j in range(4):
                            t = 4 * n + j
                            last = pe.matmul(vproj[n % 2][:, j * P:(j + 1) * P], xn_t[:, t * P:(t + 1) * P],
                                             w_t[:, 2, :], start=True, stop=True)
                        last.then_inc(v_full, 1)
            clear_semaphores(ctx)

        with heads_stack, ExitStack() as ctx:
            sb, ps, sem1 = alloc(ctx)
            mpart = [sb(f"mpart{s}", [P, NT, NCH]) for s in range(2)]
            mrow = [sb(f"mrow{s}", [P, NT]) for s in range(2)]
            nm = [sb(f"nm{s}", [NT, PARTS, P], BF16) for s in range(2)]
            nrest = [sb(f"nrest{s}", [NT, P]) for s in range(2)]
            probs = [sb(f"probs{r}", [P, BANK]) for r in range(4)]
            Oh = [sb(f"Oh{s}", [DK + 1, T]) for s in range(2)]
            sc_bank = [ps(f"sc{r}", [P, BANK]) for r in range(2)]
            st_bank = [ps(f"st{r}", [P, BANK]) for r in range(4)]
            o_bank = [ps(f"o{r}", [P, BANK]) for r in range(2)]
            m_bank = sc_bank[0]
            qk_loaded = [sem1(f"qk_loaded{s}") for s in range(2)]
            loads_begun = sem1("loads_begun")
            vh_made, mpart_set = sem1("vh_made"), sem1("mpart_set")
            sc_full, sc_free = sem1("sc_full"), sem1("sc_free")
            m_made, m_turned = sem1("m_made"), sem1("m_turned")
            n1, n2, n3, n4 = (sem1(n) for n in ("n1_made", "nrest_made", "n2_made", "n3_made"))
            m_placed = sem1("m_placed")
            st_full, exp_done, pv_done = sem1("st_full"), sem1("exp_done"), sem1("pv_done")
            o_free = sem1("o_free")
            o_stored = [sem1(f"o_stored{s}") for s in range(2)]

            max_units = [(i, kc) for i in range(NT) for kc in range(i // 4 + 1)]
            pv_units = [(c, j) for c in range(NCH) for j in range(4 * c + 4)]
            U = len(pv_units)
            assert len(max_units) == U
            PV_LAG = 2
            LOADS = PARTS * (PARTS + 1)
            SPAN = U // 2
            FIRST = U // 4 + 3 * U // 40
            assert U % 4 == 0

            with nc.Block() as block:
                @block.sync
                def _(sp):
                    for s in range(2):
                        sp.sem_inc(o_stored[s], 32)
                    sp.sem_inc(loads_begun, 1)

                    def load(h, s, free=True, parts=range(PARTS)):
                        if free:
                            sp.wait_ge(loads_begun, 1)
                            sp.wait_ge(pv_done, U * (h - 1))
                        for b in parts:
                            r0 = b * PARTS * DK
                            sp.dma_start(Qh[s][r0:r0 + PARTS * DK, :],
                                         q_parts[:, bass.ds(h * DK, DK), :]).then_inc(qk_loaded[s], 16)
                            for a in range(PARTS):
                                sp.dma_start(Kh[s][r0 + a * DK:r0 + (a + 1) * DK, :],
                                             k_parts[b, bass.ds(h * DK, DK), :]).then_inc(qk_loaded[s], 16)

                    def place_max(h, s):
                        sp.wait_ge(n4, h + 1)
                        for a in range(PARTS):
                            sp.dma_start(Qh[s][MROW + a:MROW + a + 1, :],
                                         nm[s][:, a, :]).then_inc(m_placed, 16)

                    def store(h, s):
                        sp.wait_ge(o_free, NCH * (h + 1))
                        sp.dma_start(o_sums[bass.ds(h * DK, DK), :], Oh[s][0:DK, :]).then_inc(o_stored[s], 16)
                        sp.dma_start(o_dens[bass.ds(h, 1), :], Oh[s][DK:DK + 1, :]).then_inc(o_stored[s], 16)

                    load(0, 0, False, range(1))
                    load(1, 1, False)
                    place_max(0, 0)
                    place_max(1, 1)
                    store(0, 0)
                    load(2, 0)
                    with loop(sp, 0, HEADS1 // 2 - 2) as it:
                        for r in range(2):
                            h = it * 2 + (1 + r)
                            place_max(h + 1, r)
                            store(h, 1 - r)
                            load(h + 2, 1 - r)
                    h = HEADS1 - 3
                    place_max(h + 1, 0)
                    store(h, 1)
                    load(h + 2, 1)
                    place_max(h + 2, 1)
                    store(h + 1, 0)
                    store(h + 2, 1)
                    for s in range(2):
                        sp.wait_ge(o_stored[s], 32 * (HEADS1 // 2 + 1))

                @block.gpsimd
                def _(g):
                    for s in range(2):
                        g.tensor_copy(Vh[s][:, :, 0:DK], v_all[:, :, s * DK:(s + 1) * DK]).then_inc(vh_made, 1)
                    with loop(g, 0, HEADS1 // 2 - 1) as it:
                        for s in range(2):
                            h = it * 2 + s
                            g.wait_ge(pv_done, U * (h + 1))
                            g.tensor_copy(Vh[s][:, :, 0:DK],
                                          v_all[:, :, bass.ds((h + 2) * DK, DK)]).then_inc(vh_made, 1)

                @block.vector
                def _(v):
                    for s in range(2):
                        v.memset(mpart[s][:], LOWEST).then_inc(mpart_set, 1)
                    v.wait_ge(mpart_set, 2)

                    def maxima(h, s, u):
                        i, kc = max_units[u]
                        n = BANK if kc < i // 4 else P * (i % 4 + 1)
                        v.wait_ge(sc_full, h * U + (u + 1))
                        v.tensor_reduce(mpart[s][:, i, kc:kc + 1], sc_bank[u % 2][:, 0:n], AX.X,
                                        ALU.max).then_inc(sc_free, 1)

                    def row_max(h, s):
                        v.wait_ge(sc_free, (h + 1) * U)
                        if not isinstance(h, int) or h >= 2:
                            v.wait_ge(m_turned, h - 1)
                        v.tensor_reduce(mrow[s][:], mpart[s][:], AX.X, ALU.max).then_inc(m_made, 1)

                    def split_max(h, s):
                        mt = m_bank[0:NT, 0:P]
                        v.wait_ge(m_turned, h + 1)
                        if not isinstance(h, int) or h >= 2:
                            v.wait_ge(m_placed, 16 * PARTS * (h - 1))
                        v.tensor_scalar(nm[s][:, 0, :], mt, -1.0, None, ALU.mult).then_inc(n1, 1)
                        v.wait_ge(n1, h + 1)
                        v.scalar_tensor_tensor(out=nrest[s][:], in0=mt, scalar=-1.0, in1=nm[s][:, 0, :],
                                               op0=ALU.mult, op1=ALU.subtract).then_inc(n2, 1)
                        v.wait_ge(n2, h + 1)
                        v.tensor_copy(nm[s][:, 1, :], nrest[s][:]).then_inc(n3, 1)
                        v.wait_ge(n3, h + 1)
                        v.tensor_tensor(nm[s][:, 2, :], nrest[s][:], nm[s][:, 1, :],
                                        ALU.subtract).then_inc(n4, 1)

                    def take_out(h, s, c, before):
                        last = pv_units.index((c, 4 * c + 3))
                        v.wait_ge(pv_done, h * U + (last + 1))
                        if c == 0 and (not isinstance(h, int) or h >= 2):
                            v.wait_ge(o_stored[s], 32 * before + 32)
                        v.tensor_copy(Oh[s][:, c * BANK:(c + 1) * BANK],
                                      o_bank[c % 2][0:DK + 1, :]).then_inc(o_free, 1)

                    def step(h, s, with_max, with_pv, before=0):
                        for u in range(U):
                            if with_max and FIRST <= u < FIRST + SPAN:
                                for k in range(2):
                                    maxima(h + 1, 1 - s, 2 * (u - FIRST) + k)
                            if with_max and u == FIRST + SPAN:
                                row_max(h + 1, 1 - s)
                                split_max(h + 1, 1 - s)
                            if with_pv and pv_units[u][0] > 0 and pv_units[u][1] == 3:
                                take_out(h, s, pv_units[u][0] - 1, before)
                        if with_pv:
                            take_out(h, s, NCH - 1, before)

                    step(-1, 1, True, False)
                    step(0, 0, True, True)
                    with loop(v, 0, HEADS1 // 2 - 1) as it:
                        for r in range(2):
                            step(it * 2 + (1 + r), 1 - r, True, True, it + r if r else it)
                    step(HEADS1 - 1, 1, False, True, HEADS1 // 2 - 1)

                @block.scalar
                def _(a):
                    for b in range(1, PARTS):
                        r0 = b * PARTS * DK
                        a.dma_start(Qh[0][r0:r0 + PARTS * DK, :], q_parts[:, 0:DK, :]).then_inc(qk_loaded[0], 16)
                        for k in range(PARTS):
                            a.dma_start(Kh[0][r0 + k * DK:r0 + (k + 1) * DK, :],
                                        k_parts[b, 0:DK, :]).then_inc(qk_loaded[0], 16)

                    def head(h, s):
                        for u, (c, j) in enumerate(pv_units):
                            off = max(0, j - 4 * c) * P
                            a.wait_ge(st_full, h * U + (u + 1))
                            if not isinstance(h, int) or h * U + u >= len(probs):
                                a.wait_ge(pv_done, h * U + (u + 1 - len(probs)))
                            a.activation(probs[u % 4][:, off:BANK], st_bank[u % 4][:, off:BANK],
                                         ACT.Exp, scale=float(DK) ** -0.5).then_inc(exp_done, 1)
                    head(0, 0)
                    head(1, 1)
                    with loop(a, 1, HEADS1 // 2) as it:
                        for s in range(2):
                            head(it * 2 + s, s)

                @block.tensor
                def _(pe):
                    def scores_qk(h, s, u):
                        i, kc = max_units[u]
                        n = BANK if kc < i // 4 else P * (i % 4 + 1)
                        if not isinstance(h, int) or h * U + u >= 2:
                            pe.wait_ge(sc_free, h * U + (u - 1))
                        if u == 0 and (not isinstance(h, int) or h >= 1):
                            pe.wait_ge(n2, h)
                        last = kc == i // 4
                        mm = pe.matmul(sc_bank[u % 2][:, 0:n], Qh[s][0:MROW, i * P:(i + 1) * P],
                                       Kh[s][0:MROW, kc * BANK:kc * BANK + n], start=True, stop=not last,
                                       skip_group_check=True)
                        if last:
                            mm = pe.matmul(sc_bank[u % 2][:, n - P:n], ident_bf[:], mask_qk[:], start=False,
                                           stop=True, skip_group_check=True)
                        mm.then_inc(sc_full, 1)

                    def turn_max(h, s):
                        pe.wait_ge(m_made, h + 1)
                        pe.transpose(m_bank[0:NT, 0:P], mrow[s][:], ident[:]).then_inc(m_turned, 1)

                    def scores_kq(h, s, u):
                        c, j = pv_units[u]
                        off = max(0, j - 4 * c) * P
                        st = st_bank[u % 4]
                        lag = len(st_bank)
                        if not isinstance(h, int) or h * U + u >= lag:
                            pe.wait_ge(exp_done, h * U + (u + 1 - lag))
                        diag = j >= 4 * c
                        mm = pe.matmul(st[:, off:BANK], Kh[s][0:KROWS, j * P:(j + 1) * P],
                                       Qh[s][0:KROWS, c * BANK + off:(c + 1) * BANK], start=True, stop=not diag,
                                       skip_group_check=True)
                        if diag:
                            mm = pe.matmul(st[:, off:off + P], ident_bf[:], mask_kq[:], start=False, stop=True,
                                           skip_group_check=True)
                        mm.then_inc(st_full, 1)

                    def values(h, s, u):
                        c, j = pv_units[u]
                        off = max(0, j - 4 * c) * P
                        pe.wait_ge(exp_done, h * U + (u + 1))
                        if j == 0 and (not isinstance(h, int) or NCH * h + c >= 2):
                            pe.wait_ge(o_free, NCH * h + (c - 1))
                        mm = pe.matmul(o_bank[c % 2][0:DK + 1, off:BANK], Vh[s][:, j, :], probs[u % 4][:, off:BANK],
                                       start=(j == 0), stop=(j == 4 * c + 3), skip_group_check=True)
                        mm.then_inc(pv_done, 1)

                    def step(h, s, with_max, with_pv, loads=1):
                        if with_pv:
                            pe.wait_ge(m_placed, 16 * PARTS * (h + 1))
                            pe.wait_ge(vh_made, h + 1)
                        for u in range(U + PV_LAG):
                            if with_max and u == FIRST:
                                pe.wait_ge(qk_loaded[1 - s], 16 * LOADS * loads)
                            if with_max and FIRST <= u < FIRST + SPAN:
                                scores_qk(h + 1, 1 - s, 2 * (u - FIRST))
                            if with_max and u == FIRST + SPAN + 1:
                                turn_max(h + 1, 1 - s)
                            if with_pv and u < U:
                                scores_kq(h, s, u)
                            if with_max and FIRST <= u < FIRST + SPAN:
                                scores_qk(h + 1, 1 - s, 2 * (u - FIRST) + 1)
                            if with_pv and u >= PV_LAG:
                                values(h, s, u - PV_LAG)

                    step(-1, 1, True, False)
                    step(0, 0, True, True)
                    with loop(pe, 0, HEADS1 // 2 - 1) as it:
                        for r in range(2):
                            step(it * 2 + (1 + r), 1 - r, True, True, it + 2)
                    step(HEADS1 - 1, 1, False, True)
            clear_semaphores(ctx)

        NCHK = INNER // BANK
        HC = BANK // DIM_HEAD
        PC = PAIRS // NCHK
        QKC = 2 * NCHK
        CONSTS = 7
        KW = WINDOW + P
        wqkv_sb = outer_sb("wqkv_sb", [P, 3 * INNER])
        wo_sb = outer_sb("wo_sb", [P, PAIRS, P])
        rot = outer_sb("rot", [P, NT, 4, DIM_HEAD])
        qk_scales = outer_sb("qk_scales", [P, DEPTH, 4, DIM_HEAD])
        halo_col = outer_sb("halo_col", [P, 1])
        wmask_f = outer_sb("wmask_f", [P, 2, P])
        qbd = outer_sb("qbd", [P, PAIRS, NW, 2, WINDOW])
        ptbd = outer_sb("ptbd", [P, PAIRS, 2, 2, 2 * WINDOW])
        kt = [outer_sb(f"kt{s}", [P, PAIRS, KW]) for s in range(2)]
        v_even = [outer_sb(f"v_even{s}", [P, INNER]) for s in range(2)]
        inits, consts_loaded = sem("inits"), sem("consts_loaded")
        wqk_loaded, wv_loaded, wo_loaded, ffn_loaded = (
            sem(x) for x in ("wqk_loaded", "wv_loaded", "wo_loaded", "ffn_loaded"))

        with ExitStack() as ctx:
            sb, ps, sem1 = alloc(ctx)
            o_t = sb("o_t", [P, T])
            den_rows = sb("den_rows", [HEADS1, T])
            rden = sb("rden", [P, NT, HEADS1])
            rden_c = sb("rden_c", [P, NT, HEADS1, DK])
            rt_bank = [ps(f"rt{g}", [P, BANK]) for g in range(4)]
            att_bank = [ps(f"att{g}", [P, BANK]) for g in range(4)]
            den_bank = att_bank[3]
            den_loaded, o_loaded = sem1("den_loaded"), sem1("o_loaded")
            den_turned, r_made, r_spread, r_turned = (sem1(x) for x in ("den_turned", "r_made", "r_spread", "r_turned"))
            on_made, a_full, a_normed, x1_made = (sem1(x) for x in ("on_made", "a_full", "a_normed", "x1_made"))
            y_rows, t_full, t_free = sem1("y_rows"), sem1("t_full"), sem1("t_free")
            stats1, power1, apply1, _, _ = group_norm("ln1", sb)
            stats2, power2, _, offset2, scaled2 = group_norm("ln2", sb)
            assert NG <= 4 and NT * HEADS1 <= BANK

            with nc.Block() as block:
                @block.sync
                def _(sp):
                    sp.dma_start(den_rows[:], o_dens).then_inc(den_loaded, 16)
                    sp.dma_start(o_t[:], o_sums).then_inc(o_loaded, 16)
                    for m in range(QKC + 2):
                        cols = slice(m * BANK, (m + 1) * BANK)
                        sp.dma_start(wqkv_sb[:, cols], wqkv[0, :, cols]).then_inc(wqk_loaded if m < QKC else wv_loaded, 16)
                    sp.dma_start(rot[:], rot_tables.rearrange("(n p) (k d) -> p n k d", p=P, k=4)).then_inc(consts_loaded, 16)
                    sp.dma_start(halo_col[:], halo_factor).then_inc(consts_loaded, 16)
                    sp.dma_start(wmask_f[:], window_mask).then_inc(consts_loaded, 16)
                    for k, src in enumerate((q_scale, q_scale, k_scale, k_scale)):
                        sp.dma_start(qk_scales[:, :, k, :], src.unsqueeze(0).broadcast_to([P, DEPTH, DIM_HEAD])
                                     ).then_inc(consts_loaded, 16)
                    sp.dma_start(wo_sb[:], wo[0].rearrange("(n p) c -> p n c", p=P)).then_inc(wo_loaded, 16)

                @block.gpsimd
                def _(g):
                    g.memset(kt[1][:], 0.0).then_inc(inits, 1)
                    g.memset(v_even[1][:], 0.0).then_inc(inits, 1)
                    g.memset(qbd[:], 0.0).then_inc(inits, 1)
                    g.memset(ptbd[:], 0.0).then_inc(inits, 1)
                    for n in range(NG):
                        power1(g, n)
                    for n in range(NG):
                        power2(g, n)

                @block.vector
                def _(v):
                    v.memset(Y[:, 0:1], 0.0)
                    v.wait_ge(den_turned, 1)
                    v.reciprocal(rden[:].rearrange("p n h -> p (n h)"), den_bank[:, 0:NT * HEADS1]).then_inc(r_made, 1)
                    v.wait_ge(o_loaded, 16)
                    for n in range(NG):
                        cols = slice(n * BANK, (n + 1) * BANK)
                        v.wait_ge(r_turned, n + 1)
                        v.tensor_tensor(o_t[:, cols], rt_bank[n][:], o_t[:, cols], ALU.mult).then_inc(on_made, 1)
                    for n in range(NG):
                        v.wait_ge(a_full, n + 1)
                        stats1(v, n, tiles_of(att_bank[n]))
                    for n in range(NG):
                        apply1(v, n, yrow_tiles(n), tiles_of(att_bank[n])).then_inc(a_normed, 1)
                        v.wait_ge(a_normed, n + 1)
                        rows = slice(4 * n, 4 * n + 4)
                        v.tensor_tensor(xin[:, rows, :], xin[:, rows, :], yrow[:, rows, :], ALU.add).then_inc(x1_made, 1)
                        v.wait_ge(x1_made, n + 1)
                        stats2(v, n, xin_tiles(n))
                        if n >= 1:
                            offset2(v, n - 1)
                    offset2(v, NG - 1)

                @block.scalar
                def _(a):
                    a.wait_ge(r_made, 1)
                    for n in range(NG):
                        rows = slice(4 * n, 4 * n + 4)
                        a.activation(rden_c[:, rows, :, :], rden[:, rows, :].unsqueeze(3).broadcast_to([P, 4, HEADS1, DK]),
                                     ACT.Copy).then_inc(r_spread, 1)
                    for n in range(NG):
                        scaled2(a, n, yrow_tiles(n), xin_tiles(n)).then_inc(y_rows, 1)
                    for n in range(NG):
                        a.wait_ge(t_full, n + 1)
                        a.activation(Y[:, 1 + n * BANK:1 + (n + 1) * BANK], rt_bank[n][:], ACT.Copy).then_inc(t_free, 1)

                @block.tensor
                def _(pe):
                    pe.wait_ge(den_loaded, 16)
                    for t in range(NT):
                        last = pe.transpose(den_bank[:, t * HEADS1:(t + 1) * HEADS1], den_rows[:, t * P:(t + 1) * P],
                                            ident[0:HEADS1, 0:HEADS1])
                    last.then_inc(den_turned, 1)
                    for n in range(NG):
                        pe.wait_ge(r_spread, n + 1)
                        for k in range(4):
                            last = pe.transpose(rt_bank[n][:, k * P:(k + 1) * P],
                                                rden_c[:, 4 * n + k, :, :].rearrange("p h d -> p (h d)"), ident[:])
                        last.then_inc(r_turned, 1)
                    for n in range(NG):
                        pe.wait_ge(on_made, n + 1)
                        for k in range(4):
                            t = 4 * n + k
                            last = pe.matmul(att_bank[n][:, k * P:(k + 1) * P], o_t[:, t * P:(t + 1) * P],
                                             wproj_t[:], start=True, stop=True)
                        last.then_inc(a_full, 1)
                    for n in range(NG):
                        pe.wait_ge(y_rows, n + 1)
                        for k in range(4):
                            last = pe.transpose(rt_bank[n][:, k * P:(k + 1) * P], yrow[:, 4 * n + k, :], ident[:])
                        last.then_inc(t_full, 1)
            clear_semaphores(ctx)

        with ExitStack() as ctx:
            sb, ps, sem2 = alloc(ctx)
            SIN_ON_GPSIMD = (3,)
            FFN_LOADS = 4 + 3 * NF

            w1_sb = sb("w1_sb", [P, 2 * FF])
            w2_sb = sb("w2_sb", [FW[0], NF, P])
            g_col, b_col, b2_col = sb("g_col", [P, 1]), sb("b_col", [P, 1]), sb("b2_col", [P, 1])
            b1_col = sb("b1_col", [FW[0], 2, NF])
            wmask = sb("wmask", [P, 2, P], BF16)
            Z = sb("Z", [P, T + 1])
            xs = [sb(f"xs{s}", [P, P]) for s in range(2)]
            tab = [sb(f"tab{s}", [P, 4, DIM_HEAD]) for s in range(2)]
            squares = [sb(f"squares{m}", [P, HC, DIM_HEAD]) for m in range(QKC)]
            ssum = [sb(f"ssum{m}", [P, HC]) for m in range(QKC)]
            rnorm = [sb(f"rnorm{m}", [P, HC]) for m in range(QKC)]
            raw = [sb(f"raw{m}", [P, HC, DIM_HEAD]) for m in range(QKC)]
            qk_n = [sb(f"qk_n{m}", [P, HC, DIM_HEAD]) for m in range(QKC)]
            prod_c = [sb(f"prod_c{m}", [P, HC, DIM_HEAD]) for m in range(QKC)]
            prod_s = [sb(f"prod_s{m}", [P, HC, DIM_HEAD]) for m in range(QKC)]
            v_odd = [sb(f"v_odd{s}", [P, INNER]) for s in range(2)]
            G = PC * 2
            smax = [sb(f"smax{b}", [P, G]) for b in range(2)]
            ssx = [sb(f"ssx{b}", [P, G, 2 * WINDOW]) for b in range(2)]
            den = [sb(f"wden{b}", [P, G]) for b in range(2)]
            rden = [sb(f"wrden{b}", [P, G]) for b in range(2)]
            probs = [sb(f"wprobs{b}", [P, G, 2 * WINDOW]) for b in range(2)]
            ot = sb("ot", [P, PAIRS, P])
            sx = sb("sx", [P, BANK])
            stats = sb("stats", [P, 4, 6])
            mv = sb("mv", [P, 4, 2])
            frstd = sb("frstd", [P, 4])
            xr = sb("xr", [P, 4, P])
            xn = sb("xn", [P, BANK])
            gate = [sb(f"gate{j}", [FW[0], BANK]) for j in range(NF)]
            hid = [sb(f"hid{j}", [FW[0], BANK]) for j in range(NF)]

            pj = [ps(f"pj{b}", [P, BANK]) for b in range(2)]
            tb = [ps(f"tb{b}", [P, BANK]) for b in range(2)]
            sb_ = [ps(f"sb{b}", [P, BANK]) for b in range(2)]
            ub = [ps(f"ub{b}", [P, BANK]) for b in range(2)]

            def per(name, count):
                return [sem2(f"{name}{m}") for m in range(count)]
            mask_made = sem2("mask_made")
            shifted, tabled = sem2("shifted"), sem2("tabled")
            proj_full = per("wproj_full", 6)
            squared, copied, summed, clamped, rsqrted, normed = (
                per(x, QKC) for x in ("squared", "copied", "summed", "clamped", "rsqrted", "normed"))
            v_made = per("v_made", 2)
            cos_done, sin_done = per("cos_done", QKC), per("sin_done", QKC)
            turn_full, turn_taken = per("wturn_full", QKC), per("wturn_taken", QKC)
            halo_made, odd_made = sem2("halo_made"), sem2("odd_made")
            sc_full, sc_max, sc_taken, exped, den_made, rden_made, prob_made = (
                per(x, 2) for x in ("wsc_full", "sc_max", "sc_taken", "exped", "den_made", "rden_made", "prob_made"))
            pt_full, pt_taken = per("pt_full", 2), per("pt_taken", 2)
            pv_full, pv_taken = per("pv_full", 4), per("pv_taken", 4)
            wo_full, z_made = sem2("wo_full"), sem2("z_made")
            y_made = sem2("y_made")
            f_shifted, f_turned, f_stats, f_mv, f_eps, f_rstd, f_rows, f_back, f_xn = (
                sem2(x) for x in ("f_shifted", "f_turned", "f_stats", "f_mv", "f_eps", "f_rstd", "f_rows",
                                  "f_back", "f_xn"))
            gate_full, val_full, gated, hid_made = (per(x, NF) for x in ("gate_full", "val_full", "gated", "hid_made"))
            f_out = sem2("f_out")

            COUNT0 = 2
            ahead = {
                "gpsimd": (tabled, *rsqrted, *[sin_done[m] for m in SIN_ON_GPSIMD], f_rstd),
                "vector": (*summed, *clamped, *normed, *cos_done,
                           *[sin_done[m] for m in range(QKC) if m not in SIN_ON_GPSIMD], *sc_max,
                           *sc_taken, *den_made, *rden_made, *prob_made, z_made, f_stats, f_mv, f_eps, f_rows,
                           *hid_made),
                "scalar": (shifted, halo_made, *squared, *copied, *v_made, *turn_taken, *exped, *pt_taken, *pv_taken,
                           f_shifted, f_xn, *gated),
                "tensor": (*proj_full, *turn_full, *sc_full, *pt_full, *pv_full, wo_full,
                           f_turned, f_back, *gate_full, *val_full, f_out),
            }

            def start_ahead(eng, name):
                for q in ahead[name]:
                    eng.sem_inc(q, COUNT0)

            def done(n):
                return n + 1

            def odd_done(n):
                return 32 * (n + 1)

            def chunk_done(f):
                return f + 1 + NCH

            SLOTS = BANK // P
            ALL = ("qk", "turn", "attend", "out", "ffn")

            def run_slots(eng, chunk):
                everything = [ALL] * SLOTS
                chunk(0, 0, [ALL[:k + 1] for k in range(SLOTS)])
                with loop(eng, 0, DEPTH - 1) as l:
                    with loop(eng, 1, NCH) as c:
                        chunk(l, c, everything)
                    chunk(l + 1, 0, everything)
                with loop(eng, 1, NCH) as c:
                    chunk(DEPTH - 1, c, everything)
                chunk(DEPTH, 0, [ALL[1:], ALL[2:], ALL[3:], ALL[4:]])

            def count_of(l, c, k):
                return l * NT + c * SLOTS + (k + COUNT0)

            def layer_start(c):
                return isinstance(c, int) and c == 0

            def tile_at(c, k):
                return (NT + k if k < 0 else k) if layer_start(c) else c * SLOTS + k

            def ffn_chunk(l, c):
                return l * NCH + c + (COUNT0 - 1), (NCH - 1 if layer_start(c) else c - 1)

            def ffn_layers(l, c):
                return l if layer_start(c) else l + 1

            def sine_product(eng, m, s):
                k = 2 * (m // NCHK) + 1
                table = tab[s][:, k, :].rearrange("p (t d) -> p t d", t=2).unsqueeze(1)
                src = qk_n[m][:].rearrange("p h (t d) -> p h t d", t=2)
                dst = prod_s[m][:].rearrange("p h (t d) -> p h t d", t=2)
                eng.tensor_tensor(dst[:, :, ::-1, :], src, table.broadcast_to([P, HC, 2, DIM_HEAD // 2]),
                                  ALU.mult).then_inc(sin_done[m], 1)

            with nc.Block() as block:
                @block.sync
                def _(sp):
                    sp.sem_inc(odd_made, 32 * COUNT0)

                    def shift_values(n, s):
                        sp.wait_ge(v_made[0], done(n))
                        sp.wait_ge(v_made[1], done(n))
                        sp.dma_start(v_odd[s][WINDOW:P, :], v_even[s][0:P - WINDOW, :]).then_inc(odd_made, 16)
                        sp.dma_start(v_odd[s][0:WINDOW, :], v_even[1 - s][P - WINDOW:P, :]).then_inc(odd_made, 16)

                    def load_projection(l, m, loaded):
                        sp.wait_ge(consts_loaded, 16 * CONSTS)
                        sp.wait_ge(proj_full[m], l * NT + COUNT0)
                        cols = slice(m * BANK, (m + 1) * BANK)
                        sp.dma_start(wqkv_sb[:, cols],
                                     wqkv[bass.ds(l, 1), :, cols].rearrange("a c n -> (a c) n")).then_inc(loaded, 16)

                    def load_out_weights(l):
                        sp.wait_ge(consts_loaded, 16 * CONSTS)
                        sp.wait_ge(wo_full, l * NT + COUNT0)
                        sp.dma_start(wo_sb[:], wo[bass.ds(l, 1), :, :].rearrange("a (n p) c -> p (a n) c", p=P)
                                     ).then_inc(wo_loaded, 16)

                    def load_ffn(l):
                        sp.wait_ge(consts_loaded, 16 * CONSTS)
                        sp.wait_ge(y_made, l * NCH + (NCH + COUNT0))
                        wl = bass.ds(l, 1)
                        for dst, src in ((g_col, ln_g), (b_col, ln_b), (b2_col, b2)):
                            sp.dma_start(dst[:], src[wl, :].rearrange("a p -> p a")).then_inc(ffn_loaded, 16)
                        for k in range(2):
                            for j in range(NF):
                                sp.dma_start(b1_col[0:FW[j], k, j:j + 1],
                                             b1[wl, k * FF + FO[j]:k * FF + FO[j] + FW[j]].rearrange("a p -> p a")
                                             ).then_inc(ffn_loaded, 16)
                        sp.dma_start(w1_sb[:], w1[wl, :, :].rearrange("a c n -> (a c) n")).then_inc(ffn_loaded, 16)
                        for j in range(NF):
                            sp.dma_start(w2_sb[0:FW[j], j, :],
                                         w2[wl, FO[j]:FO[j] + FW[j], :].rearrange("a c n -> (a c) n")
                                         ).then_inc(ffn_loaded, 16)

                    def chunk(l, c, slots):
                        loads = layer_start(c) and not (isinstance(l, int) and l in (0, DEPTH))
                        if loads:
                            for m in range(QKC):
                                load_projection(l, m, wqk_loaded)
                        for k, stages in enumerate(slots):
                            if k == 2 and loads:
                                load_out_weights(l)
                            if "turn" in stages:
                                shift_values(count_of(l, c, k) - 1, (k + 1) % 2)
                            if k == 0 and loads:
                                load_projection(l, QKC, wv_loaded)
                                load_projection(l, QKC + 1, wv_loaded)
                        if layer_start(c) and not (isinstance(l, int) and l == DEPTH):
                            load_ffn(l)

                    run_slots(sp, chunk)
                    for q, count in ((consts_loaded, CONSTS), (wqk_loaded, QKC * DEPTH), (wv_loaded, 2 * DEPTH),
                                     (wo_loaded, DEPTH), (ffn_loaded, FFN_LOADS * DEPTH),
                                     (odd_made, 2 * (NT * DEPTH + COUNT0))):
                        sp.wait_ge(q, 16 * count)

                @block.gpsimd
                def _(g):
                    start_ahead(g, "gpsimd")

                    def make_table(n, l, i, s):
                        g.wait_ge(consts_loaded, 16 * CONSTS)
                        g.wait_ge(cos_done[QKC - 1], done(n - 2))
                        g.wait_ge(sin_done[QKC - 1], done(n - 2))
                        scales = qk_scales[:, bass.ds(l, 1), :, :].rearrange("p a k d -> p (a k) d")
                        g.tensor_tensor(tab[s][:], rot[:, bass.ds(i, 1), :, :].rearrange("p a k d -> p (a k) d"),
                                        scales, ALU.mult).then_inc(tabled, 1)

                    def power(n, m):
                        g.wait_ge(clamped[m], done(n))
                        g.wait_ge(normed[m], done(n - 1))
                        g.tensor_tensor(rnorm[m][:], ssum[m][:], minus_half[:, 0:HC], ALU.pow).then_inc(rsqrted[m], 1)

                    def sines(n, m, s):
                        g.wait_ge(normed[m], done(n))
                        g.wait_ge(tabled, done(n))
                        g.wait_ge(turn_full[m], done(n - 1))
                        sine_product(g, m, s)

                    def ffn_power(f):
                        g.wait_ge(f_eps, done(f))
                        g.tensor_tensor(frstd[:], frstd[:], minus_half[:, 0:4], ALU.pow).then_inc(f_rstd, 1)

                    def chunk(l, c, slots):
                        f, _ = ffn_chunk(l, c)
                        for k, stages in enumerate(slots):
                            n, s = count_of(l, c, k), k % 2
                            if "turn" in stages:
                                for m in SIN_ON_GPSIMD:
                                    sines(n - 1, m, 1 - s)
                            if "qk" in stages:
                                make_table(n, l, tile_at(c, k), s)
                            if "qk" in stages:
                                power(n, 0)
                                power(n, 1)
                            if "ffn" in stages and k == 2:
                                ffn_power(f)
                            if "qk" in stages:
                                power(n, 2)
                                power(n, 3)

                    g.wait_ge(consts_loaded, 16 * CONSTS)
                    run_slots(g, chunk)

                @block.vector
                def _(v):
                    start_ahead(v, "vector")
                    v.sem_inc(y_made, COUNT0 + NCH)
                    v.memset(Z[:, 0:1], 0.0)
                    v.wait_ge(consts_loaded, 16 * CONSTS)
                    v.tensor_copy(wmask[:], wmask_f[:]).then_inc(mask_made, 1)

                    def sums(n, m):
                        v.wait_ge(squared[m], done(n))
                        v.tensor_reduce(ssum[m][:], squares[m][:], AX.X, ALU.add).then_inc(summed[m], 1)
                        v.wait_ge(summed[m], done(n))
                        v.tensor_scalar(ssum[m][:], ssum[m][:], NORM_EPS ** 2, None, ALU.max).then_inc(clamped[m], 1)

                    def rotate(n, m, s):
                        v.wait_ge(copied[m], done(n))
                        v.wait_ge(rsqrted[m], done(n))
                        v.wait_ge(sin_done[m], done(n - 1))
                        v.tensor_tensor(qk_n[m][:], raw[m][:], rnorm[m][:].unsqueeze(2).broadcast_to([P, HC, DIM_HEAD]),
                                        ALU.mult).then_inc(normed[m], 1)
                        v.wait_ge(normed[m], done(n))
                        v.wait_ge(turn_full[m], done(n - 1))
                        v.wait_ge(tabled, done(n))
                        k = 2 * (m // NCHK)
                        v.tensor_tensor(prod_c[m][:], qk_n[m][:],
                                        tab[s][:, k, :].unsqueeze(1).broadcast_to([P, HC, DIM_HEAD]),
                                        ALU.mult).then_inc(cos_done[m], 1)
                        if m not in SIN_ON_GPSIMD:
                            sine_product(v, m, s)

                    def soft_in(n, b):
                        v.wait_ge(sc_full[b], done(n))
                        src = sb_[b][:].rearrange("p (g k) -> p g k", g=G)
                        v.tensor_reduce(smax[b][:], src, AX.X, ALU.max).then_inc(sc_max[b], 1)
                        v.wait_ge(sc_max[b], done(n))
                        v.wait_ge(prob_made[b], done(n - 1))
                        v.tensor_tensor(ssx[b][:], src, smax[b][:].unsqueeze(2).broadcast_to([P, G, 2 * WINDOW]),
                                        ALU.subtract).then_inc(sc_taken[b], 1)

                    def soft_out(n, b):
                        v.wait_ge(exped[b], done(n))
                        v.tensor_reduce(den[b][:], ssx[b][:], AX.X, ALU.add).then_inc(den_made[b], 1)
                        v.wait_ge(den_made[b], done(n))
                        v.reciprocal(rden[b][:], den[b][:]).then_inc(rden_made[b], 1)
                        v.wait_ge(rden_made[b], done(n))
                        v.wait_ge(pt_full[b], done(n - 1))
                        v.tensor_tensor(probs[b][:], ssx[b][:],
                                        rden[b][:].unsqueeze(2).broadcast_to([P, G, 2 * WINDOW]),
                                        ALU.mult).then_inc(prob_made[b], 1)

                    def add_stream(n, i):
                        v.wait_ge(wo_full, done(n))
                        v.tensor_tensor(Z[:, bass.ds(i * P + 1, P)], ub[0][:, 0:P], Y[:, bass.ds(i * P + 1, P)],
                                        ALU.add).then_inc(z_made, 1)

                    def ffn_stats(f):
                        v.wait_ge(f_turned, done(f))
                        for k in range(4):
                            last = v.bn_stats(stats[:, k, :], tb[0][:, k * P:(k + 1) * P])
                        last.then_inc(f_stats, 1)
                        v.wait_ge(consts_loaded, 16 * CONSTS)
                        v.wait_ge(f_stats, done(f))
                        for k in range(4):
                            last = v.bn_aggr(mv[:, k, :], stats[:, k, :])
                        last.then_inc(f_mv, 1)
                        v.wait_ge(f_mv, done(f))
                        v.tensor_scalar(frstd[:], mv[:, :, 1], LN_EPS, None, ALU.add).then_inc(f_eps, 1)

                    def ffn_rows(f):
                        v.wait_ge(f_rstd, done(f))
                        for k in range(4):
                            last = v.tensor_scalar(xr[:, k, :], tb[0][:, k * P:(k + 1) * P], mv[:, k, 0:1],
                                                   frstd[:, k:k + 1], ALU.subtract, ALU.mult)
                        last.then_inc(f_rows, 1)

                    def hidden(f, j):
                        v.wait_ge(val_full[j], done(f))
                        v.wait_ge(gated[j], done(f))
                        v.wait_ge(f_out, done(f - 1))
                        v.scalar_tensor_tensor(out=hid[j][0:FW[j], :], in0=pj[1][0:FW[j], :],
                                               scalar=b1_col[0:FW[j], 0, j:j + 1], in1=gate[j][0:FW[j], :],
                                               op0=ALU.add, op1=ALU.mult).then_inc(hid_made[j], 1)

                    def add_ffn(f, place):
                        v.wait_ge(f_out, done(f))
                        cols = bass.ds(place * BANK + 1, BANK)
                        v.scalar_tensor_tensor(out=Y[:, cols], in0=tb[0][:], scalar=b2_col[:, 0:1], in1=Z[:, cols],
                                               op0=ALU.add, op1=ALU.add).then_inc(y_made, 1)

                    def chunk(l, c, slots):
                        f, place = ffn_chunk(l, c)
                        for k, stages in enumerate(slots):
                            n, s = count_of(l, c, k), k % 2
                            qk, turn, attend = (x in stages for x in ALL[:3])
                            norm, mlp = ("ffn" in stages and k == x for x in (2, 3))
                            if attend:
                                soft_in(n - 2, 0)
                                soft_in(n - 2, 1)
                                soft_out(n - 2, 0)
                            if turn:
                                rotate(n - 1, 2, 1 - s)
                            if "out" in stages:
                                add_stream(n - 3, tile_at(c, k - 3))
                            if turn:
                                rotate(n - 1, 3, 1 - s)
                            if attend:
                                soft_out(n - 2, 1)
                            if qk:
                                sums(n, 0)
                                sums(n, 1)
                            if mlp:
                                v.wait_ge(ffn_loaded, 16 * FFN_LOADS * ffn_layers(l, c))
                                hidden(f, 0)
                            if norm:
                                ffn_stats(f)
                            if mlp:
                                hidden(f, 1)
                            if qk:
                                rotate(n, 0, s)
                            if norm:
                                ffn_rows(f)
                            if mlp:
                                hidden(f, 2)
                            if qk:
                                sums(n, 2)
                                rotate(n, 1, s)
                                sums(n, 3)
                            if mlp:
                                add_ffn(f, place)

                    run_slots(v, chunk)

                @block.scalar
                def _(a):
                    half = P // 2

                    def shift_tile(n, l, c, i, s):
                        a.wait_ge(y_made, l * NCH + c + (COUNT0 + 1))
                        a.wait_ge(proj_full[5], done(n - 2))
                        a.activation(xs[s][0:half, :], Y[0:half, bass.ds(i * P + 1, P)], ACT.Copy)
                        a.activation(xs[s][half:P, :], Y[half:P, bass.ds(i * P, P)], ACT.Copy).then_inc(shifted, 1)

                    def take_qk(n, m):
                        a.wait_ge(proj_full[m], done(n))
                        a.wait_ge(summed[m], done(n - 1))
                        a.activation(squares[m][:], pj[m % 2][:].rearrange("p (h d) -> p h d", h=HC),
                                     ACT.Square).then_inc(squared[m], 1)
                        a.wait_ge(normed[m], done(n - 1))
                        a.activation(raw[m][:], pj[m % 2][:].rearrange("p (h d) -> p h d", h=HC),
                                     ACT.Copy).then_inc(copied[m], 1)

                    def take_v(n, k, s):
                        a.wait_ge(proj_full[QKC + k], done(n))
                        a.wait_ge(pv_full[3], done(n - 2))
                        a.wait_ge(odd_made, odd_done(n - 1))
                        a.activation(v_even[s][:, k * BANK:(k + 1) * BANK], pj[k][:], ACT.Copy).then_inc(v_made[k], 1)

                    def take_q(n, m):
                        a.wait_ge(turn_full[m], done(n))
                        a.wait_ge(sc_full[1], done(n - 1))
                        for h in range(2):
                            rows = slice(h * half, (h + 1) * half)
                            last = a.activation(qbd[rows, m * PC:(m + 1) * PC, :, h, :],
                                                tb[m % 2][rows, :].rearrange("p (a w q) -> p a w q", a=PC, w=NW), ACT.Copy)
                        last.then_inc(turn_taken[m], 1)

                    def take_k(n, m, s):
                        a.wait_ge(turn_full[m], done(n))
                        a.wait_ge(halo_made, done(n - 1))
                        a.wait_ge(sc_full[1], done(n - 2))
                        k = m - NCHK
                        a.activation(kt[s][:, k * PC:(k + 1) * PC, WINDOW:KW],
                                     tb[m % 2][:].rearrange("p (a t) -> p a t", a=PC), ACT.Copy).then_inc(turn_taken[m], 1)

                    def halo(n, s):
                        for m in range(NCHK, QKC):
                            a.wait_ge(turn_taken[m], done(n - 1))
                        a.wait_ge(sc_full[1], done(n - 2))
                        a.activation(kt[s][:, :, 0:WINDOW], kt[1 - s][:, :, P:KW], ACT.Copy,
                                     scale=halo_col[:, 0:1]).then_inc(halo_made, 1)

                    def exps(n, b):
                        a.wait_ge(sc_taken[b], done(n))
                        a.activation(ssx[b][:], ssx[b][:], ACT.Exp, scale=QK_SCALE).then_inc(exped[b], 1)

                    def take_pt(n, b):
                        a.wait_ge(pt_full[b], done(n))
                        a.wait_ge(pv_full[3], done(n - 1))
                        for w in range(2):
                            rows = slice(w * half, (w + 1) * half)
                            last = a.activation(ptbd[rows, b * PC:(b + 1) * PC, :, w, :],
                                                ub[b][rows, :].rearrange("p (a g q) -> p a g q", a=PC, g=2), ACT.Copy)
                        last.then_inc(pt_taken[b], 1)

                    def take_o(n, u):
                        a.wait_ge(pv_full[u], done(n))
                        a.wait_ge(wo_full, done(n - 1))
                        for h in range(2):
                            rows = slice(h * half, (h + 1) * half)
                            src = ub[u % 2][rows, :].rearrange("p (aw h q) -> p aw h q", h=2, q=2 * WINDOW)[:, :, h, :]
                            last = a.activation(ot[rows, 2 * u:2 * u + 2, :].rearrange("p a (w q) -> p (a w) q", w=2),
                                                src, ACT.Copy)
                        last.then_inc(pv_taken[u], 1)

                    def ffn_shift(n, f, place):
                        a.wait_ge(z_made, done(n))
                        a.wait_ge(f_turned, done(f - 1))
                        a.activation(sx[0:half, :], Z[0:half, bass.ds(place * BANK + 1, BANK)], ACT.Copy)
                        a.activation(sx[half:P, :], Z[half:P, bass.ds(place * BANK, BANK)],
                                     ACT.Copy).then_inc(f_shifted, 1)

                    def ffn_scale(f):
                        a.wait_ge(f_back, done(f))
                        a.wait_ge(val_full[NF - 1], done(f - 1))
                        a.activation(xn[:], tb[1][:], ACT.Identity, bias=b_col[:, 0:1],
                                     scale=g_col[:, 0:1]).then_inc(f_xn, 1)

                    def gelu(f, j):
                        a.wait_ge(gate_full[j], done(f))
                        a.wait_ge(hid_made[j], done(f - 1))
                        a.activation(gate[j][0:FW[j], :], pj[0][0:FW[j], :], ACT.Gelu,
                                     bias=b1_col[0:FW[j], 1, j:j + 1]).then_inc(gated[j], 1)

                    def chunk(l, c, slots):
                        f, place = ffn_chunk(l, c)
                        for k, stages in enumerate(slots):
                            n, s = count_of(l, c, k), k % 2
                            qk, turn, attend = (x in stages for x in ALL[:3])
                            norm, mlp = ("ffn" in stages and k == x for x in (2, 3))
                            if qk:
                                shift_tile(n, l, c, tile_at(c, k), s)
                            if turn:
                                halo(n - 1, 1 - s)
                            if attend:
                                exps(n - 2, 0)
                            if qk:
                                take_qk(n, 0)
                            if attend:
                                exps(n - 2, 1)
                            if qk:
                                take_qk(n, 1)
                            if mlp:
                                a.wait_ge(ffn_loaded, 16 * FFN_LOADS * ffn_layers(l, c))
                                ffn_scale(f)
                                if turn:
                                    take_v(n - 1, 0, 1 - s)
                                    take_v(n - 1, 1, 1 - s)
                                    take_q(n - 1, 0)
                                    take_q(n - 1, 1)
                                gelu(f, 0)
                                if turn:
                                    take_k(n - 1, 2, 1 - s)
                                    take_k(n - 1, 3, 1 - s)
                                if attend:
                                    take_pt(n - 2, 0)
                                    take_pt(n - 2, 1)
                                gelu(f, 1)
                                if attend:
                                    take_o(n - 2, 0)
                                    take_o(n - 2, 1)
                                gelu(f, 2)
                                if attend:
                                    take_o(n - 2, 2)
                                    take_o(n - 2, 3)
                                if qk:
                                    take_qk(n, 2)
                                    take_qk(n, 3)
                                continue
                            if turn:
                                take_q(n - 1, 0)
                                take_q(n - 1, 1)
                                take_v(n - 1, 0, 1 - s)
                                take_v(n - 1, 1, 1 - s)
                            if norm:
                                ffn_shift(n - 3, f, place)
                            if turn:
                                take_k(n - 1, 2, 1 - s)
                                take_k(n - 1, 3, 1 - s)
                            if attend:
                                take_pt(n - 2, 0)
                                take_pt(n - 2, 1)
                            if qk:
                                take_qk(n, 2)
                            if attend:
                                take_o(n - 2, 0)
                                take_o(n - 2, 1)
                            if qk:
                                take_qk(n, 3)
                            if attend:
                                take_o(n - 2, 2)
                                take_o(n - 2, 3)

                    start_ahead(a, "scalar")
                    a.wait_ge(inits, 4)
                    run_slots(a, chunk)

                @block.tensor
                def _(pe):
                    def project(n, m, s, ffn_f=None, alone=False):
                        if m == 0:
                            pe.wait_ge(shifted, done(n))
                        if ffn_f is not None and m % 2 == 0:
                            pe.wait_ge(gated[NF - 1], done(ffn_f))
                            pe.wait_ge(hid_made[NF - 1], done(ffn_f))
                        if m < 2:
                            pe.wait_ge(copied[m + 2], done(n - 1))
                        elif m < QKC:
                            pe.wait_ge(*((copied[m - 2], done(n)) if alone else (v_made[m - 2], done(n - 1))))
                        else:
                            pe.wait_ge(*((copied[m - 2], done(n)) if alone else (copied[m - QKC], done(n + 1))))
                        pe.matmul(pj[m % 2][:], xs[s][:], wqkv_sb[:, m * BANK:(m + 1) * BANK], start=True,
                                  stop=True).then_inc(proj_full[m], 1)

                    def turn_qk(n, m, out_f, norm_f):
                        pe.wait_ge(cos_done[m], done(n))
                        pe.wait_ge(sin_done[m], done(n))
                        if m < 2:
                            pe.wait_ge(turn_taken[m + 2], done(n - 1))
                            if out_f is not None and m == 0:
                                pe.wait_ge(y_made, chunk_done(out_f))
                            if norm_f is not None and m == 1:
                                pe.wait_ge(f_xn, done(norm_f))
                        else:
                            pe.wait_ge(turn_taken[m - 2], done(n))
                        for a in range(PC):
                            for k, src in enumerate((prod_c, prod_s)):
                                last = pe.matmul(tb[m % 2][:, a * P:(a + 1) * P],
                                                 src[m][:].rearrange("p h d -> p (h d)")[:, a * P:(a + 1) * P], ident[:],
                                                 start=(k == 0), stop=(k == 1), is_transpose=True, skip_group_check=True)
                        last.then_inc(turn_full[m], 1)

                    def scores(n, first, b, s):
                        pe.wait_ge(sc_taken[b], done(n - 1))
                        for m in (b, b + 2):
                            pe.wait_ge(turn_taken[m], done(n))
                        pe.wait_ge(halo_made, done(n))
                        which = 0 if first else 1
                        pe.matmul(sb_[b][:], ident_bf[:], wmask[:, which:which + 1, :].broadcast_to([P, PC, P]),
                                  start=True, stop=False, skip_group_check=True)
                        for a in range(PC):
                            pair = b * PC + a
                            for g in range(2):
                                for w in range(2):
                                    win = 2 * w + g
                                    col = (2 * a + w) * 2 * WINDOW
                                    last = pe.matmul(sb_[b][64 * g:64 * g + 64, col:col + 2 * WINDOW],
                                                     qbd[:, pair, win, :, :].rearrange("p h q -> p (h q)"),
                                                     kt[s][:, pair, win * WINDOW:win * WINDOW + 2 * WINDOW],
                                                     start=False, stop=True, skip_group_check=True)
                        last.then_inc(sc_full[b], 1)

                    def turn_probs(n, b):
                        pe.wait_ge(prob_made[b], done(n))
                        if b == 0:
                            pe.wait_ge(z_made, done(n - 1))
                        else:
                            pe.wait_ge(pv_taken[3], done(n - 1))
                        for a in range(PC):
                            last = pe.transpose(ub[b][:, a * P:(a + 1) * P],
                                                probs[b][:].rearrange("p g k -> p (g k)")[:, a * P:(a + 1) * P], ident[:])
                        last.then_inc(pt_full[b], 1)

                    def values(n, u, s):
                        pe.wait_ge(pt_taken[u // 2], done(n))
                        if u < 2:
                            pe.wait_ge(pt_taken[u], done(n))
                            if u == 0:
                                pe.wait_ge(odd_made, odd_done(n))
                                pe.wait_ge(v_made[1], done(n))
                        else:
                            pe.wait_ge(pv_taken[u - 2], done(n))
                        for a in range(2):
                            pair = 2 * u + a
                            for g in range(2):
                                vals = (v_odd if g == 0 else v_even)[s]
                                dst = ub[u % 2][:, a * 256:(a + 1) * 256].rearrange(
                                    "p (wh g q) -> p wh g q", g=2, q=WINDOW)[:, :, g, :]
                                last = pe.matmul(dst, vals[:, pair * P:(pair + 1) * P],
                                                 ptbd[:, pair, g, :, :].rearrange("p w (h q) -> p (w h) q", h=2),
                                                 start=True, stop=True, skip_group_check=True)
                        last.then_inc(pv_full[u], 1)

                    def project_out(n):
                        pe.wait_ge(pv_taken[2], done(n))
                        pe.wait_ge(pv_taken[3], done(n))
                        for pair in range(PAIRS):
                            last = pe.matmul(ub[0][:, 0:P], wo_sb[:, pair, :], ot[:, pair, :], start=(pair == 0),
                                             stop=(pair == PAIRS - 1))
                        last.then_inc(wo_full, 1)

                    def ffn_turn(n, f, turned):
                        pe.wait_ge(f_shifted, done(f))
                        if turned:
                            pe.wait_ge(turn_taken[2], done(n))
                        for k in range(4):
                            last = pe.transpose(tb[0][:, k * P:(k + 1) * P], sx[:, k * P:(k + 1) * P], ident[:])
                        last.then_inc(f_turned, 1)

                    def ffn_turn_back(f):
                        pe.wait_ge(f_rows, done(f))
                        for k in range(4):
                            last = pe.transpose(tb[1][:, k * P:(k + 1) * P], xr[:, k, :], ident[:])
                        last.then_inc(f_back, 1)

                    def feature(n, f, j, turned):
                        if j == 0:
                            pe.wait_ge(f_xn, done(f))
                            for q in v_made:
                                pe.wait_ge(q, done(n - 1 if turned else n - 4))
                        else:
                            pe.wait_ge(gated[j - 1], done(f))
                            pe.wait_ge(hid_made[j - 1], done(f))
                        for k, full in ((0, gate_full), (1, val_full)):
                            col = (FF if k == 0 else 0) + FO[j]
                            pe.matmul(pj[k][0:FW[j], :], w1_sb[:, col:col + FW[j]], xn[:], start=True,
                                      stop=True).then_inc(full[j], 1)

                    def ffn_out(f):
                        for j in range(NF):
                            pe.wait_ge(hid_made[j], done(f))
                        for j in range(NF):
                            last = pe.matmul(tb[0][:], w2_sb[0:FW[j], j, :], hid[j][0:FW[j], :], start=(j == 0),
                                             stop=(j == NF - 1))
                        last.then_inc(f_out, 1)

                    def chunk(l, c, slots):
                        f, _ = ffn_chunk(l, c)
                        for k, stages in enumerate(slots):
                            n, s = count_of(l, c, k), k % 2
                            qk, turn, attend = (x in stages for x in ALL[:3])
                            norm, mlp = ("ffn" in stages and k == x for x in (2, 3))
                            after = f - 1 if k == 0 else None
                            if attend:
                                scores(n - 2, layer_start(c) and k == 2, 0, s)
                                scores(n - 2, layer_start(c) and k == 2, 1, s)
                            if mlp:
                                ffn_turn_back(f)
                            if qk:
                                if k == 0 and layer_start(c):
                                    pe.wait_ge(wqk_loaded, (l + 1) * (16 * QKC))
                                project(n, 0, s)
                                project(n, 1, s)
                            if "out" in stages:
                                if k == 3 and layer_start(c):
                                    pe.wait_ge(wo_loaded, (l + 1) * 16)
                                project_out(n - 3)
                            if mlp:
                                pe.wait_ge(ffn_loaded, 16 * FFN_LOADS * ffn_layers(l, c))
                                if turn:
                                    project(n - 1, 4, 1 - s)
                                    project(n - 1, 5, 1 - s)
                                    turn_qk(n - 1, 0, None, f)
                                    turn_qk(n - 1, 1, None, f)
                                feature(n, f, 0, turn)
                                if turn:
                                    turn_qk(n - 1, 2, None, f)
                                    turn_qk(n - 1, 3, None, f)
                                if attend:
                                    turn_probs(n - 2, 0)
                                    turn_probs(n - 2, 1)
                                feature(n, f, 1, turn)
                                if attend:
                                    values(n - 2, 0, s)
                                    values(n - 2, 1, s)
                                feature(n, f, 2, turn)
                                if attend:
                                    values(n - 2, 2, s)
                                    values(n - 2, 3, s)
                                if qk:
                                    project(n, 2, s, f)
                                    project(n, 3, s, f)
                                ffn_out(f)
                                continue
                            if turn:
                                turn_qk(n - 1, 0, after, None)
                                turn_qk(n - 1, 1, after, None)
                                if k == 1 and layer_start(c):
                                    pe.wait_ge(wv_loaded, (l + 1) * (16 * 2))
                                project(n - 1, 4, 1 - s, None, not qk)
                                project(n - 1, 5, 1 - s, None, not qk)
                                turn_qk(n - 1, 2, after, None)
                                turn_qk(n - 1, 3, after, None)
                            if attend:
                                turn_probs(n - 2, 0)
                                turn_probs(n - 2, 1)
                            if norm:
                                ffn_turn(n - 1, f, turn)
                            if qk:
                                project(n, 2, s, None, not turn)
                                project(n, 3, s, None, not turn)
                            if attend:
                                for u in range(4):
                                    values(n - 2, u, s)

                    start_ahead(pe, "tensor")
                    pe.wait_ge(mask_made, 1)
                    pe.wait_ge(inits, 4)
                    run_slots(pe, chunk)
            clear_semaphores(ctx)

        with ExitStack() as ctx:
            sb, ps, sem1 = alloc(ctx)
            banks = [ps(f"fbank{g}", [P, BANK]) for g in range(NT // 4)]
            t_full, normed3, out_made, stored = (sem1(x) for x in ("l_full", "normed3", "out_made", "stored"))
            stats3, power3, apply3, _, _ = group_norm("ln3", sb)
            with nc.Block() as block:
                @block.tensor
                def _(pe):
                    for n in range(NT // 4):
                        for k in range(4):
                            t = 4 * n + k
                            last = pe.transpose(banks[n][:, k * P:(k + 1) * P], Y[:, 1 + t * P:1 + (t + 1) * P], ident[:])
                        last.then_inc(t_full, 1)

                @block.gpsimd
                def _(g):
                    for n in range(NT // 4):
                        power3(g, n)

                @block.vector
                def _(v):
                    def finish(n):
                        apply3(v, n, yrow_tiles(n), tiles_of(banks[n])).then_inc(normed3, 1)
                        v.wait_ge(normed3, n + 1)
                        rows = slice(4 * n, 4 * n + 4)
                        v.tensor_tensor(xin[:, rows, :], xin[:, rows, :], yrow[:, rows, :], ALU.add).then_inc(out_made, 1)

                    for n in range(NT // 4):
                        v.wait_ge(t_full, n + 1)
                        stats3(v, n, tiles_of(banks[n]))
                        if n >= 1:
                            finish(n - 1)
                    finish(NT // 4 - 1)

                @block.sync
                def _(sp):
                    for n in range(NT // 4):
                        sp.wait_ge(out_made, n + 1)
                        rows = slice(4 * n, 4 * n + 4)
                        sp.dma_start(out[:, n * BANK:(n + 1) * BANK, :].rearrange("a (n p) c -> p (a n) c", p=P),
                                     xin[:, rows, :]).then_inc(stored, 16)
                    sp.wait_ge(stored, 16 * (NT // 4))


def shape_constants(T):
    import numpy as np
    half = np.arange(0, DIM_HEAD, 2, dtype=np.float32)
    inv_freq = np.float32(1.0) / np.float32(10000.0) ** (half / np.float32(DIM_HEAD))
    t = np.arange(T, dtype=np.float32)
    freqs = (t[:, None] * inv_freq[None, :]).astype(np.float64)
    base = (half.astype(np.float64) + 0.4 * DIM_HEAD) / (1.4 * DIM_HEAD)
    power = (np.arange(T) % P - P // 2) / (WINDOW // 2)
    scale = base[None, :] ** power[:, None]
    cos, sin = np.cos(freqs), np.sin(freqs)
    tables = []
    for sc in (scale, 1.0 / scale):
        tables += [cos * sc, cos * sc, sin * sc, -sin * sc]
    rot = np.concatenate(tables, 1).astype(np.float32)
    factor = np.tile(base ** (P / (WINDOW // 2)), 2 * 2).astype(np.float32)[:, None]
    p = np.arange(P)
    q, key = p[:, None, None] % WINDOW, np.arange(2 * WINDOW)[None, None, :]
    hidden = (key < q) | (key > q + WINDOW) | np.zeros((1, 2, 1), bool)
    before = (p[:, None, None] < P // 2) & (np.arange(2)[None, :, None] == 0) & (key < WINDOW)
    mask = np.stack([(hidden | before).reshape(P, P), hidden.reshape(P, P)], 1)
    return rot, factor, np.where(mask, np.float32(MASKED), np.float32(0.0))


_INS = ["L0_attn_x", "L0_attn_w_attn", "L0_attn_w_proj", "L0_ffn_Wqkv", "L0_ffn_q_scale", "L0_ffn_k_scale",
        "L0_ffn_Wo", "L0_ffn_ln_g", "L0_ffn_ln_b", "L0_ffn_W1", "L0_ffn_b1", "L0_ffn_W2", "L0_ffn_b2"]


def build(nc, inputs):
    import numpy as _np
    arrays = {f"in_{n}_dram": _np.ascontiguousarray(inputs[n]) for n in _INS}
    shape = arrays["in_L0_attn_x_dram"].shape
    for n, a in zip(("rot", "halo", "mask"), shape_constants(shape[1])):
        arrays[f"const_{n}_dram"] = _np.ascontiguousarray(a)
    args = [nc.dram_tensor(n, a.shape, mybir.dt.from_np(a.dtype), kind="ExternalInput").ap()
            for n, a in arrays.items()]
    out = nc.dram_tensor("out_0_dram", shape, F32, kind="ExternalOutput").ap()
    sandwich_kernel(nc, *args, out)
    return arrays, out


def kernel(**inputs):
    import concourse.bacc as _bacc
    from concourse.bass_utils import run_bass_kernel_spmd as _run

    nc = _bacc.Bacc("TRN2", target_bir_lowering=False, num_devices=1)
    arrays, _ = build(nc, inputs)
    r = _run(nc, [arrays], core_ids=[0])
    return r.results[0]["out_0_dram"]
```
